# Optimizing a Trainium2 kernel written in Bass

```python
import numpy as np
import jax
import jax.numpy as jnp

def _softmax(x, axis=-1):
    return jax.nn.softmax(x, axis=axis)

def _gelu(x):
    return jax.nn.gelu(x, approximate=True)

def _silu(x):
    return jax.nn.silu(x)

def _sigmoid(x):
    return jax.nn.sigmoid(x)

def _layernorm(x, axis=-1, eps=1e-05):
    m = jnp.mean(x, axis=axis, keepdims=True)
    v = jnp.var(x, axis=axis, keepdims=True)
    return (x - m) / jnp.sqrt(v + eps)

def _scatter_add(tgt, idx, src, axis=0):
    return tgt.at[idx].add(src)

def _segment_sum(src, seg, n):
    return jax.ops.segment_sum(src, seg, n)
kernel_name = 'mk_vit_tower_d2_tok_img256_r4_862059'

def setup_inputs(seed: int=0):
    np.random.seed(seed)
    _w = jnp.asarray

    def _rec_inputs():
        import jax
        import jax.numpy as jnp
        _rk = jax.random.key(seed)
        x = -4.65018e-05 + 0.999886 * jax.random.normal(jax.random.fold_in(_rk, 1), (128, 3, 128, 128), jnp.float32)
        return x
    x = _rec_inputs()

    def _L0_tok_setup():
        import jax, jax.numpy as jnp
        import numpy as np
        B = 64
        IMG = 128
        P = 32
        DIM = 64
        DEPTH = 4
        HEADS = 4
        DH = 64
        MLP = 128
        PD = 3 * P * P
        GRID = IMG // P
        NPATCH = GRID * GRID

        def _ln(x, g, b):
            m = jnp.mean(x, -1, keepdims=True)
            v = jnp.mean((x - m) ** 2, -1, keepdims=True)
            return (x - m) * jax.lax.rsqrt(v + 1e-05) * g + b
        key = jax.random.key(seed)
        ks = jax.random.split(key, 10)

        def n(k, shape, s=0.02):
            return jax.random.normal(k, shape, jnp.float32) * s
        return {'img': jax.random.normal(ks[0], (B, 3, IMG, IMG), jnp.float32), 'ln_p1_g': jnp.ones((PD,), jnp.float32), 'ln_p1_b': jnp.zeros((PD,), jnp.float32), 'W_patch': n(ks[1], (PD, DIM)), 'b_patch': jnp.zeros((DIM,), jnp.float32), 'ln_p2_g': jnp.ones((DIM,), jnp.float32), 'ln_p2_b': jnp.zeros((DIM,), jnp.float32), 'cls': n(ks[2], (1, 1, DIM), 1.0), 'pos': n(ks[3], (1, NPATCH + 1, DIM), 1.0), 'attn_ln_g': jnp.ones((DEPTH, DIM), jnp.float32), 'attn_ln_b': jnp.zeros((DEPTH, DIM), jnp.float32), 'Wqkv': n(ks[4], (DEPTH, DIM, 3 * HEADS * DH)), 'Wo': n(ks[5], (DEPTH, HEADS * DH, DIM)), 'bo': jnp.zeros((DEPTH, DIM), jnp.float32), 'ff_ln_g': jnp.ones((DEPTH, DIM), jnp.float32), 'ff_ln_b': jnp.zeros((DEPTH, DIM), jnp.float32), 'W1': n(ks[6], (DEPTH, DIM, MLP)), 'b1': jnp.zeros((DEPTH, MLP), jnp.float32), 'W2': n(ks[7], (DEPTH, MLP, DIM)), 'b2': jnp.zeros((DEPTH, DIM), jnp.float32), 'ln_f_g': jnp.ones((DIM,), jnp.float32), 'ln_f_b': jnp.zeros((DIM,), jnp.float32)}
    _L0_tok_all = _L0_tok_setup()
    _L0_tok_in = {k: v for k, v in _L0_tok_all.items() if k in ('ln_p1_g', 'ln_p1_b', 'W_patch', 'b_patch', 'ln_p2_g', 'ln_p2_b', 'cls', 'pos', 'attn_ln_g', 'attn_ln_b', 'Wqkv', 'Wo', 'bo', 'ff_ln_g', 'ff_ln_b', 'W1', 'b1', 'W2', 'b2', 'ln_f_g', 'ln_f_b')}
    del _L0_tok_all

    def _L0_attn_setup():
        import jax, jax.numpy as jnp
        import numpy as np
        B, N, C, H = (1024, 64, 64, 8)
        key = jax.random.key(seed)
        ks = jax.random.split(key, 6)
        return {'x': jax.random.normal(ks[0], (B, N, C), dtype=jnp.float32), 'qkv_w': jax.random.normal(ks[1], (C, 3 * C), dtype=jnp.float32) * 0.02, 'qkv_b': jax.random.normal(ks[2], (3 * C,), dtype=jnp.float32) * 0.02, 'proj_w': jax.random.normal(ks[3], (C, C), dtype=jnp.float32) * 0.02, 'proj_b': jax.random.normal(ks[4], (C,), dtype=jnp.float32) * 0.02, 'rpb_table': jax.random.normal(ks[5], (2 * N - 1, H), dtype=jnp.float32) * 0.02}
    _L0_attn_all = _L0_attn_setup()
    _L0_attn_in = {k: v for k, v in _L0_attn_all.items() if k in ('qkv_w', 'qkv_b', 'proj_w', 'proj_b', 'rpb_table')}
    del _L0_attn_all

    def _L0_ffn_setup():
        import jax, jax.numpy as jnp
        import numpy as np
        B, T, IN_DIM = (64, 64, 64)
        HID, OUT_DIM = (128, 64)
        N_LAYERS, N_EXPERTS, N_SHARED = (2, 16, 1)
        key = jax.random.key(seed)
        ks = jax.random.split(key, 10)
        s = 0.02
        x = jax.random.normal(ks[0], (B, T, IN_DIM), dtype=jnp.float32)
        route_id = jax.random.randint(ks[1], (B,), 0, N_EXPERTS)
        Wi = jax.random.normal(ks[2], (HID, IN_DIM), dtype=jnp.float32) * s
        bi = jnp.zeros((HID,), dtype=jnp.float32)
        Wr = jax.random.normal(ks[3], (N_LAYERS, N_EXPERTS, HID, HID), dtype=jnp.float32) * s
        br = jax.random.normal(ks[4], (N_LAYERS, N_EXPERTS, HID), dtype=jnp.float32) * s
        Ws = jax.random.normal(ks[5], (N_LAYERS, N_SHARED, HID, HID), dtype=jnp.float32) * s
        bs = jax.random.normal(ks[6], (N_LAYERS, N_SHARED, HID), dtype=jnp.float32) * s
        Wo = jax.random.normal(ks[7], (OUT_DIM, HID), dtype=jnp.float32) * s
        bo = jnp.zeros((OUT_DIM,), dtype=jnp.float32)
        return {'x': x, 'route_id': route_id, 'Wi': Wi, 'bi': bi, 'Wr': Wr, 'br': br, 'Ws': Ws, 'bs': bs, 'Wo': Wo, 'bo': bo}
    _L0_ffn_all = _L0_ffn_setup()
    _L0_ffn_in = {k: v for k, v in _L0_ffn_all.items() if k in ('route_id', 'Wi', 'bi', 'Wr', 'br', 'Ws', 'bs', 'Wo', 'bo')}
    del _L0_ffn_all

    def _L1_attn_setup():
        import jax, jax.numpy as jnp
        import numpy as np
        import math
        B, T, D_MODEL = (1, 512, 64)
        N_Q, N_KV = (16, 1)
        D_HEAD = D_MODEL // N_KV
        QPG = N_Q // N_KV
        ROPE_BASE = 10000.0
        WINDOW = 128
        EPS = 1.1920929e-07
        NEG = -1e+30

        def _rope(x, base=ROPE_BASE):
            t, d = (x.shape[-2], x.shape[-1])
            freqs = base ** (-2.0 * jnp.arange(d // 2, dtype=jnp.float32) / d)
            theta = jnp.arange(t, dtype=jnp.float32)[:, None] * freqs[None, :]
            cos, sin = (jnp.cos(theta), jnp.sin(theta))
            x1, x2 = (x[..., 0::2], x[..., 1::2])
            r1 = x1 * cos - x2 * sin
            r2 = x1 * sin + x2 * cos
            return jnp.stack([r1, r2], axis=-1).reshape(x.shape)

        def _rmsnorm(x, w):
            return x * jax.lax.rsqrt(jnp.mean(x * x, axis=-1, keepdims=True) + EPS) * w
        key = jax.random.key(seed)
        k0, k1, k2, k3 = jax.random.split(key, 4)
        x = jax.random.normal(k0, (B, T, D_MODEL), dtype=jnp.float32)
        wq = jax.random.normal(k1, (QPG * N_KV * D_HEAD, D_MODEL), dtype=jnp.float32) * 0.02
        wkv = jax.random.normal(k2, (2 * D_HEAD * N_KV, D_MODEL), dtype=jnp.float32) * 0.02
        wo = jax.random.normal(k3, (D_MODEL, D_HEAD * N_Q * N_KV), dtype=jnp.float32) * 0.02
        q_norm_w = jnp.ones((D_HEAD,), dtype=jnp.float32)
        k_norm_w = jnp.ones((D_HEAD,), dtype=jnp.float32)
        return {'x': x, 'wq': wq, 'wkv': wkv, 'wo': wo, 'q_norm_w': q_norm_w, 'k_norm_w': k_norm_w}
    _L1_attn_all = _L1_attn_setup()
    _L1_attn_in = {k: v for k, v in _L1_attn_all.items() if k in ('wq', 'wkv', 'wo', 'q_norm_w', 'k_norm_w')}
    del _L1_attn_all

    def _L1_ffn_setup():
        import jax, jax.numpy as jnp
        import numpy as np
        B, S, D, E, H, K = (4, 1024, 64, 8, 128, 2)
        key = jax.random.key(seed)
        ks = jax.random.split(key, 6)
        x = jax.random.normal(ks[0], (B, S, D), jnp.float32)
        Wg = jax.random.normal(ks[1], (D, E), jnp.float32) * 0.02
        bg = jnp.zeros((E,), jnp.float32)
        W1 = jax.random.normal(ks[2], (E, D, H), jnp.float32) * 0.02
        b1 = jnp.zeros((E, H), jnp.float32)
        W2 = jax.random.normal(ks[3], (E, H, D), jnp.float32) * 0.02
        b2 = jnp.zeros((E, D), jnp.float32)
        return {'x': x, 'Wg': Wg, 'bg': bg, 'W1': W1, 'b1': b1, 'W2': W2, 'b2': b2}
    _L1_ffn_all = _L1_ffn_setup()
    _L1_ffn_in = {k: v for k, v in _L1_ffn_all.items() if k in ('Wg', 'bg', 'W1', 'b1', 'W2', 'b2')}
    del _L1_ffn_all
    return {'x': x, 'L0_tok_ln_p1_g': _L0_tok_in['ln_p1_g'], 'L0_tok_ln_p1_b': _L0_tok_in['ln_p1_b'], 'L0_tok_W_patch': _L0_tok_in['W_patch'], 'L0_tok_b_patch': _L0_tok_in['b_patch'], 'L0_tok_ln_p2_g': _L0_tok_in['ln_p2_g'], 'L0_tok_ln_p2_b': _L0_tok_in['ln_p2_b'], 'L0_tok_cls': _L0_tok_in['cls'], 'L0_tok_pos': _L0_tok_in['pos'], 'L0_tok_attn_ln_g': _L0_tok_in['attn_ln_g'], 'L0_tok_attn_ln_b': _L0_tok_in['attn_ln_b'], 'L0_tok_Wqkv': _L0_tok_in['Wqkv'], 'L0_tok_Wo': _L0_tok_in['Wo'], 'L0_tok_bo': _L0_tok_in['bo'], 'L0_tok_ff_ln_g': _L0_tok_in['ff_ln_g'], 'L0_tok_ff_ln_b': _L0_tok_in['ff_ln_b'], 'L0_tok_W1': _L0_tok_in['W1'], 'L0_tok_b1': _L0_tok_in['b1'], 'L0_tok_W2': _L0_tok_in['W2'], 'L0_tok_b2': _L0_tok_in['b2'], 'L0_tok_ln_f_g': _L0_tok_in['ln_f_g'], 'L0_tok_ln_f_b': _L0_tok_in['ln_f_b'], 'L0_attn_qkv_w': _L0_attn_in['qkv_w'], 'L0_attn_qkv_b': _L0_attn_in['qkv_b'], 'L0_attn_proj_w': _L0_attn_in['proj_w'], 'L0_attn_proj_b': _L0_attn_in['proj_b'], 'L0_attn_rpb_table': _L0_attn_in['rpb_table'], 'L0_ffn_route_id': _L0_ffn_in['route_id'], 'L0_ffn_Wi': _L0_ffn_in['Wi'], 'L0_ffn_bi': _L0_ffn_in['bi'], 'L0_ffn_Wr': _L0_ffn_in['Wr'], 'L0_ffn_br': _L0_ffn_in['br'], 'L0_ffn_Ws': _L0_ffn_in['Ws'], 'L0_ffn_bs': _L0_ffn_in['bs'], 'L0_ffn_Wo': _L0_ffn_in['Wo'], 'L0_ffn_bo': _L0_ffn_in['bo'], 'L1_attn_wq': _L1_attn_in['wq'], 'L1_attn_wkv': _L1_attn_in['wkv'], 'L1_attn_wo': _L1_attn_in['wo'], 'L1_attn_q_norm_w': _L1_attn_in['q_norm_w'], 'L1_attn_k_norm_w': _L1_attn_in['k_norm_w'], 'L1_ffn_Wg': _L1_ffn_in['Wg'], 'L1_ffn_bg': _L1_ffn_in['bg'], 'L1_ffn_W1': _L1_ffn_in['W1'], 'L1_ffn_b1': _L1_ffn_in['b1'], 'L1_ffn_W2': _L1_ffn_in['W2'], 'L1_ffn_b2': _L1_ffn_in['b2']}

def reference(x, L0_tok_ln_p1_g, L0_tok_ln_p1_b, L0_tok_W_patch, L0_tok_b_patch, L0_tok_ln_p2_g, L0_tok_ln_p2_b, L0_tok_cls, L0_tok_pos, L0_tok_attn_ln_g, L0_tok_attn_ln_b, L0_tok_Wqkv, L0_tok_Wo, L0_tok_bo, L0_tok_ff_ln_g, L0_tok_ff_ln_b, L0_tok_W1, L0_tok_b1, L0_tok_W2, L0_tok_b2, L0_tok_ln_f_g, L0_tok_ln_f_b, L0_attn_qkv_w, L0_attn_qkv_b, L0_attn_proj_w, L0_attn_proj_b, L0_attn_rpb_table, L0_ffn_route_id, L0_ffn_Wi, L0_ffn_bi, L0_ffn_Wr, L0_ffn_br, L0_ffn_Ws, L0_ffn_bs, L0_ffn_Wo, L0_ffn_bo, L1_attn_wq, L1_attn_wkv, L1_attn_wo, L1_attn_q_norm_w, L1_attn_k_norm_w, L1_ffn_Wg, L1_ffn_bg, L1_ffn_W1, L1_ffn_b1, L1_ffn_W2, L1_ffn_b2):
    import jax
    import jax.numpy as jnp

    def _L0_tok_ref(img, ln_p1_g, ln_p1_b, W_patch, b_patch, ln_p2_g, ln_p2_b, cls, pos, attn_ln_g, attn_ln_b, Wqkv, Wo, bo, ff_ln_g, ff_ln_b, W1, b1, W2, b2, ln_f_g, ln_f_b):
        import jax, jax.numpy as jnp
        import numpy as np
        B = 64
        IMG = 128
        P = 32
        DIM = 64
        DEPTH = 4
        HEADS = 4
        DH = 64
        MLP = 128
        PD = 3 * P * P
        GRID = IMG // P
        NPATCH = GRID * GRID

        def _ln(x, g, b):
            m = jnp.mean(x, -1, keepdims=True)
            v = jnp.mean((x - m) ** 2, -1, keepdims=True)
            return (x - m) * jax.lax.rsqrt(v + 1e-05) * g + b
        Bsz = img.shape[0]
        x = img.reshape(Bsz, 3, GRID, P, GRID, P)
        x = x.transpose(0, 2, 4, 1, 3, 5).reshape(Bsz, NPATCH, PD)
        x = _ln(x, ln_p1_g, ln_p1_b) @ W_patch + b_patch
        x = _ln(x, ln_p2_g, ln_p2_b)
        x = jnp.concatenate([jnp.broadcast_to(cls, (Bsz, 1, DIM)), x], axis=1) + pos
        scale = DH ** (-0.5)
        for i in range(DEPTH):
            h = _ln(x, attn_ln_g[i], attn_ln_b[i])
            qkv = h @ Wqkv[i]
            q, k, v = jnp.split(qkv, 3, axis=-1)

            def to_heads(t):
                return t.reshape(Bsz, -1, HEADS, DH).transpose(0, 2, 1, 3)
            q, k, v = (to_heads(q), to_heads(k), to_heads(v))
            a = jax.nn.softmax(jnp.einsum('bhqd,bhkd->bhqk', q, k) * scale, axis=-1)
            o = jnp.einsum('bhqk,bhkd->bhqd', a, v)
            o = o.transpose(0, 2, 1, 3).reshape(Bsz, -1, HEADS * DH)
            x = x + o @ Wo[i] + bo[i]
            h = _ln(x, ff_ln_g[i], ff_ln_b[i])
            x = x + jax.nn.gelu(h @ W1[i] + b1[i], approximate=False) @ W2[i] + b2[i]
        return _ln(x, ln_f_g, ln_f_b)

    def _L0_attn_ref(x, qkv_w, qkv_b, proj_w, proj_b, rpb_table):
        import jax, jax.numpy as jnp
        import numpy as np
        B, N, C, H = (1024, 64, 64, 8)
        Bw, Nw, Cd = x.shape
        nh = rpb_table.shape[1]
        dh = Cd // nh
        scale = dh ** (-0.5)
        qkv = (x @ qkv_w + qkv_b).reshape(Bw, Nw, 3, nh, dh)
        q, k, v = (qkv[:, :, 0], qkv[:, :, 1], qkv[:, :, 2])
        attn = jnp.einsum('bnhd,bmhd->bhnm', q * scale, k)
        coords = jnp.arange(Nw)
        rel_idx = coords[:, None] - coords[None, :] + (Nw - 1)
        bias = jnp.transpose(rpb_table[rel_idx], (2, 0, 1))
        attn = jax.nn.softmax(attn + bias[None], axis=-1)
        out = jnp.einsum('bhnm,bmhd->bnhd', attn, v).reshape(Bw, Nw, Cd)
        return out @ proj_w + proj_b

    def _L0_ffn_ref(x, route_id, Wi, bi, Wr, br, Ws, bs, Wo, bo):
        import jax, jax.numpy as jnp
        import numpy as np
        B, T, IN_DIM = (64, 64, 64)
        HID, OUT_DIM = (128, 64)
        N_LAYERS, N_EXPERTS, N_SHARED = (2, 16, 1)
        flat = x.reshape(-1, x.shape[-1])
        n_tok = flat.shape[0]
        route = jnp.repeat(route_id, n_tok // route_id.shape[0])
        h = jax.nn.relu(flat @ Wi.T + bi)
        n_layers, n_experts = (Wr.shape[0], Wr.shape[1])
        for l in range(n_layers):
            shared = (jnp.einsum('nd,shd->snh', h, Ws[l]) + bs[l][:, None, :]).mean(axis=0)
            routed = jnp.zeros_like(h)
            for e in range(n_experts):
                ye = h @ Wr[l, e].T + br[l, e]
                routed = routed + jnp.where((route == e)[:, None], ye, 0.0)
            h = jax.nn.relu(shared + routed + h)
        out = h @ Wo.T + bo
        return out.reshape(*x.shape[:-1], out.shape[-1])

    def _L1_attn_ref(x, wq, wkv, wo, q_norm_w, k_norm_w):
        import jax, jax.numpy as jnp
        import numpy as np
        import math
        B, T, D_MODEL = (1, 512, 64)
        N_Q, N_KV = (16, 1)
        D_HEAD = D_MODEL // N_KV
        QPG = N_Q // N_KV
        ROPE_BASE = 10000.0
        WINDOW = 128
        EPS = 1.1920929e-07
        NEG = -1e+30

        def _rope(x, base=ROPE_BASE):
            t, d = (x.shape[-2], x.shape[-1])
            freqs = base ** (-2.0 * jnp.arange(d // 2, dtype=jnp.float32) / d)
            theta = jnp.arange(t, dtype=jnp.float32)[:, None] * freqs[None, :]
            cos, sin = (jnp.cos(theta), jnp.sin(theta))
            x1, x2 = (x[..., 0::2], x[..., 1::2])
            r1 = x1 * cos - x2 * sin
            r2 = x1 * sin + x2 * cos
            return jnp.stack([r1, r2], axis=-1).reshape(x.shape)

        def _rmsnorm(x, w):
            return x * jax.lax.rsqrt(jnp.mean(x * x, axis=-1, keepdims=True) + EPS) * w
        Bx, Tx, C = x.shape
        q = x @ wq.T
        kv = x @ wkv.T
        k, v = (kv[..., :N_KV * D_HEAD], kv[..., N_KV * D_HEAD:])
        q = q.reshape(Bx, Tx, QPG, N_KV, D_HEAD).transpose(0, 2, 3, 1, 4)
        k = k.reshape(Bx, Tx, 1, N_KV, D_HEAD).transpose(0, 2, 3, 1, 4)
        v = v.reshape(Bx, Tx, 1, N_KV, D_HEAD).transpose(0, 2, 3, 1, 4)
        q = _rmsnorm(_rope(q), q_norm_w)
        k = _rmsnorm(_rope(k), k_norm_w)
        rows = jnp.arange(Tx)[:, None]
        cols = jnp.arange(Tx)[None, :]
        mask = (cols <= rows) & (rows - cols <= WINDOW)
        scale = 1.0 / math.sqrt(D_HEAD)
        scores = jnp.einsum('bqgtd,bqgsd->bqgts', q, k) * scale
        scores = jnp.where(mask[None, None, None], scores, NEG)
        attn = jax.nn.softmax(scores, axis=-1)
        out = jnp.einsum('bqgts,bqgsd->bqgtd', attn, v)
        out = out.transpose(0, 3, 1, 2, 4).reshape(Bx, Tx, QPG * N_KV * D_HEAD)
        return out @ wo.T

    def _L1_ffn_ref(x, Wg, bg, W1, b1, W2, b2):
        import jax, jax.numpy as jnp
        import numpy as np
        B, S, D, E, H, K = (4, 1024, 64, 8, 128, 2)
        Bv, Sv, Dv = x.shape
        gate_scores = x @ Wg + bg
        _, idx = jax.lax.top_k(gate_scores, K)
        mask = jax.nn.one_hot(idx, E, dtype=x.dtype).sum(axis=-2)
        xf = x.reshape(-1, Dv)
        mf = mask.reshape(-1, E)
        h = jax.nn.gelu(jnp.einsum('td,edh->teh', xf, W1) + b1[None], approximate=False)
        y = jnp.einsum('teh,ehd->ted', h, W2) + b2[None]
        out = jnp.einsum('ted,te->td', y, mf)
        return out.reshape(Bv, Sv, Dv)
    h = _L0_tok_ref(x, L0_tok_ln_p1_g, L0_tok_ln_p1_b, L0_tok_W_patch, L0_tok_b_patch, L0_tok_ln_p2_g, L0_tok_ln_p2_b, L0_tok_cls, L0_tok_pos, L0_tok_attn_ln_g, L0_tok_attn_ln_b, L0_tok_Wqkv, L0_tok_Wo, L0_tok_bo, L0_tok_ff_ln_g, L0_tok_ff_ln_b, L0_tok_W1, L0_tok_b1, L0_tok_W2, L0_tok_b2, L0_tok_ln_f_g, L0_tok_ln_f_b)
    h = h + _L0_attn_ref(_layernorm(h, axis=-1), L0_attn_qkv_w, L0_attn_qkv_b, L0_attn_proj_w, L0_attn_proj_b, L0_attn_rpb_table)
    h = h + _L0_ffn_ref(_layernorm(h, axis=-1), L0_ffn_route_id, L0_ffn_Wi, L0_ffn_bi, L0_ffn_Wr, L0_ffn_br, L0_ffn_Ws, L0_ffn_bs, L0_ffn_Wo, L0_ffn_bo)
    h = h + _L1_attn_ref(_layernorm(h, axis=-1), L1_attn_wq, L1_attn_wkv, L1_attn_wo, L1_attn_q_norm_w, L1_attn_k_norm_w)
    h = h + _L1_ffn_ref(_layernorm(h, axis=-1), L1_ffn_Wg, L1_ffn_bg, L1_ffn_W1, L1_ffn_b1, L1_ffn_W2, L1_ffn_b2)
    return h

_drawn_inputs = setup_inputs


def setup_inputs(seed=0):
    import zlib

    import numpy as np

    out = dict(_drawn_inputs(seed))
    spreads = {'L0_tok_ln_p1_g': (1.0, 0.2),
     'L0_tok_ln_p1_b': (0.0, 0.1),
     'L0_tok_b_patch': (0.0, 0.1),
     'L0_tok_ln_p2_g': (1.0, 0.2),
     'L0_tok_ln_p2_b': (0.0, 0.1),
     'L0_tok_attn_ln_g': (1.0, 0.6),
     'L0_tok_attn_ln_b': (0.0, 0.483),
     'L0_tok_bo': (0.0, 0.1),
     'L0_tok_ff_ln_g': (1.0, 0.6),
     'L0_tok_ff_ln_b': (0.0, 0.8),
     'L0_tok_b1': (0.0, 0.328),
     'L0_tok_b2': (0.0, 0.1),
     'L0_tok_ln_f_g': (1.0, 0.2),
     'L0_tok_ln_f_b': (0.0, 0.1),
     'L0_ffn_bi': (0.0, 0.315),
     'L0_ffn_bo': (0.0, 0.1),
     'L1_attn_q_norm_w': (1.0, 0.6),
     'L1_attn_k_norm_w': (1.0, 0.6),
     'L1_ffn_bg': (0.0, 0.1),
     'L1_ffn_b1': (0.0, 0.502),
     'L1_ffn_b2': (0.0, 0.1)}
    factors = {'L0_attn_qkv_w': 3.666,
     'L0_attn_qkv_b': 5.899,
     'L0_attn_proj_w': 3.28,
     'L0_attn_rpb_table': 22.474,
     'L0_ffn_Wr': 3.872,
     'L0_ffn_br': 4.498,
     'L0_ffn_Ws': 3.635,
     'L0_ffn_bs': 4.175}
    for name, (base, spread) in spreads.items():
        noise = np.random.default_rng([zlib.crc32(name.encode()), seed]).standard_normal(out[name].shape)
        drawn = base * np.exp(spread * noise) if base else spread * noise
        out[name] = jnp.asarray(drawn.astype(out[name].dtype))
    for name, factor in factors.items():
        out[name] = (out[name] * factor).astype(out[name].dtype)
    return out
```

```python
from contextlib import ExitStack

import numpy as np
import concourse.bass as bass
import concourse.mybir as mybir

FP32 = mybir.dt.float32
BF16 = mybir.dt.bfloat16
I32 = mybir.dt.int32
ALU = mybir.AluOpType
ACT = mybir.ActivationFunctionType
AX = mybir.AxisListType

IMAGES, PATCH, GRID, CHANNELS, DIM = 128, 32, 4, 3, 64
PATCHES = GRID * GRID
FEATURES = CHANNELS * PATCH * PATCH
T = PATCHES + 1
LAYERS, HEADS, HIDDEN = 4, 4, 128
PIECES, HALVES = 4, 2
IMG = IMAGES // (PIECES * HALVES)
N = IMG * T
NP = IMG * PATCHES
PAD = 32
SETS = IMG // 4
HQ = HEADS * T
CHUNKS = FEATURES // 128
TILES = PIECES * HALVES
EPS = 1e-5
RMS_EPS = 1.1920929e-07
WIN_HEADS, WIN_DH = 8, 8
ROT_HEADS = 16
ROUTES, FFN_LAYERS, EXPERTS = 64, 2, 16
PAIRS = IMG // 2
TOP_EXPERTS = 8
NEG = -1e30

L_Q, L_K, L_V, L_O, L_W1, L_W2, L_VEC = 0, 256, 384, 640, 768, 896, 960
L_ALL = L_VEC + 7
X_EMBED, X_FINAL, X_WIN, X_FFN, X_ROT, X_TOP = 0, 9, 10, 12, 13, 17
K_EMBED, K_FINAL, K_WIN, K_FFN, K_ROT, K_TOP = 0, 9, 10, 11, 12, 13
H_WIN, H_FFN, H_ROT, H_TOP = 8, 9, 10, 11
A_WIN, A_ROT = 4, 6
WIN_PASSES, ROT_PASSES = 2, 4


def build(nc, d, out):
    ctx = ExitStack()
    with ctx:
        def sb(name, shape, dt=FP32):
            return ctx.enter_context(nc.sbuf_tensor(name, shape, dt))

        def sem(name):
            return ctx.enter_context(nc.semaphore(name))

        X = sb("X", [128, PIECES, IMG, T])
        Z = sb("Z", [128, PIECES, IMG, PAD])
        ZN = sb("ZN", [128, PIECES, N])
        SQ = sb("SQ", [128, PIECES, N])
        RS = sb("RS", [128, PIECES, N])
        QO = sb("QO", [128, PIECES, IMG, HEADS, T])
        KT = sb("KT", [128, PIECES, IMG, T])
        E = sb("E", [HQ, TILES, IMG, PAD])
        PH = sb("PH", [128, TILES, N])
        VT = sb("VT", [128, PIECES, SETS, 128])
        mx = sb("mx", [HQ, TILES, IMG])
        sm = sb("sm", [HQ, TILES, IMG])
        rc = sb("rc", [HQ, TILES, IMG])
        consts = sb("consts", [128, 3 * 128 + 3 * T])
        ident, cen, avg = (consts[:, 128 * n:128 * n + 128] for n in range(3))
        cos_t, sin_t, causal = (consts[:, 384 + T * n:384 + T * n + T] for n in range(3))
        eps_t = sb("eps_t", [128, 2])
        ones = sb("ones", [128, 128])
        LW = sb("LW", [128, L_ALL])
        lvec = sb("lvec", [128, 7 + 128 + 64])
        AB = sb("AB", [128, 2, HEADS, 128])
        evec = sb("evec", [128, 6 + T])
        arena = sb("arena", [128, 24300])

        used = [0]

        def part(*shape):
            n = int(np.prod(shape))
            o = used[0]
            used[0] += n
            v = arena[:, o:o + n]
            if len(shape) == 2:
                v = v.rearrange("p (a b) -> p a b", a=shape[0])
            if len(shape) == 3:
                v = v.rearrange("p (a b c) -> p a b c", a=shape[0], b=shape[1])
            return v

        img = [part(CHUNKS, NP) for _ in range(2)]
        sqi = part(CHUNKS, NP)
        WA = part(CHUNKS, 192)
        lnp = part(2, CHUNKS)
        assert used[0] <= 24300
        used[0] = 0
        winw = part(2 * WIN_HEADS + 2, 128)
        winv = part(WIN_HEADS + 2 + 128 + T * 2)
        rotw = part(3 * ROT_HEADS + 3, 128)
        rotv = part(3)
        ffw = part(128 + 64 + 2 + 2 + 256)
        rw = part(FFN_LAYERS * EXPERTS, 129)
        picked = part(2, PAIRS, 129)
        topw = part(TOP_EXPERTS * (128 + 64 + 1) + 16 + 16)
        rope = part(4, 2 * N).rearrange("p k (b n) -> p k b n", b=2)
        gate = part(3, 32, 8)
        mk32 = part(PIECES, IMG, T)[0:16]
        assert used[0] <= 24300
        route = sb("route", [1, ROUTES], I32)
        selb = sb("selb", [16, 16], BF16)
        b2d = sb("b2d", [16, 128])
        gmax = sb("gmax", [128, 32])
        idx = sb("idx", [128, 8])
        mkb = sb("mkb", [16, PIECES, N], BF16)
        B = [ctx.enter_context(nc.psum_tensor(f"bank{n}", [128, 512], FP32)) for n in range(8)]

        w_embed, w_const, w_late, w_route = sem("w_embed"), sem("w_const"), sem("w_late"), sem("w_route")
        w_layer, layer_used = sem("w_layer"), sem("layer_used")
        img_in = [sem("img_in0"), sem("img_in1")]
        pads_zero, scaled, colsum, wa_ready = sem("pads_zero"), sem("scaled"), sem("colsum"), sem("wa_ready")
        cvec_psum, cvec_ready = sem("cvec_psum"), sem("cvec_ready")
        img_sq, img_sum, embed_psum, sq_psum = sem("img_sq"), sem("img_sum"), sem("embed_psum"), sem("sq_psum")
        mean_sq, e_var, e_log, e_rstd, embedded = (sem("mean_sq"), sem("e_var"), sem("e_log"), sem("e_rstd"),
                                                   sem("embedded"))
        stage_done = sem("stage_done")
        x_ready, centered, squared, var_psum = sem("x_ready"), sem("centered"), sem("squared"), sem("var_psum")
        logged, rstd_ready, normed, h_ready = sem("logged"), sem("rstd_ready"), sem("normed"), sem("h_ready")
        gained = sem("gained")
        ab_psum, ab_ready, lvec_ready = sem("ab_psum"), sem("ab_ready"), sem("lvec_ready")
        q_psum, q_ready, v_psum, v_ready = sem("q_psum"), sem("q_ready"), sem("v_psum"), sem("v_ready")
        k_psum, k_ready = sem("k_psum"), sem("k_ready")
        s_psum, s_taken, biased, maxed, expd = sem("s_psum"), sem("s_taken"), sem("biased"), sem("maxed"), sem("expd")
        summed, inv_ready, probs_ready = sem("summed"), sem("inv_ready"), sem("probs_ready")
        pt_psum, pt_ready, pv_psum, o_ready, y_psum = (sem("pt_psum"), sem("pt_ready"), sem("pv_psum"),
                                                       sem("o_ready"), sem("y_psum"))
        hid_psum, hid_ready, down_psum = sem("hid_psum"), sem("hid_ready"), sem("down_psum")
        fh_psum, fh_ready, g_psum, g_biased, g_ready = (sem("fh_psum"), sem("fh_ready"), sem("g_psum"),
                                                        sem("g_biased"), sem("g_ready"))
        rw_ready, picked_ready, fo_psum, rw_part = sem("rw_ready"), sem("picked_ready"), sem("fo_psum"), sem("rw_part")
        r_psum, r_sq, r_mult, r_ss, r_log, r_inv, r_sum, r_done, r_prod = (
            sem("r_psum"), sem("r_sq"), sem("r_mult"), sem("r_ss"), sem("r_log"), sem("r_inv"), sem("r_sum"),
            sem("r_done"), sem("r_prod"))
        wqk_ready = sem("wqk_ready")
        gate_psum, gate_step, mask_ready, mt_psum, mt_ready = (sem("gate_psum"), sem("gate_step"), sem("mask_ready"),
                                                               sem("mt_psum"), sem("mt_ready"))
        sel_ready, eh_psum, eh_ready, em_ready, top_psum = (sem("sel_ready"), sem("eh_psum"), sem("eh_ready"),
                                                            sem("em_ready"), sem("top_psum"))
        out_psum, out_ready, out_sent = sem("out_psum"), sem("out_ready"), sem("out_sent")
        idx_ready, pool_turn = sem("idx_ready"), sem("pool_turn")

        def rows(half):
            return slice(64 * half, 64 * half + 64)

        def zv(p):
            return Z[:, p, :, 0:T]

        def bank3(b, parts=slice(0, 128), n=IMG):
            return B[b][parts, 0:n * T].rearrange("p (i t) -> p i t", t=T)


        def pe_norm(pe, k, src, width, arrived):
            for p in range(PIECES):
                pe.wait_ge(*arrived(p))
                nc.tensor.matmul(B[p][:, 0:width], cen, src(p), start=True, stop=True).then_inc(centered, 1)
            for p in range(PIECES):
                pe.wait_ge(squared, 4 * k + p + 1)
                if p >= 2:
                    pe.wait_ge(logged, 4 * k + p - 1)
                nc.tensor.matmul(B[4 + p % 2][:, 0:width], avg, SQ[:, p, 0:width], start=True,
                                 stop=True).then_inc(var_psum, 1)

        def act_norm(act, k, width):
            for p in range(PIECES):
                act.wait_ge(centered, 4 * k + p + 1)
                nc.scalar.activation(SQ[:, p, 0:width], B[p][:, 0:width], ACT.Square).then_inc(squared, 1)
            for p in range(PIECES):
                act.wait_ge(var_psum, 4 * k + p + 1)
                nc.scalar.activation(RS[:, p, 0:width], B[4 + p % 2][:, 0:width], ACT.Ln,
                                     bias=eps_t[:, 0:1]).then_inc(logged, 1)
                act.wait_ge(logged, 4 * k + p + 1)
                nc.scalar.activation(RS[:, p, 0:width], RS[:, p, 0:width], ACT.Exp, scale=-0.5).then_inc(rstd_ready, 1)

        def dve_norm(dve, k, width, dst, done):
            for p in range(PIECES):
                dve.wait_ge(rstd_ready, 4 * k + p + 1)
                shape = "p (i t) -> p i t"
                t = width // IMG
                nc.vector.tensor_tensor(dst(p), B[p][:, 0:width].rearrange(shape, t=t),
                                        RS[:, p, 0:width].rearrange(shape, t=t), ALU.mult).then_inc(done, 1)

        def zn(p, t=T):
            return ZN[:, p, 0:IMG * t].rearrange("p (i t) -> p i t", t=t)

        def pool_affine(pool, k, dst, gain, shift, done):
            for p in range(PIECES):
                pool.wait_ge(normed, 4 * k + p + 1)
                pool.sem_inc(pool_turn, 1)
                nc.gpsimd.tensor_scalar(dst(p), zn(p), gain, shift, ALU.mult, ALU.add).then_inc(done, 1)


        def pe_queries(pe, a, weight, ready, w_ready):
            pe.wait_ge(*w_ready)
            for p in range(PIECES):
                pe.wait_ge(*ready(p))
                for h in range(HEADS):
                    n = HEADS * p + h
                    if n >= HEADS:
                        pe.wait_ge(q_ready, 16 * a + n - 3)
                    nc.tensor.matmul(B[4 + h][:, 0:N], weight(h), zv(p), start=True, stop=True).then_inc(q_psum, 1)

        def act_queries(act, a, bias):
            for n in range(PIECES * HEADS):
                p, h = n // HEADS, n % HEADS
                act.wait_ge(q_psum, 16 * a + n + 1)
                if bias is None:
                    nc.scalar.copy(QO[:, p, :, h, :], bank3(4 + h)).then_inc(q_ready, 1)
                else:
                    nc.scalar.activation(QO[:, p, :, h, :], bank3(4 + h), ACT.Identity,
                                         bias=bias(h)).then_inc(q_ready, 1)

        def pe_values(pe, v, weight):
            for p in range(PIECES):
                for s in range(SETS):
                    src = Z[:, p, 4 * s:4 * s + 4, :].rearrange("p i t -> p (i t)")
                    o = B[4 + p][:, 128 * s:128 * s + 128]
                    if weight is None:
                        last = nc.tensor.transpose(o, src, ident)
                    else:
                        last = nc.tensor.matmul(o, src, weight, start=True, stop=True)
                last.then_inc(v_psum, 1)

        def act_values(act, v):
            for p in range(PIECES):
                act.wait_ge(v_psum, 4 * v + p + 1)
                nc.scalar.copy(VT[:, p, :, :], B[4 + p][:, :].rearrange("p (s f) -> p s f", s=SETS)).then_inc(v_ready, 1)

        def pe_scores(pe, a, keys, bank_free):
            for m in range(TILES):
                p, half = m // 2, m % 2
                if m < 4:
                    bank_free(m)
                else:
                    pe.wait_ge(s_taken, 8 * a + m - 3)
                for i in range(IMG):
                    last = nc.tensor.matmul(B[m % 4][0:HQ, T * i:T * i + T],
                                            QO[rows(half), p, i, :, :].rearrange("p h t -> p (h t)"),
                                            keys(p)[rows(half), i, :], start=True, stop=True)
                last.then_inc(s_psum, 1)

        def dve_softmax(dve, a, scale, table):
            def centre(m):
                dve.wait_ge(s_psum, 8 * a + m + 1)
                src = bank3(m % 4, slice(0, HQ))
                e = E[:, m, :, 0:T]
                if table is not None:
                    nc.vector.scalar_tensor_tensor(e, src, scale, table, ALU.mult, ALU.add).then_inc(s_taken, 1)
                    dve.wait_ge(s_taken, 8 * a + m + 1)
                    src = e
                nc.vector.tensor_reduce(mx[:, m, :], src, AX.X, ALU.max).then_inc(maxed, 1)
                dve.wait_ge(maxed, 8 * a + m + 1)
                last = nc.vector.tensor_tensor(e, src, mx[:, m, :].unsqueeze(2).to_broadcast([HQ, IMG, T]), ALU.subtract)
                if table is None:
                    last.then_inc(s_taken, 1)
                else:
                    last.then_inc(biased, 1)

            def total(m):
                dve.wait_ge(expd, 8 * a + m + 1)
                nc.vector.tensor_reduce(sm[:, m, :], E[:, m, :, 0:T], AX.X, ALU.add).then_inc(summed, 1)
                dve.wait_ge(summed, 8 * a + m + 1)
                nc.vector.reciprocal(rc[:, m, :], sm[:, m, :]).then_inc(inv_ready, 1)

            for m in range(TILES):
                centre(m)
                if m >= 1:
                    total(m - 1)
            total(TILES - 1)

        def act_exp(act, a, scale, ready, base):
            for m in range(TILES):
                act.wait_ge(ready, base + m + 1)
                nc.scalar.activation(E[:, m, :, 0:T], E[:, m, :, 0:T], ACT.Exp, scale=scale).then_inc(expd, 1)

        def pool_probs(pool, a):
            for m in range(TILES):
                pool.wait_ge(inv_ready, 8 * a + m + 1)
                nc.gpsimd.tensor_tensor(E[:, m, :, 0:T], E[:, m, :, 0:T],
                                        rc[:, m, :].unsqueeze(2).to_broadcast([HQ, IMG, T]),
                                        ALU.mult).then_inc(probs_ready, 1)

        def pe_mix(pe, a, weight, bank_free):
            for m in range(TILES):
                if m < 4:
                    bank_free(m)
                else:
                    pe.wait_ge(pt_ready, 8 * a + m - 3)
                pe.wait_ge(probs_ready, 8 * a + m + 1)
                for s in range(SETS):
                    last = nc.tensor.transpose(B[4 + m % 4][:, HQ * s:HQ * s + HQ],
                                               E[:, m, 4 * s:4 * s + 4, :].rearrange("p i t -> p (i t)"),
                                               ident[0:HQ, 0:HQ])
                last.then_inc(pt_psum, 1)

            def project(p):
                pe.wait_ge(o_ready, 16 * a + 4 * p + 4)
                pe.wait_ge(pt_ready, 8 * a + 5 + p)
                for h in range(HEADS):
                    last = nc.tensor.matmul(B[4 + p][:, 0:N], weight(h), QO[:, p, :, h, :], start=h == 0,
                                            stop=h == HEADS - 1)
                last.then_inc(y_psum, 1)

            for p in range(PIECES):
                pe.wait_ge(pt_ready, 8 * a + 2 * p + 2)
                for j in range(4):
                    if p == 0:
                        pe.wait_ge(s_taken, 8 * a + 5 + j)
                    else:
                        pe.wait_ge(o_ready, 16 * a + 4 * p + j - 3)
                    for s in range(SETS):
                        for half in range(HALVES):
                            last = nc.tensor.matmul(B[j][rows(half), HQ * s:HQ * s + HQ],
                                                    VT[32 * j:32 * j + T, p, s, rows(half)],
                                                    PH[32 * j:32 * j + T, 2 * p + half, HQ * s:HQ * s + HQ],
                                                    start=True, stop=True)
                    last.then_inc(pv_psum, 1)
                if p >= 1:
                    project(p - 1)
            project(PIECES - 1)

        def act_mix(act, a):
            for m in range(TILES):
                act.wait_ge(pt_psum, 8 * a + m + 1)
                nc.scalar.copy(PH[:, m, :], B[4 + m % 4][:, 0:N]).then_inc(pt_ready, 1)
            for p in range(PIECES):
                for j in range(4):
                    act.wait_ge(pv_psum, 16 * a + 4 * p + j + 1)
                    nc.scalar.copy(QO[:, p, j:IMG:4, :, :].rearrange("p s h t -> p s (h t)"),
                                   B[j][:, 0:N].rearrange("p (s c) -> p s c", s=SETS)).then_inc(o_ready, 1)

        def dve_add(dve, u, produced, count, bank, bias):
            for p in range(PIECES):
                dve.wait_ge(produced, count(p))
                b = bank3(bank(p))
                if bias is None:
                    nc.vector.tensor_tensor(X[:, p], b, X[:, p], ALU.add).then_inc(x_ready, 1)
                else:
                    nc.vector.scalar_tensor_tensor(X[:, p], b, bias, X[:, p], ALU.add, ALU.add).then_inc(x_ready, 1)

        def from_x(u):
            return lambda p: (x_ready, 4 * u + p + 1)

        def x_of(p):
            return X[:, p, :, :].rearrange("p i t -> p (i t)")

        def ab(kind):
            return lambda h: AB[:, kind, h, :]

        vec = {name: lvec[:, n:n + 1] for n, name in enumerate(["ga", "ba", "bo", "gf", "bf", "b2", "b1"])}
        lw1, lw2 = lvec[:, 7:135], lvec[:, 135:199]
        egain, eshift, fgain, fshift = (evec[:, n:n + 1] for n in range(4))
        epatch_bias, ecls = evec[:, 4:5], evec[:, 5:6]
        epos = evec[:, 6:6 + T]
        wq_w, wk_w = (lambda h: winw[:, h, :]), winw[:, 2 * WIN_HEADS, :]
        wv_w, wo_w = winw[:, 2 * WIN_HEADS + 1, :], (lambda h: winw[:, WIN_HEADS + h, :])
        wbq, wbk, wbo = (lambda h: winv[:, h:h + 1]), winv[:, WIN_HEADS:WIN_HEADS + 1], \
            winv[:, WIN_HEADS + 1:WIN_HEADS + 2]
        wbv = winv[:, WIN_HEADS + 2:WIN_HEADS + 130]
        wtab = [winv[0:HQ, WIN_HEADS + 130 + T * g:WIN_HEADS + 130 + T * g + T] for g in range(2)]
        f_wi, f_wo = ffw[:, 0:128], ffw[:, 128:192]
        f_bi, f_bo, f_bs = ffw[:, 192:193], ffw[:, 193:194], ffw[:, 194:196]
        f_ws = ffw[:, 196:452].rearrange("p (l f) -> p l f", l=2)
        t_w1 = topw[:, 0:1024].rearrange("p (e f) -> p e f", e=8)
        t_w2 = topw[:, 1024:1536].rearrange("p (e f) -> p e f", e=8)
        t_b1, t_wg, t_bg = topw[:, 1536:1544], topw[:, 1544:1560], topw[:, 1560:1576]

        block = ctx.enter_context(nc.Block())

        @block.sync
        def _(sp):
            def load_image(q):
                if q >= 2:
                    sp.wait_ge(embed_psum, q - 1)
                    sp.wait_ge(img_sq, q - 1)
                sp.dma_start(img[q % 2], d["img"][q]).then_inc(img_in[q % 2], 16)

            sp.dma_start(WA[:, :, 64:128], d["w_patch"]).then_inc(w_embed, 16)
            sp.dma_start(lnp, d["ln_p1"]).then_inc(w_embed, 16)
            sp.dma_start(evec[:, :], d["evec"]).then_inc(w_embed, 16)
            sp.dma_start(consts[:, :], d["consts"]).then_inc(w_const, 16)
            load_image(0)
            load_image(1)
            sp.dma_start(LW[:, :], d["layers"][0]).then_inc(w_layer, 16)
            sp.dma_start(route[:, :], d["route"]).then_inc(w_route, 16)
            sp.dma_start(b2d[:, :], d["top_b2"]).then_inc(w_route, 16)
            for q in range(2, TILES):
                load_image(q)
            sp.wait_ge(stage_done, 1)
            sp.wait_ge(embedded, 16)
            sp.wait_ge(sq_psum, TILES)
            for dst, name in ((winw, "win_w"), (winv, "win_v"), (rotw, "rot_w"), (rotv, "rot_v"), (ffw, "ff_w"),
                              (rw, "ff_r"), (topw, "top_w")):
                sp.dma_start(dst, d[name]).then_inc(w_late, 16)
            with sp.Fori(1, LAYERS) as i:
                sp.wait_ge(layer_used, 2 * i)
                sp.dma_start(LW[:, :], d["layers"][bass.ds(i, 1)].rearrange("a p n -> (a p) n")).then_inc(w_layer, 16)
            for p in range(PIECES):
                sp.wait_ge(out_ready, p + 1)
                for half in range(HALVES):
                    sp.dma_start(out[HALVES * p + half], QO[0:HQ, p].rearrange("p i h t -> p (i h t)")[:, 0:512]
                                 .rearrange("p (s h f) -> p s h f", s=SETS, h=2)[:, :, half, :]).then_inc(out_sent, 16)
            sp.wait_ge(out_sent, 16 * TILES)

        @block.tensor
        def _(pe):
            def embed_rows(q):
                half = q % 2
                pe.wait_ge(img_in[q % 2], 16 * (q // 2 + 1))
                if q >= 2:
                    pe.wait_ge(embedded, 2 * (q - 1))
                lo = 64 if half == 0 else 0
                for c in range(CHUNKS):
                    last = nc.tensor.matmul(B[q % 2][:, 0:NP], WA[:, c, lo:lo + 128], img[q % 2][:, c, :],
                                            start=c == 0, stop=c == CHUNKS - 1)
                last.then_inc(embed_psum, 1)

            def embed_squares(q):
                pe.wait_ge(img_sum, q + 1)
                if q >= 2:
                    pe.wait_ge(e_var, q - 1)
                nc.tensor.matmul(B[2 + q % 2][:, 0:NP], ones[:, :], SQ[:, 0, 0:NP], start=True,
                                 stop=True).then_inc(sq_psum, 1)

            pe.wait_ge(scaled, 2)
            for c in range(CHUNKS):
                last = nc.tensor.matmul(B[4][:, 0:64], ones[:, :], WA[:, c, 64:128], start=c == 0,
                                        stop=c == CHUNKS - 1)
            last.then_inc(colsum, 1)
            pe.wait_ge(cvec_psum, 1)
            for half in range(HALVES):
                for c in range(CHUNKS):
                    last = nc.tensor.matmul(B[5 + half][rows(half), 0:1], sqi[:, c, 0:64], lnp[:, 1, c:c + 1],
                                            start=c == 0, stop=c == CHUNKS - 1)
            last.then_inc(cvec_ready, 1)
            pe.wait_ge(wa_ready, 1)
            for q in range(TILES):
                embed_rows(q)
                if q >= 1:
                    embed_squares(q - 1)
            embed_squares(TILES - 1)
            pe.wait_ge(w_const, 16)
            pe_norm(pe, K_EMBED, lambda p: QO[:, p].rearrange("p i h t -> p (i h t)")[:, 0:NP], NP,
                    lambda p: (embedded, 2 * TILES))

            with pe.Fori(0, LAYERS) as i:
                pe.wait_ge(w_layer, 16 * i + 16)
                pe.wait_ge(x_ready, 8 * i + 4)
                for h in range(HEADS):
                    r = rows(h % 2)
                    hp = h // 2
                    o = B[6 + h % 2]
                    nc.tensor.matmul(o[:, 128 * hp:128 * hp + 64], LW[r, L_Q + 128 * hp:L_Q + 128 * hp + 128],
                                     LW[r, L_K + 64 * hp:L_K + 64 * hp + 64], start=True, stop=True)
                    last = nc.tensor.matmul(o[:, 128 * hp + 64:128 * hp + 128],
                                            LW[r, L_V + 128 * hp:L_V + 128 * hp + 128],
                                            LW[r, L_O + 64 * hp:L_O + 64 * hp + 64], start=True, stop=True)
                last.then_inc(ab_psum, 1)
                pe_norm(pe, 1 + 2 * i, x_of, N, from_x(2 * i))
                pe.wait_ge(logged, 8 * i + 8)
                pe_queries(pe, i, ab(0), lambda p: (h_ready, 8 * i + p + 1), (ab_ready, 8 * i + 8))
                for p in range(PIECES):
                    pe.wait_ge(q_ready, 16 * i + 13 + p)
                pe_values(pe, i, None)
                pe_scores(pe, i, zv, lambda m: None)
                pe_mix(pe, i, ab(1), lambda m: pe.wait_ge(v_ready, 4 * i + m + 1))
                pe_norm(pe, 2 + 2 * i, x_of, N, from_x(2 * i + 1))
                for m in range(TILES):
                    p, half = m // 2, m % 2
                    pe.wait_ge(h_ready, 8 * i + 5 + p)
                    if m in (2, 3):
                        pe.wait_ge(logged, 8 * i + 9 + m)
                    if m >= 4:
                        pe.wait_ge(hid_ready, 8 * i + m - 3)
                    nc.tensor.matmul(B[4 + (m + 2) % 4][:, 0:N], lw1[rows(half), :], zv(p)[rows(half)], start=True,
                                     stop=True).then_inc(hid_psum, 1)
                for p in range(PIECES):
                    pe.wait_ge(hid_ready, 8 * i + 2 * p + 2)
                    for half in range(HALVES):
                        last = nc.tensor.matmul(B[p][rows(half), 0:N], lw2, PH[:, 2 * p + half, :], start=True,
                                                stop=True)
                    last.then_inc(down_psum, 1)

            pe_norm(pe, K_FINAL, x_of, N, from_x(X_FINAL - 1))

            pe_norm(pe, K_WIN, x_of, N, from_x(X_FINAL))
            pe.wait_ge(w_late, 16 * 7)
            for p in range(PIECES):
                pe.wait_ge(h_ready, 4 * H_WIN + p + 1)
                nc.tensor.matmul(B[p][:, 0:N], wk_w, zv(p), start=True, stop=True).then_inc(k_psum, 1)
            for g in range(WIN_PASSES):
                a = A_WIN + g
                if g == 0:
                    pe.wait_ge(logged, 4 * K_WIN + 4)
                else:
                    pe.wait_ge(x_ready, 4 * X_WIN + 4)
                pe_queries(pe, a, lambda h: wq_w(HEADS * g + h), lambda p: (h_ready, 4 * H_WIN + p + 1),
                           (w_late, 16 * 7))
                for p in range(PIECES):
                    pe.wait_ge(q_ready, 16 * a + 13 + p)
                if g == 0:
                    pe_values(pe, 4, wv_w)
                    pe.wait_ge(k_ready, PIECES)
                    pe_scores(pe, a, lambda p: KT[:, p], lambda m: None)
                else:
                    pe_scores(pe, a, lambda p: KT[:, p], lambda m: pe.wait_ge(o_ready, 16 * a - 3 + m))
                pe_mix(pe, a, lambda h: wo_w(HEADS * g + h), lambda m: pe.wait_ge(v_ready, 17 + m))

            pe_norm(pe, K_FFN, x_of, N, from_x(X_WIN + 1))
            for m in range(TILES):
                p, half = m // 2, m % 2
                pe.wait_ge(h_ready, 4 * H_FFN + p + 1)
                if m in (2, 3):
                    pe.wait_ge(logged, 4 * K_FFN + 1 + m)
                if m >= 4:
                    pe.wait_ge(fh_ready, m - 3)
                nc.tensor.matmul(B[4 + (m + 2) % 4][:, 0:N], f_wi[rows(half), :], zv(p)[rows(half)], start=True,
                                 stop=True).then_inc(fh_psum, 1)
            for l in range(FFN_LAYERS):
                for m in range(TILES):
                    n = TILES * l + m
                    if l == 0:
                        pe.wait_ge(fh_ready, TILES if m < 1 else m + 1)
                        if m >= 4:
                            pe.wait_ge(g_biased, n - 3)
                    else:
                        pe.wait_ge(g_ready, m + 1)
                        if m >= 4:
                            pe.wait_ge(g_biased, n - 3)
                    pe.wait_ge(picked_ready, n + 1)
                    for w in range(PAIRS):
                        last = nc.tensor.matmul(B[4 * l + m % 4][:, 2 * T * w:2 * T * w + 2 * T],
                                                picked[:, n % 2, w, 0:128], PH[:, m, 2 * T * w:2 * T * w + 2 * T],
                                                start=True, stop=True)
                    last.then_inc(g_psum, 1)
            for p in range(PIECES):
                pe.wait_ge(g_ready, TILES + 2 * p + 2)
                for half in range(HALVES):
                    last = nc.tensor.matmul(B[p][rows(half), 0:N], f_wo, PH[:, 2 * p + half, :], start=True, stop=True)
                last.then_inc(fo_psum, 1)

            pe_norm(pe, K_ROT, x_of, N, from_x(X_FFN))

            def turned(r, w, w_swapped, p):
                if r >= 2:
                    pe.wait_ge(r_mult, r - 1)
                nc.tensor.matmul(B[r % 2][:, 0:N], w, zv(p), start=True, stop=True)
                nc.tensor.matmul(B[2 + r % 2][:, 0:N], w_swapped, zv(p), start=True, stop=True).then_inc(r_psum, 1)

            def lengths(r):
                pe.wait_ge(r_sq, r + 1)
                if r >= 2:
                    pe.wait_ge(r_log, r - 1)
                nc.tensor.matmul(B[4 + r % 2][:, 0:N], avg, rope[:, 2, r % 2, :], start=True, stop=True).then_inc(r_ss, 1)

            for p in range(PIECES):
                pe.wait_ge(h_ready, 4 * H_ROT + p + 1)
            pe.wait_ge(logged, 4 * K_ROT + 4)
            for p in range(PIECES):
                turned(p, rotw[:, 3 * ROT_HEADS, :], rotw[:, 3 * ROT_HEADS + 1, :], p)
                if p >= 1:
                    lengths(p - 1)
            for g in range(ROT_PASSES):
                a = A_ROT + g
                if g:
                    for j in range(4):
                        pe.wait_ge(o_ready, 16 * a - 3 + j)
                    pe.wait_ge(x_ready, 4 * (X_ROT + g - 1) + 4)
                for n in range(PIECES * HEADS):
                    r = PIECES + 16 * g + n
                    hh = HEADS * g + n % HEADS
                    turned(r, rotw[:, hh, :], rotw[:, ROT_HEADS + hh, :], n // HEADS)
                    if n or g == 0:
                        lengths(r - 1)
                lengths(PIECES + 16 * g + 15)
                r_last = PIECES + 16 * g + 16
                pe.wait_ge(r_log, r_last)
                pe.wait_ge(r_done, r_last)
                if g == 0:
                    pe_values(pe, 5, rotw[:, 3 * ROT_HEADS + 2, :])
                pe_scores(pe, a, lambda p: KT[:, p], lambda m: None)
                pe_mix(pe, a, lambda h: rotw[:, 2 * ROT_HEADS + HEADS * g + h, :],
                       lambda m: pe.wait_ge(v_ready, 21 + m))

            pe_norm(pe, K_TOP, x_of, N, from_x(X_TOP - 1))
            for p in range(PIECES):
                pe.wait_ge(h_ready, 4 * H_TOP + p + 1)
            for p in range(PIECES):
                for s in range(SETS):
                    n = SETS * p + s
                    last = nc.tensor.matmul(B[6][:, 16 * n:16 * n + 16],
                                            Z[:, p, 4 * s:4 * s + 4, :].rearrange("p i t -> p (i t)"), t_wg,
                                            start=True, stop=True)
            last.then_inc(gate_psum, 1)
            pe.wait_ge(mask_ready, 1)
            pe.wait_ge(logged, 4 * K_TOP + 4)
            for p in range(PIECES):
                for s in range(SETS):
                    n = SETS * p + s
                    last = nc.tensor.transpose(B[4 + p][0:16, 128 * s:128 * s + 128],
                                               gate[:, 2, 2 * n:2 * n + 2, :].rearrange("p a e -> p (a e)"), ident)
                last.then_inc(mt_psum, 1)
            pe.wait_ge(mt_ready, 2 * PIECES)
            pe.wait_ge(sel_ready, 1)
            pe.wait_ge(w_route, 32)
            for p in range(PIECES):
                nc.tensor.matmul(B[p][:, 0:N], b2d[:, :], mk32[:, p], start=True, stop=False, skip_group_check=True)

            def expert_up(n):
                e, m = n // TILES, n % TILES
                p, half = m // 2, m % 2
                if n >= 2:
                    pe.wait_ge(em_ready, n - 1)
                nc.tensor.matmul(B[4 + n % 2][:, 0:N], t_w1[rows(half), e, :], zv(p)[rows(half)], start=True, stop=True)
                nc.tensor.matmul(B[6 + n % 2][:, 0:N], selb[:, 8 * half + e:8 * half + e + 1].to_broadcast([16, 128]), mkb[:, p, :], start=True,
                                 stop=True).then_inc(eh_psum, 1)

            def expert_down(n):
                e, m = n // TILES, n % TILES
                p, half = m // 2, m % 2
                pe.wait_ge(em_ready, n + 1)
                nc.tensor.matmul(B[p][rows(half), 0:N], t_w2[:, e, :], PH[:, m, :], start=False,
                                 stop=e == TOP_EXPERTS - 1, skip_group_check=True).then_inc(top_psum, 1)

            for n in range(TOP_EXPERTS * TILES):
                expert_up(n)
                if n >= 2:
                    expert_down(n - 2)
            expert_down(TOP_EXPERTS * TILES - 2)
            expert_down(TOP_EXPERTS * TILES - 1)

            for p in range(PIECES):
                pe.wait_ge(x_ready, 4 * X_TOP + p + 1)
                for s in range(SETS):
                    last = nc.tensor.transpose(B[p][0:HQ, 128 * s:128 * s + 128],
                                               X[:, p, 4 * s:4 * s + 4, :].rearrange("p i t -> p (i t)"), ident)
                last.then_inc(out_psum, 1)

        @block.scalar
        def _(act):
            nc.scalar.preload_act_table_set("natural_log_exp_and_others")
            act.wait_ge(cvec_ready, 1)
            act.wait_ge(w_embed, 48)
            for half in range(HALVES):
                last = nc.scalar.activation(ZN[rows(half), 0, 0:1], B[5 + half][rows(half), 0:1], ACT.Identity,
                                            bias=epatch_bias[rows(half)])
            last.then_inc(mean_sq, 1)
            act.wait_ge(cvec_ready, 1)
            for q in range(TILES):
                half = q % 2
                act.wait_ge(img_in[q % 2], 16 * (q // 2 + 1))
                if q >= 1:
                    act.wait_ge(img_sum, q)
                nc.scalar.activation(sqi, img[q % 2], ACT.Square).then_inc(img_sq, 1)
                act.wait_ge(embed_psum, q + 1)
                if q >= 1:
                    act.wait_ge(e_var, q)
                nc.scalar.activation(SQ[rows(half), 1, 0:NP], B[q % 2][rows(1 - half), 0:NP], ACT.Square,
                                     scale=1.0 / FEATURES).then_inc(mean_sq, 1)
                act.wait_ge(e_var, q + 1)
                nc.scalar.activation(RS[rows(half), 0, 0:NP], RS[rows(half), 0, 0:NP], ACT.Ln,
                                     bias=eps_t[rows(half), 0:1]).then_inc(e_log, 1)
                act.wait_ge(e_log, q + 1)
                nc.scalar.activation(RS[rows(half), 0, 0:NP], RS[rows(half), 0, 0:NP], ACT.Exp,
                                     scale=-0.5).then_inc(e_rstd, 1)
            act_norm(act, K_EMBED, NP)

            with act.Fori(0, LAYERS) as i:
                act.wait_ge(ab_psum, i + 1)
                if True:
                    for kind in range(2):
                        for h in range(HEADS):
                            src = B[6 + h % 2][:, 128 * (h // 2) + 64 * kind:128 * (h // 2) + 64 * kind + 64]
                            nc.scalar.copy(AB[0:64, kind, h, 0:64], src[0:64])
                            last = nc.scalar.copy(AB[64:128, kind, h, 64:128], src[64:128])
                            last.then_inc(ab_ready, 1)
                act.wait_ge(ab_ready, 8 * i + 8)
                act.sem_inc(layer_used, 1)
                act_norm(act, 1 + 2 * i, N)
                act_queries(act, i, None)
                act_values(act, i)
                act_exp(act, i, DIM ** -0.5, s_taken, 8 * i)
                act_mix(act, i)
                act_norm(act, 2 + 2 * i, N)
                for m in range(TILES):
                    act.wait_ge(hid_psum, 8 * i + m + 1)
                    nc.scalar.activation(PH[:, m, :], B[4 + (m + 2) % 4][:, 0:N], ACT.Gelu,
                                         bias=vec["b1"]).then_inc(hid_ready, 1)
                nc.scalar.preload_act_table_set("natural_log_exp_and_others")
            act_norm(act, K_FINAL, N)

            act_norm(act, K_WIN, N)
            act.wait_ge(w_late, 16 * 7)
            for p in range(PIECES):
                act.wait_ge(k_psum, p + 1)
                nc.scalar.activation(KT[:, p], bank3(p), ACT.Identity, bias=wbk).then_inc(k_ready, 1)
            for g in range(WIN_PASSES):
                a = A_WIN + g
                act_queries(act, a, lambda h: wbq(HEADS * g + h))
                act_exp(act, a, 1.0, biased, 8 * g)
                act_mix(act, a)

            act_norm(act, K_FFN, N)
            for m in range(TILES):
                act.wait_ge(fh_psum, m + 1)
                nc.scalar.activation(PH[:, m, :], B[4 + (m + 2) % 4][:, 0:N], ACT.Relu, bias=f_bi).then_inc(fh_ready, 1)
            for n in range(FFN_LAYERS * TILES):
                act.wait_ge(g_biased, n + 1)
                nc.scalar.activation(PH[:, n % TILES, :], PH[:, n % TILES, :], ACT.Relu).then_inc(g_ready, 1)

            act_norm(act, K_ROT, N)

            def rope_square(r):
                act.wait_ge(r_psum, r + 1)
                if r >= 2:
                    act.wait_ge(r_ss, r - 1)
                nc.scalar.activation(rope[:, 2, r % 2, :], B[r % 2][:, 0:N], ACT.Square).then_inc(r_sq, 1)

            def rope_inverse(r):
                act.wait_ge(r_ss, r + 1)
                if r >= 2:
                    act.wait_ge(r_done, r - 1)
                nc.scalar.activation(rope[:, 3, r % 2, :], B[4 + r % 2][:, 0:N], ACT.Ln,
                                     bias=eps_t[:, 1:2]).then_inc(r_log, 1)
                act.wait_ge(r_log, r + 1)
                nc.scalar.activation(rope[:, 3, r % 2, :], rope[:, 3, r % 2, :], ACT.Exp, scale=-0.5).then_inc(r_inv, 1)

            r = 0
            for g in range(ROT_PASSES):
                count = 16 + (PIECES if g == 0 else 0)
                for n in range(count):
                    rope_square(r)
                    if n:
                        rope_inverse(r - 1)
                    r += 1
                rope_inverse(r - 1)
                if g == 0:
                    act_values(act, 5)
                act_exp(act, A_ROT + g, 1.0, biased, 8 * (WIN_PASSES + g))
                act_mix(act, A_ROT + g)

            act_norm(act, K_TOP, N)
            for p in range(PIECES):
                act.wait_ge(mt_psum, p + 1)
                src = B[4 + p][0:16, :].rearrange("p (i t) -> p i t", t=PAD)[:, :, 0:T]
                nc.scalar.copy(mk32[:, p], src).then_inc(mt_ready, 1)
                nc.scalar.copy(mkb[:, p, :].rearrange("p (i t) -> p i t", t=T), src).then_inc(mt_ready, 1)
            for n in range(TOP_EXPERTS * TILES):
                e, m = n // TILES, n % TILES
                act.wait_ge(eh_psum, n + 1)
                if n >= TILES:
                    act.wait_ge(top_psum, n - TILES + 1)
                nc.scalar.activation(PH[:, m, :], B[4 + n % 2][:, 0:N], ACT.Gelu, bias=t_b1[:, e:e + 1]).then_inc(eh_ready, 1)
            for p in range(PIECES):
                act.wait_ge(out_psum, p + 1)
                nc.scalar.copy(QO[0:HQ, p].rearrange("p i h t -> p (i h t)")[:, 0:512],
                               B[p][0:HQ, :]).then_inc(out_ready, 1)

        @block.vector
        def _(dve):
            nc.vector.memset(ones[:, :], 1.0)
            nc.vector.memset(WA[:, :, 0:64], 1.0).then_inc(scaled, 1)
            nc.vector.memset(WA[:, :, 128:192], 1.0)
            nc.vector.memset(eps_t[:, 0:1], EPS)
            nc.vector.memset(eps_t[:, 1:2], RMS_EPS).then_inc(pads_zero, 1)
            dve.wait_ge(w_embed, 48)
            nc.vector.tensor_copy(sqi[:, :, 0:64], WA[:, :, 64:128]).then_inc(cvec_psum, 1)
            dve.wait_ge(cvec_psum, 1)
            nc.vector.tensor_tensor(WA[:, :, 64:128], WA[:, :, 64:128],
                                    lnp[:, 0, :].unsqueeze(2).to_broadcast([128, CHUNKS, 64]),
                                    ALU.mult).then_inc(scaled, 1)
            dve.wait_ge(colsum, 1)
            nc.vector.tensor_scalar(ZN[:, 1, 0:64], B[4][:, 0:64], 1.0 / FEATURES, None, ALU.mult).then_inc(colsum, 1)
            dve.wait_ge(colsum, 2)
            nc.vector.tensor_tensor(WA[:, :, 64:128], WA[:, :, 64:128],
                                    ZN[:, 1, 0:64].unsqueeze(1).to_broadcast([128, CHUNKS, 64]),
                                    ALU.subtract).then_inc(wa_ready, 1)

            for q in range(TILES):
                p, half = q // 2, q % 2
                dve.wait_ge(img_sq, q + 1)
                if q >= 1:
                    dve.wait_ge(sq_psum, q)
                nc.vector.tensor_reduce(SQ[:, 0, 0:NP], sqi.rearrange("p c n -> p n c"), AX.X, ALU.add).then_inc(img_sum, 1)
                dve.wait_ge(sq_psum, q + 1)
                dve.wait_ge(mean_sq, q + 2)
                nc.vector.scalar_tensor_tensor(RS[rows(half), 0, 0:NP], B[2 + q % 2][rows(half), 0:NP], 1.0 / FEATURES,
                                               SQ[rows(half), 1, 0:NP], ALU.mult, ALU.subtract).then_inc(e_var, 1)
                dve.wait_ge(e_rstd, q + 1)
                y = QO[rows(half), p].rearrange("p i h t -> p (i h t)")[:, 0:NP]
                nc.vector.tensor_tensor(y, B[q % 2][rows(half), 0:NP], RS[rows(half), 0, 0:NP], ALU.mult).then_inc(embedded, 1)
                dve.wait_ge(embedded, 2 * q + 1)
                nc.vector.tensor_scalar(y, y, ZN[rows(half), 0, 0:1], None, ALU.add).then_inc(embedded, 1)
            dve.sem_inc(stage_done, 1)
            dve_norm(dve, K_EMBED, NP, lambda p: zn(p, PATCHES), normed)

            with dve.Fori(0, LAYERS) as i:
                dve_norm(dve, 1 + 2 * i, N, lambda p: zn(p), normed)
                dve_softmax(dve, i, 1.0, None)
                dve_add(dve, 2 * i + 1, y_psum, lambda p: 4 * i + p + 1, lambda p: 4 + p, vec["bo"])
                dve_norm(dve, 2 + 2 * i, N, lambda p: zn(p), normed)
                dve_add(dve, 2 * i + 2, down_psum, lambda p: 4 * i + p + 1, lambda p: p, vec["b2"])
            dve_norm(dve, K_FINAL, N, lambda p: zn(p), normed)

            dve_norm(dve, K_WIN, N, zv, h_ready)
            for g in range(WIN_PASSES):
                a = A_WIN + g
                if g == 0:
                    dve.wait_ge(w_late, 16 * 7)
                    for p in range(PIECES):
                        dve.wait_ge(v_psum, 17 + p)
                        nc.vector.tensor_tensor(VT[:, p, :, :], B[4 + p][:, :].rearrange("p (s f) -> p s f", s=SETS),
                                                wbv.unsqueeze(1).to_broadcast([128, SETS, 128]),
                                                ALU.add).then_inc(v_ready, 1)
                dve_softmax(dve, a, WIN_DH ** -0.5, wtab[g].unsqueeze(1).to_broadcast([HQ, IMG, T]))
                dve_add(dve, X_WIN + g, y_psum, lambda p: 4 * a + p + 1, lambda p: 4 + p, wbo if g == 0 else None)

            dve_norm(dve, K_FFN, N, zv, h_ready)
            for n in range(FFN_LAYERS * TILES):
                m, l = n % TILES, n // TILES
                dve.wait_ge(g_psum, n + 1)
                nc.vector.tensor_tensor(PH[:, m, :].rearrange("p (w c) -> p w c", w=PAIRS),
                                        B[4 * l + m % 4][:, 0:N].rearrange("p (w c) -> p w c", w=PAIRS),
                                        picked[:, n % 2, :, 128:129].to_broadcast([128, PAIRS, 2 * T]),
                                        ALU.add).then_inc(g_biased, 1)
            dve_add(dve, X_FFN, fo_psum, lambda p: p + 1, lambda p: p, f_bo)

            dve_norm(dve, K_ROT, N, zv, h_ready)

            def rope_mult(r):
                dve.wait_ge(r_psum, r + 1)
                if r >= 2:
                    dve.wait_ge(r_done, r - 1)

                def turn(k, table, bank):
                    return nc.vector.tensor_tensor(rope[:, k, r % 2, :].rearrange("p (i t) -> p i t", t=T), bank3(bank),
                                                   table.unsqueeze(1).to_broadcast([128, IMG, T]), ALU.mult)
                turn(1, sin_t, 2 + r % 2)
                dve.wait_ge(r_sq, r + 1)
                turn(0, cos_t, r % 2).then_inc(r_mult, 1)

            r = 0
            for g in range(ROT_PASSES):
                for n in range(16 + (PIECES if g == 0 else 0)):
                    rope_mult(r)
                    r += 1
                dve_softmax(dve, A_ROT + g, DIM ** -0.5, causal[0:HQ].unsqueeze(1).to_broadcast([HQ, IMG, T]))
                dve_add(dve, X_ROT + g, y_psum, lambda p: 4 * (A_ROT + g) + p + 1, lambda p: 4 + p, None)

            dve_norm(dve, K_TOP, N, zv, h_ready)
            step = [0]

            def chained(instruction):
                step[0] += 1
                instruction.then_inc(gate_step, 1)
                dve.wait_ge(gate_step, step[0])

            def bc(t, shape=(128, 32, 8)):
                return t.unsqueeze(2).to_broadcast(list(shape))

            scores, work, mask = gate[:, 0], gate[:, 1], gate[:, 2]
            order = idx[:, :].unsqueeze(1).to_broadcast([128, 32, 8])
            dve.wait_ge(gate_psum, 1)
            dve.wait_ge(idx_ready, 1)
            chained(nc.vector.tensor_tensor(gate[:, 0].rearrange("p (n a) e -> p n (a e)", a=2),
                                            B[6][:, 0:256].rearrange("p (n c) -> p n c", c=16),
                                            t_bg.unsqueeze(1).to_broadcast([128, 16, 16]), ALU.add))
            for rank in range(2):
                chained(nc.vector.tensor_reduce(gmax[:, :], scores, AX.X, ALU.max))
                chained(nc.vector.tensor_tensor(work, scores, bc(gmax[:, :]), ALU.is_equal))
                chained(nc.vector.tensor_tensor(work, work, order, ALU.mult))
                chained(nc.vector.tensor_reduce(gmax[:, :], work, AX.X, ALU.max))
                if rank == 0:
                    chained(nc.vector.tensor_tensor(mask, work, bc(gmax[:, :]), ALU.is_equal))
                    chained(nc.vector.scalar_tensor_tensor(scores, mask, -3e38, scores, ALU.mult, ALU.add))
                else:
                    chained(nc.vector.tensor_tensor(work, work, bc(gmax[:, :]), ALU.is_equal))
                    nc.vector.tensor_tensor(mask, mask, work, ALU.add).then_inc(mask_ready, 1)
            for n in range(TOP_EXPERTS * TILES):
                dve.wait_ge(eh_ready, n + 1)
                nc.vector.tensor_tensor(PH[:, n % TILES, :], B[6 + n % 2][:, 0:N], PH[:, n % TILES, :],
                                        ALU.mult).then_inc(em_ready, 1)
            dve_add(dve, X_TOP, top_psum, lambda p: TOP_EXPERTS * TILES - TILES + 2 * p + 2, lambda p: p, None)

        @block.gpsimd
        def _(pool):
            nc.gpsimd.memset(Z[:, :, :, :], 0.0)
            nc.gpsimd.memset(E[:, :, :, :], 0.0)
            nc.gpsimd.memset(AB[:, :, :, :], 0.0)
            for e in range(TOP_EXPERTS):
                nc.gpsimd.memset(idx[:, e:e + 1], float(TOP_EXPERTS - e))
            nc.gpsimd.memset(gmax[:, 0:1], 0.0).then_inc(idx_ready, 1)
            pool.wait_ge(w_embed, 48)
            pool.wait_ge(idx_ready, 1)
            nc.gpsimd.tensor_scalar(evec[:, 7:6 + T], evec[:, 7:6 + T], eshift, None, ALU.add).then_inc(gained, 1)
            nc.gpsimd.tensor_tensor(evec[:, 6:7], evec[:, 6:7], ecls, ALU.add).then_inc(gained, 1)
            pool.wait_ge(gained, 2)
            for p in range(PIECES):
                pool.wait_ge(normed, p + 1)
                nc.gpsimd.tensor_scalar(zn(p, PATCHES), zn(p, PATCHES), egain, None, ALU.mult).then_inc(gained, 1)
                pool.wait_ge(gained, p + 3)
                nc.gpsimd.tensor_tensor(X[:, p, :, 1:T], zn(p, PATCHES),
                                        epos[:, 1:T].unsqueeze(1).to_broadcast([128, IMG, PATCHES]), ALU.add)
                nc.gpsimd.tensor_copy(X[:, p, :, 0:1],
                                      epos[:, 0:1].unsqueeze(1).to_broadcast([128, IMG, 1])).then_inc(x_ready, 1)
            with pool.Fori(0, LAYERS) as i:
                pool.wait_ge(w_layer, 16 * i + 16)
                pool.wait_ge(x_ready, 8 * i + 4)
                pool.sem_inc(pool_turn, 1)
                nc.gpsimd.tensor_copy(lvec[:, 0:7], LW[:, L_VEC:L_VEC + 7])
                nc.gpsimd.tensor_copy(lvec[:, 7:199], LW[:, L_W1:L_W1 + 192]).then_inc(lvec_ready, 1)
                pool.wait_ge(lvec_ready, i + 1)
                pool.sem_inc(layer_used, 1)
                pool_affine(pool, 1 + 2 * i, zv, vec["ga"], vec["ba"], h_ready)
                pool_probs(pool, i)
                pool_affine(pool, 2 + 2 * i, zv, vec["gf"], vec["bf"], h_ready)
            pool_affine(pool, K_FINAL, lambda p: X[:, p], fgain, fshift, x_ready)

            pool.wait_ge(w_late, 16 * 7)
            pool.wait_ge(w_const, 16)
            for l in range(FFN_LAYERS):
                for e in range(EXPERTS):
                    n = EXPERTS * l + e
                    if e == 0:
                        nc.gpsimd.tensor_tensor(f_ws[:, l, :], f_ws[:, l, :], ident, ALU.add).then_inc(rw_part, 1)
                        pool.wait_ge(rw_part, l + 1)
                    nc.gpsimd.tensor_tensor(rw[:, n, 0:128], rw[:, n, 0:128], f_ws[:, l, :], ALU.add)
                nc.gpsimd.tensor_scalar(rw[:, EXPERTS * l:EXPERTS * l + EXPERTS, 128:129],
                                        rw[:, EXPERTS * l:EXPERTS * l + EXPERTS, 128:129], f_bs[:, l:l + 1], None,
                                        ALU.add).then_inc(rw_ready, 1)
            pool.wait_ge(w_route, 32)
            nc.gpsimd.tensor_copy(selb[:, :], ident[0:16, 0:16]).then_inc(sel_ready, 1)
            nc.gpsimd.tensor_tensor(rotv[:, 0:1], rotv[:, 0:1], rotv[:, 1:2], ALU.mult).then_inc(wqk_ready, 1)
            for g in range(WIN_PASSES):
                pool_probs(pool, A_WIN + g)
            pool.wait_ge(rw_ready, 2)
            for n in range(FFN_LAYERS * TILES):
                l, m = n // TILES, n % TILES
                if n >= 2:
                    pool.wait_ge(g_biased, n - 1)
                for w in range(PAIRS):
                    expert = pool.value_load(route[0:1, PAIRS * m + w:PAIRS * m + w + 1], min_val=0,
                                             max_val=EXPERTS - 1)
                    last = nc.gpsimd.tensor_copy(picked[:, n % 2, w, :],
                                                 rw[:, bass.ds(expert + EXPERTS * l, 1), :]
                                                 .rearrange("p a c -> p (a c)"))
                last.then_inc(picked_ready, 1)

            def rope_finish(r, dst, gain):
                a_, b_, inv = rope[:, 0, r % 2, :], rope[:, 1, r % 2, :], rope[:, 3, r % 2, :]
                pool.wait_ge(r_mult, r + 1)
                nc.gpsimd.tensor_tensor(a_, a_, b_, ALU.add).then_inc(r_sum, 1)
                pool.wait_ge(r_sum, r + 1)
                pool.wait_ge(r_inv, r + 1)
                a3, i3 = (v.rearrange("p (i t) -> p i t", t=T) for v in (a_, inv))
                if gain is None:
                    nc.gpsimd.tensor_tensor(dst, a3, i3, ALU.mult).then_inc(r_done, 1)
                else:
                    nc.gpsimd.tensor_tensor(a3, a3, i3, ALU.mult).then_inc(r_prod, 1)
                    pool.wait_ge(r_prod, r + 1)
                    nc.gpsimd.tensor_scalar(dst, a3, gain, None, ALU.mult).then_inc(r_done, 1)

            pool.wait_ge(wqk_ready, 1)
            for p in range(PIECES):
                rope_finish(p, KT[:, p], rotv[:, 0:1])
            for g in range(ROT_PASSES):
                for n in range(16):
                    rope_finish(PIECES + 16 * g + n, QO[:, n // HEADS, :, n % HEADS, :], None)
                pool_probs(pool, A_ROT + g)


def _blocks(maps):
    n, k, m = maps.shape
    full = np.zeros((2 * k, n, 2 * m), maps.dtype)
    full[:k, :, :m] = full[k:, :, m:] = maps.transpose(1, 0, 2)
    return full


def _twice(a, axis=0):
    return np.concatenate([a, a], axis=axis)


def _rows(*vectors):
    return np.stack([_twice(v) for v in vectors], axis=1)


def _laid_out(v):
    f = {}
    g = lambda name: np.asarray(v[name])
    x = g("x").reshape(IMAGES, CHANNELS, GRID, PATCH, GRID, PATCH).transpose(1, 3, 5, 0, 2, 4)
    f["img"] = x.reshape(CHUNKS, 128, TILES, NP).transpose(2, 1, 0, 3)
    f["w_patch"] = g("L0_tok_W_patch").reshape(CHUNKS, 128, DIM).transpose(1, 0, 2)
    f["ln_p1"] = np.stack([g("L0_tok_ln_p1_g").reshape(CHUNKS, 128).T, g("L0_tok_ln_p1_b").reshape(CHUNKS, 128).T], 1)
    f["evec"] = np.concatenate([_rows(*(g("L0_tok_" + n) for n in ("ln_p2_g", "ln_p2_b", "ln_f_g", "ln_f_b",
                                                                  "b_patch"))),
                                _rows(g("L0_tok_cls").reshape(DIM)), _twice(g("L0_tok_pos").reshape(T, DIM).T)], 1)
    layers = []
    for i in range(LAYERS):
        def heads(m, twice):
            m = m.reshape(2, 128, DIM).transpose(1, 0, 2)
            return (np.concatenate([m, m], 2) if twice else m).reshape(128, -1)
        qkv = g("L0_tok_Wqkv")[i].T.reshape(3, HEADS * DIM, DIM)
        layers.append(np.concatenate(
            [heads(qkv[0], True), heads(qkv[1], False), heads(qkv[2], True), heads(g("L0_tok_Wo")[i], False),
             _twice(g("L0_tok_W1")[i]), g("L0_tok_W2")[i],
             _rows(*(g("L0_tok_" + n)[i] for n in ("attn_ln_g", "attn_ln_b", "bo", "ff_ln_g", "ff_ln_b", "b2"))),
             g("L0_tok_b1")[i][:, None]], 1))
    f["layers"] = np.stack(layers)

    qkv_w, qkv_b, pw = g("L0_attn_qkv_w"), g("L0_attn_qkv_b"), g("L0_attn_proj_w")
    wq, wo, bq = (np.zeros(s, np.float32) for s in ((WIN_HEADS, DIM, DIM), (WIN_HEADS, DIM, DIM), (128, WIN_HEADS)))
    for h in range(WIN_HEADS):
        own = slice(WIN_DH * h, WIN_DH * h + WIN_DH)
        wq[h, :, own] = qkv_w[:, own]
        wo[h, own, :] = pw[own, :]
        bq[own, h] = bq[DIM + WIN_DH * h:DIM + WIN_DH * h + WIN_DH, h] = qkv_b[own]
    f["win_w"] = _blocks(np.concatenate([wq, wo, qkv_w[None, :, DIM:2 * DIM], qkv_w[None, :, 2 * DIM:]]))
    at = np.arange(T)[:, None] - np.arange(T)[None, :] + T - 1
    tab = g("L0_attn_rpb_table")[at].transpose(2, 0, 1).reshape(2, HQ, T)
    tabs = np.zeros((128, 2, T), np.float32)
    tabs[:HQ] = tab.transpose(1, 0, 2)
    f["win_v"] = np.concatenate([bq, _rows(qkv_b[DIM:2 * DIM], g("L0_attn_proj_b")),
                                 np.broadcast_to(_twice(qkv_b[2 * DIM:])[None], (128, 128)),
                                 tabs.reshape(128, -1)], 1)

    wq = g("L1_attn_wq").reshape(ROT_HEADS, DIM, DIM).transpose(0, 2, 1)
    wk, wv = g("L1_attn_wkv").reshape(2, DIM, DIM).transpose(0, 2, 1)
    swap = np.arange(DIM) ^ 1
    wo = g("L1_attn_wo").reshape(DIM, ROT_HEADS, DIM).transpose(1, 2, 0)
    f["rot_w"] = _blocks(np.concatenate([wq, wq[:, :, swap], wo, wk[None], wk[None][:, :, swap], wv[None]]))
    f["rot_v"] = np.concatenate([_rows(g("L1_attn_q_norm_w"), g("L1_attn_k_norm_w")), np.zeros((128, 1), np.float32)], 1)

    f["ff_w"] = np.concatenate([_twice(g("L0_ffn_Wi").T), g("L0_ffn_Wo").T, g("L0_ffn_bi")[:, None],
                                _rows(g("L0_ffn_bo")), g("L0_ffn_bs")[:, 0].T,
                                g("L0_ffn_Ws")[:, 0].transpose(2, 0, 1).reshape(128, 256)], 1)
    wr = g("L0_ffn_Wr").reshape(FFN_LAYERS * EXPERTS, 128, 128).transpose(2, 0, 1)
    br = g("L0_ffn_br").reshape(FFN_LAYERS * EXPERTS, 128).T[:, :, None]
    f["ff_r"] = np.concatenate([wr, br], 2)
    f["route"] = g("L0_ffn_route_id").reshape(1, ROUTES)

    wg = np.zeros((128, 2, 8), np.float32)
    wg[:64, 0] = wg[64:, 1] = g("L1_ffn_Wg")
    f["top_w"] = np.concatenate([_twice(g("L1_ffn_W1").transpose(1, 0, 2).reshape(DIM, -1)),
                                 g("L1_ffn_W2").transpose(1, 0, 2).reshape(128, -1), g("L1_ffn_b1").T,
                                 wg.reshape(128, 16), np.broadcast_to(_twice(g("L1_ffn_bg"))[None], (128, 16))], 1)
    b2 = np.zeros((16, 128), np.float32)
    b2[:8, :64] = b2[8:, 64:] = g("L1_ffn_b2")
    f["top_b2"] = b2

    eye = np.eye(128, dtype=np.float32)
    mean = np.zeros((128, 128), np.float32)
    mean[:64, :64] = mean[64:, 64:] = 1.0 / DIM
    freqs = np.float32(10000.0) ** (-2.0 * np.arange(DIM // 2, dtype=np.float32) / DIM).astype(np.float32)
    theta = (np.arange(T, dtype=np.float32)[None] * freqs[:, None]).astype(np.float32)
    cos = _twice(np.repeat(np.cos(theta), 2, axis=0))
    sin = np.repeat(np.sin(theta), 2, axis=0)
    sin[0::2] = -sin[0::2]
    mask = np.zeros((128, T), np.float32)
    mask[:HQ] = np.tile(np.where(np.arange(T)[None] <= np.arange(T)[:, None], 0.0, NEG), (HEADS, 1))
    f["consts"] = np.concatenate([eye, eye - mean, mean, cos, _twice(sin), mask], 1).astype(np.float32)
    return {k: np.ascontiguousarray(a) for k, a in f.items()}


def kernel(**inputs):
    import concourse.bacc as _bacc
    from concourse.bass_utils import run_bass_kernel_spmd as _run

    nc = _bacc.Bacc("TRN2", target_bir_lowering=False, num_devices=1)
    arrays = {f"in_{k}": a for k, a in _laid_out(inputs).items()}
    d = {k[3:]: nc.dram_tensor(k, a.shape, mybir.dt.from_np(a.dtype), kind="ExternalInput").ap()
         for k, a in arrays.items()}
    o = nc.dram_tensor("out_0", (IMAGES, T, DIM), FP32, kind="ExternalOutput").ap()
    o = [o[IMG * m:IMG * m + IMG].rearrange("(s j) t f -> (j t) s f", s=SETS) for m in range(TILES)]
    build(nc, d, o)
    r = _run(nc, [arrays], core_ids=[0])
    return r.results[0]["out_0"]
```

```python
from contextlib import ExitStack

import numpy as np
import concourse.bass as bass
import concourse.mybir as mybir

FP32 = mybir.dt.float32
BF16 = mybir.dt.bfloat16
I32 = mybir.dt.int32
ALU = mybir.AluOpType
ACT = mybir.ActivationFunctionType
AX = mybir.AxisListType

IMAGES, PATCH, GRID, CHANNELS, DIM = 128, 32, 4, 3, 64
PATCHES = GRID * GRID
FEATURES = CHANNELS * PATCH * PATCH
T = PATCHES + 1
LAYERS, HEADS, HIDDEN = 4, 4, 128
PIECES, HALVES = 4, 2
IMG = IMAGES // (PIECES * HALVES)
N = IMG * T
NP = IMG * PATCHES
PAD = 32
SETS = IMG // 4
HQ = HEADS * T
CHUNKS = FEATURES // 128
TILES = PIECES * HALVES
EPS = 1e-5
RMS_EPS = 1.1920929e-07
WIN_HEADS, WIN_DH = 8, 8
ROT_HEADS = 16
ROUTES, FFN_LAYERS, EXPERTS = 64, 2, 16
PAIRS = IMG // 2
SLOTS = 4
PICKER = ["dve", "act"] * (TILES // 2)
ROUTED = [(2 * p + half, l) for p in range(PIECES) for l in range(FFN_LAYERS) for half in range(HALVES)]
TOP_EXPERTS = 8
NEG = -1e30
ARENA = 24600

L_Q, L_K, L_V, L_O, L_W1, L_W2, L_VEC = 0, 256, 384, 640, 768, 896, 960
L_ALL = L_VEC + 7
X_EMBED, X_FINAL, X_WIN, X_FFN, X_ROT, X_TOP = 0, 9, 10, 12, 13, 17
K_EMBED, K_FINAL, K_WIN, K_FFN, K_ROT, K_TILE, K_TOP = 0, 9, 10, 11, 12, 13, 14 + ROT_HEADS
H_WIN, H_FFN, H_ROT, H_TOP = 8, 9, 10, 11
A_WIN, A_ROT = 4, 6
WIN_PASSES, ROT_PASSES = 2, 4


def wave(steps, skew):
    for t in range(steps + skew * (PIECES - 1)):
        for p in range(PIECES):
            if 0 <= t - skew * p < steps:
                yield t - skew * p, p


def build(nc, d, out):
    ctx = ExitStack()
    with ctx:
        def sb(name, shape, dt=FP32):
            return ctx.enter_context(nc.sbuf_tensor(name, shape, dt))

        def sem(name):
            return ctx.enter_context(nc.semaphore(name))

        X = sb("X", [128, PIECES, IMG, T])
        Z = sb("Z", [128, PIECES, IMG, PAD])
        ZN = sb("ZN", [128, PIECES, N])
        SQ = sb("SQ", [128, PIECES, N])
        RS = sb("RS", [128, PIECES, N])
        QO = sb("QO", [128, PIECES, IMG, HEADS, T])
        KB = sb("KB", [128, PIECES, IMG, HALVES, T])
        E = sb("E", [HQ, TILES, IMG, PAD])
        PH = sb("PH", [128, TILES, N])
        VT = sb("VT", [128, PIECES, SETS, 128])
        mx = sb("mx", [HQ, TILES, IMG])
        sm = sb("sm", [HQ, TILES, IMG])
        rc = sb("rc", [HQ, TILES, IMG])
        consts = sb("consts", [128, 3 * 128 + 3 * T])
        ident, cen, avg = (consts[:, 128 * n:128 * n + 128] for n in range(3))
        cos_t, sin_t, causal = (consts[:, 384 + T * n:384 + T * n + T] for n in range(3))
        eps_t = sb("eps_t", [128, 2])
        ones = sb("ones", [128, 128])
        LW = sb("LW", [128, L_ALL])
        lvec = sb("lvec", [128, 7 + 128 + 64])
        AB = sb("AB", [128, 2, HEADS, 128])
        evec = sb("evec", [128, 6 + T])
        arena = sb("arena", [128, ARENA])

        used = [0]

        def part(*shape):
            n = int(np.prod(shape))
            o = used[0]
            used[0] += n
            v = arena[:, o:o + n]
            if len(shape) == 2:
                v = v.rearrange("p (a b) -> p a b", a=shape[0])
            if len(shape) == 3:
                v = v.rearrange("p (a b c) -> p a b c", a=shape[0], b=shape[1])
            return v

        img = [part(CHUNKS, NP) for _ in range(2)]
        sqi = part(CHUNKS, NP)
        WA = part(CHUNKS, 192)
        lnp = part(2, CHUNKS)
        assert used[0] <= ARENA
        used[0] = 0
        winw = part(2 * WIN_HEADS + 2, 128)
        winv = part(WIN_HEADS + 2 + 128 + T * 2)
        rotw = part(3 * ROT_HEADS + 3, 128)
        rotv = part(3)
        ffw = part(128 + 64 + 2 + 2 + 256)
        rw = part(FFN_LAYERS * EXPERTS, 129)
        picked = part(SLOTS * FFN_LAYERS, PAIRS, 129)
        topw = part(TOP_EXPERTS * (64 + 1) + 16 + 16)
        turned_sin = part(PIECES, N)
        assert used[0] <= ARENA
        gate = picked[:, 0].rearrange("p a b -> p (a b)")[:, 0:768].rearrange("p (a b c) -> p a b c", a=3, b=32)
        mk32 = picked[0:16, 1:3].rearrange("p n a b -> p (n a b)")[:, 0:PIECES * N] \
            .rearrange("p (q i t) -> p q i t", q=PIECES, i=IMG)
        route = sb("route", [1, ROUTES], I32)
        selb = sb("selb", [16, 16], BF16)
        b2d = sb("b2d", [16, 128])
        gmax = sb("gmax", [128, 32])
        idx = sb("idx", [128, 8])
        mkb = sb("mkb", [16, PIECES, N], BF16)
        B = [ctx.enter_context(nc.psum_tensor(f"bank{n}", [128, 512], FP32)) for n in range(8)]

        def each(name):
            return [sem(f"{name}{p}") for p in range(PIECES)]

        w_embed, w_const, w_late, w_route = sem("w_embed"), sem("w_const"), sem("w_late"), sem("w_route")
        w_layer, layer_used = sem("w_layer"), sem("layer_used")
        img_in = [[sem(f"img_in{n}{half}") for half in range(2)] for n in range(2)]
        raw_kept, scaled, colsum, mean_w, wa_ready = (sem("raw_kept"), sem("scaled"), sem("colsum"), sem("mean_w"),
                                                      sem("wa_ready"))
        shift_psum, shift_ready = sem("shift_psum"), sem("shift_ready")
        img_sq, img_sum, embed_psum, sq_psum = sem("img_sq"), sem("img_sum"), sem("embed_psum"), sem("sq_psum")
        mean_sq, e_var, e_rstd, embedded = (sem("mean_sq"), sem("e_var"), sem("e_rstd"),
                                                   sem("embedded"))
        x_ready, centered, squared, var_psum = each("x_ready"), each("centered"), each("squared"), each("var_psum")
        rstd_ready, normed, h_ready = each("rstd_ready"), each("normed"), each("h_ready")
        gained = sem("gained")
        ab_psum, ab_ready, fvec_ready, avec_ready = sem("ab_psum"), sem("ab_ready"), sem("fvec_ready"), sem("avec_ready")
        q_psum, q_ready, v_psum, v_ready = each("q_psum"), each("q_ready"), each("v_psum"), each("v_ready")
        k_psum, k_ready, keys_ready = sem("k_psum"), sem("k_ready"), each("keys_ready")
        s_psum, s_biased, maxed, s_ready, expd = (each("s_psum"), sem("s_biased"), sem("maxed"), each("s_ready"),
                                                  each("expd"))
        summed, inv_ready, probs_ready = sem("summed"), each("inv_ready"), each("probs_ready")
        pt_psum, pt_ready, pv_psum, o_ready, y_psum = (each("pt_psum"), each("pt_ready"), each("pv_psum"),
                                                       each("o_ready"), each("y_psum"))
        hid_psum, hid_ready, down_psum = sem("hid_psum"), sem("hid_ready"), sem("down_psum")
        g_psum, g_biased, g_ready = sem("g_psum"), sem("g_biased"), sem("g_ready")
        rw_ready = sem("rw_ready")
        picked_by = {who: sem(f"picked_by_{who}") for who in ("dve", "act")}
        r_turned, r_sum, r_done = each("r_turned"), sem("r_sum"), each("r_done")
        wqk_ready = sem("wqk_ready")
        gate_psum, gate_step, mask_ready, mt_psum, mt_ready = (sem("gate_psum"), sem("gate_step"), sem("mask_ready"),
                                                               sem("mt_psum"), sem("mt_ready"))
        sel_ready, eh_psum, eh_ready, em_ready, top_psum = (sem("sel_ready"), sem("eh_psum"), sem("eh_ready"),
                                                            sem("em_ready"), sem("top_psum"))
        out_psum, out_ready, out_sent = sem("out_psum"), sem("out_ready"), sem("out_sent")
        idx_ready, pool_turn = sem("idx_ready"), sem("pool_turn")

        def rows(half):
            return slice(64 * half, 64 * half + 64)

        def zv(p):
            return Z[:, p, :, 0:T]

        def zn(p, t=T):
            return ZN[:, p, 0:IMG * t].rearrange("p (i t) -> p i t", t=t)

        def tiled(ap):
            return ap.rearrange("p (i t) -> p i t", t=T)

        def bank(p, n):
            return B[2 * p + n]

        def x_of(p):
            return X[:, p, :, :].rearrange("p i t -> p (i t)")

        def patches_of(p):
            return QO[:, p].rearrange("p i h t -> p (i h t)")[:, 0:NP]

        def maps(m, l):
            return picked[:, FFN_LAYERS * (m % SLOTS) + l]

        def pairs_of(who):
            return [(m, w) for m in range(TILES) if PICKER[m] == who for w in range(PAIRS)]

        def load_expert(engine, experts, m, w):
            experts[m, w] = engine.value_load(route[0:1, PAIRS * m + w:PAIRS * m + w + 1], min_val=0,
                                              max_val=EXPERTS - 1)

        def pick_pair(who, copy, experts, m, w):
            for l in range(FFN_LAYERS):
                last = copy(maps(m, l)[:, w, :],
                            rw[:, bass.ds(experts[m, w] + EXPERTS * l, 1), :].rearrange("p a c -> p (a c)"))
            if w == PAIRS - 1:
                last.then_inc(picked_by[who], 1)

        def pick(who, engine, copy, experts, m):
            engine.wait_ge(g_biased, ROUTED.index((m - SLOTS, FFN_LAYERS - 1)) + 1)
            for w in range(PAIRS):
                pick_pair(who, copy, experts, m, w)

        def wait_picked(engine, m):
            engine.wait_ge(picked_by[PICKER[m]], PICKER[:m + 1].count(PICKER[m]))


        def pe_centre(pe, p, k, src, width, ready):
            pe.wait_ge(*ready)
            nc.tensor.matmul(bank(p, 0)[:, 0:width], cen, src, start=True, stop=True).then_inc(centered[p], 1)

        def pe_variance(pe, p, k, width):
            pe.wait_ge(squared[p], k + 1)
            nc.tensor.matmul(bank(p, 1)[:, 0:width], avg, SQ[:, p, 0:width], start=True,
                             stop=True).then_inc(var_psum[p], 1)

        def act_square(act, p, k, width):
            act.wait_ge(centered[p], k + 1)
            nc.scalar.activation(SQ[:, p, 0:width], bank(p, 0)[:, 0:width], ACT.Square).then_inc(squared[p], 1)

        def act_rstd(act, p, k, width, eps=0):
            act.wait_ge(var_psum[p], k + 1)
            nc.scalar.activation(RS[:, p, 0:width], bank(p, 1)[:, 0:width], ACT.Ln,
                                 bias=eps_t[:, eps:eps + 1]).then_inc(rstd_ready[p], 1)
            act.wait_ge(rstd_ready[p], 2 * k + 1)
            nc.scalar.activation(RS[:, p, 0:width], RS[:, p, 0:width], ACT.Exp, scale=-0.5).then_inc(rstd_ready[p], 1)

        def dve_norm(dve, p, k, width, dst, done):
            dve.wait_ge(rstd_ready[p], 2 * k + 2)
            nc.vector.tensor_tensor(dst, bank(p, 0)[:, 0:width].rearrange("p (i t) -> p i t", i=IMG),
                                    RS[:, p, 0:width].rearrange("p (i t) -> p i t", i=IMG), ALU.mult).then_inc(done, 1)

        def pool_affine(pool, p, k, dst, gain, shift, done):
            pool.wait_ge(normed[p], k + 1)
            if not isinstance(k, int):
                pool.sem_inc(pool_turn, 1)
            nc.gpsimd.tensor_scalar(dst, zn(p), gain, shift, ALU.mult, ALU.add).then_inc(done, 1)

        def pe_query(pe, p, a, h, weight):
            if h >= 2:
                pe.wait_ge(q_ready[p], HEADS * a + h - 1)
            nc.tensor.matmul(bank(p, h % 2)[:, 0:N], weight, zv(p), start=True, stop=True).then_inc(q_psum[p], 1)

        def act_query(act, p, a, h, bias=None):
            act.wait_ge(q_psum[p], HEADS * a + h + 1)
            src = tiled(bank(p, h % 2)[:, 0:N])
            if bias is None:
                nc.scalar.copy(QO[:, p, :, h, :], src).then_inc(q_ready[p], 1)
            else:
                nc.scalar.activation(QO[:, p, :, h, :], src, ACT.Identity, bias=bias).then_inc(q_ready[p], 1)

        def pe_values(pe, p, weight):
            for s in range(SETS):
                src = Z[:, p, 4 * s:4 * s + 4, :].rearrange("p i t -> p (i t)")
                o = bank(p, 0)[:, 128 * s:128 * s + 128]
                if weight is None:
                    last = nc.tensor.transpose(o, src, ident)
                else:
                    last = nc.tensor.matmul(o, src, weight, start=True, stop=True)
            last.then_inc(v_psum[p], 1)

        def act_values(act, p, v):
            act.wait_ge(v_psum[p], v + 1)
            nc.scalar.copy(VT[:, p, :, :], bank(p, 0)[:, :].rearrange("p (s f) -> p s f", s=SETS)).then_inc(v_ready[p], 1)

        def pe_scores(pe, p, u):
            for i in range(IMG // 2):
                o = bank(p, 1 - u)[0:HQ, 0:N].rearrange("p (k i t) -> p k i t", k=HALVES, t=T)[:, :, i, :]
                last = nc.tensor.matmul(o, QO[:, p, IMG // 2 * u + i, :, :].rearrange("p h t -> p (h t)"),
                                        KB[:, p, IMG // 2 * u + i], start=True, stop=True)
            last.then_inc(s_psum[p], 1)

        def probs(p, half):
            return E[:, 2 * p + half, :, 0:T]

        def per_row(stat, p, half):
            return stat[:, 2 * p + half, :].unsqueeze(2).to_broadcast([HQ, IMG, T])

        def nth():
            seen = [0]

            def following():
                seen[0] += 1
                return seen[0]
            return following

        def dve_centre(dve, p, a, half, rank, table=None, scale=1.0):
            dve.wait_ge(s_psum[p], 2 * a + half + 1)
            src = tiled(bank(p, 1 - half)[0:HQ, 0:N])
            if table is not None:
                nc.vector.scalar_tensor_tensor(probs(p, half), src, scale,
                                               table.unsqueeze(1).to_broadcast([HQ, IMG, T]), ALU.mult,
                                               ALU.add).then_inc(s_biased, 1)
                dve.wait_ge(s_biased, rank["biased"]())
                src = probs(p, half)
            nc.vector.tensor_reduce(mx[:, 2 * p + half, :], src, AX.X, ALU.max).then_inc(maxed, 1)
            dve.wait_ge(maxed, rank["first"] + rank["max"]())
            nc.vector.tensor_tensor(probs(p, half), src, per_row(mx, p, half), ALU.subtract).then_inc(s_ready[p], 1)

        def act_exp(act, p, a, half, scale=1.0):
            act.wait_ge(s_ready[p], 2 * a + half + 1)
            nc.scalar.activation(probs(p, half), probs(p, half), ACT.Exp, scale=scale).then_inc(expd[p], 1)

        def dve_total(dve, p, a, half, rank):
            dve.wait_ge(expd[p], 2 * a + half + 1)
            nc.vector.tensor_reduce(sm[:, 2 * p + half, :], probs(p, half), AX.X, ALU.add).then_inc(summed, 1)
            dve.wait_ge(summed, rank["first"] + rank["sum"]())
            nc.vector.reciprocal(rc[:, 2 * p + half, :], sm[:, 2 * p + half, :]).then_inc(inv_ready[p], 1)

        def pool_probs(pool, p, a, half):
            pool.wait_ge(inv_ready[p], 2 * a + half + 1)
            nc.gpsimd.tensor_tensor(probs(p, half), probs(p, half), per_row(rc, p, half),
                                    ALU.mult).then_inc(probs_ready[p], 1)

        def pe_turn_probs(pe, p, a, half):
            pe.wait_ge(probs_ready[p], 2 * a + half + 1)
            for s in range(SETS):
                last = nc.tensor.transpose(bank(p, 1 - half)[:, HQ * s:HQ * s + HQ],
                                           E[:, 2 * p + half, 4 * s:4 * s + 4, :].rearrange("p i t -> p (i t)"),
                                           ident[0:HQ, 0:HQ])
            last.then_inc(pt_psum[p], 1)

        def act_turned(act, p, a, half):
            act.wait_ge(pt_psum[p], 2 * a + half + 1)
            nc.scalar.copy(PH[:, 2 * p + half, :], bank(p, 1 - half)[:, 0:N]).then_inc(pt_ready[p], 1)

        def pe_mix(pe, p, a, j):
            if j == 0:
                pe.wait_ge(pt_ready[p], 2 * a + 2)
            if j >= 2:
                pe.wait_ge(o_ready[p], 4 * a + j - 1)
            for s in range(SETS):
                for half in range(HALVES):
                    at = HQ * (2 * half + s % 2)
                    last = nc.tensor.matmul(bank(p, j % 2)[rows(half), HQ * s:HQ * s + HQ],
                                            VT[32 * j:32 * j + T, p, s, rows(half)],
                                            PH[32 * j:32 * j + T, 2 * p + s // 2, at:at + HQ],
                                            start=True, stop=True)
            last.then_inc(pv_psum[p], 1)

        def act_mixed(act, p, a, j):
            act.wait_ge(pv_psum[p], 4 * a + j + 1)
            nc.scalar.copy(QO[:, p, j:IMG:4, :, :].rearrange("p s h t -> p s (h t)"),
                           bank(p, j % 2)[:, 0:N].rearrange("p (s c) -> p s c", s=SETS)).then_inc(o_ready[p], 1)

        def pe_project(pe, p, a, weight):
            pe.wait_ge(o_ready[p], 4 * a + 4)
            for h in range(HEADS):
                last = nc.tensor.matmul(bank(p, 0)[:, 0:N], weight(h), QO[:, p, :, h, :], start=h == 0,
                                        stop=h == HEADS - 1)
            last.then_inc(y_psum[p], 1)

        def dve_add(dve, p, produced, count, src, bias):
            dve.wait_ge(produced, count)
            if bias is None:
                nc.vector.tensor_tensor(X[:, p], tiled(src[:, 0:N]), X[:, p], ALU.add).then_inc(x_ready[p], 1)
            else:
                nc.vector.scalar_tensor_tensor(X[:, p], tiled(src[:, 0:N]), bias, X[:, p], ALU.add,
                                               ALU.add).then_inc(x_ready[p], 1)

        S0, S1, SM, PT, M0, M1, PR = range(7)
        PASS = 7

        def pe_pass(pe, p, a, step, weight):
            if step in (S0, S1):
                pe_scores(pe, p, step - S0)
            elif step == PT:
                for half in range(HALVES):
                    pe_turn_probs(pe, p, a, half)
            elif step in (M0, M1):
                for j in (2 * (step - M0), 2 * (step - M0) + 1):
                    pe_mix(pe, p, a, j)
            elif step == PR:
                pe_project(pe, p, a, weight)

        def act_pass(act, p, a, step, scale=1.0):
            if step in (S1, SM):
                act_exp(act, p, a, step - S1, scale)
            elif step == PT:
                for half in range(HALVES):
                    act_turned(act, p, a, half)
            elif step in (M0, M1):
                for j in (2 * (step - M0), 2 * (step - M0) + 1):
                    act_mixed(act, p, a, j)

        def dve_pass(dve, p, a, step, bias, rank, **table):
            if step in (S0, S1):
                dve_centre(dve, p, a, step - S0, rank, **table)
            if step in (S1, SM):
                dve_total(dve, p, a, step - S1, rank)
            elif step == PR:
                dve_add(dve, p, y_psum[p], a + 1, bank(p, 0), bias)

        def pool_pass(pool, p, a, step):
            if step in (S1, SM):
                pool_probs(pool, p, a, step - S1)

        vec = {name: lvec[:, n:n + 1] for n, name in enumerate(["ga", "ba", "bo", "gf", "bf", "b2", "b1"])}
        lw1, lw2 = lvec[:, 7:135], lvec[:, 135:199]
        egain, eshift, fgain, fshift = (evec[:, n:n + 1] for n in range(4))
        epatch_bias, ecls = evec[:, 4:5], evec[:, 5:6]
        epos = evec[:, 6:6 + T]
        wq_w, wk_w = (lambda h: winw[:, h, :]), winw[:, 2 * WIN_HEADS, :]
        wv_w, wo_w = winw[:, 2 * WIN_HEADS + 1, :], (lambda h: winw[:, WIN_HEADS + h, :])
        wbq, wbk, wbo = (lambda h: winv[:, h:h + 1]), winv[:, WIN_HEADS:WIN_HEADS + 1], \
            winv[:, WIN_HEADS + 1:WIN_HEADS + 2]
        wbv = winv[:, WIN_HEADS + 2:WIN_HEADS + 130]
        wtab = [winv[0:HQ, WIN_HEADS + 130 + T * g:WIN_HEADS + 130 + T * g + T] for g in range(2)]
        f_wi, f_wo = ffw[:, 0:128], ffw[:, 128:192]
        f_bi, f_bo, f_bs = ffw[:, 192:193], ffw[:, 193:194], ffw[:, 194:196]
        f_ws = ffw[:, 196:452].rearrange("p (l f) -> p l f", l=2)
        t_w1 = winw[:, 0:16, :]
        t_w2 = topw[:, 0:512].rearrange("p (e f) -> p e f", e=8)
        t_b1, t_wg, t_bg = topw[:, 512:520], topw[:, 520:536], topw[:, 536:552]
        EMBED_BANK = [B[0], B[1], B[6], B[7]]
        raw_w = PH[:, :, :].rearrange("p m n -> p (m n)")[:, 0:CHUNKS * DIM].rearrange("p (c f) -> p c f", c=CHUNKS)

        LAYER_STEPS = 2 + 3 + PASS + 2
        LAYER_SKEW = 2
        REST = [(kind, n) for kind, steps in (("final", 2), ("win", 5), ("win pass 0", PASS), ("win queries", 2),
                                              ("win pass 1", PASS), ("ffn", 6), ("rot", 5)) for n in range(steps)]
        REST += [step for g in range(ROT_PASSES) for step in [(f"heads {g}", n) for n in range(2 * HEADS)]
                 + [(f"rot pass {g}", n) for n in range(PASS)]]
        REST_SKEW = 4

        block = ctx.enter_context(nc.Block())

        @block.sync
        def _(sp):
            def load_image(q):
                if q >= 2:
                    sp.wait_ge(embed_psum, q - 1)
                    sp.wait_ge(img_sq, 2 * (q - 1))
                for n in range(2):
                    c = slice(n * CHUNKS // 2, (n + 1) * CHUNKS // 2)
                    sp.dma_start(img[q % 2][:, c, :], d["img"][q][:, c, :]).then_inc(img_in[q % 2][n], 16)

            sp.dma_start(WA[:, :, 64:128], d["w_patch"]).then_inc(w_embed, 16)
            sp.dma_start(lnp, d["ln_p1"]).then_inc(w_embed, 16)
            sp.dma_start(evec[:, :], d["evec"]).then_inc(w_embed, 16)
            sp.dma_start(route[:, :], d["route"]).then_inc(w_route, 16)
            sp.dma_start(b2d[:, :], d["top_b2"]).then_inc(w_route, 16)
            load_image(0)
            sp.dma_start(consts[:, :], d["consts"]).then_inc(w_const, 16)
            load_image(1)
            sp.dma_start(LW[:, :], d["layers"][0]).then_inc(w_layer, 16)
            for q in range(2, TILES):
                load_image(q)
            sp.wait_ge(embedded, 2 * TILES)
            sp.wait_ge(shift_psum, 1)
            for dst, name in ((winw, "win_w"), (winv, "win_v"), (rotw, "rot_w"), (rotv, "rot_v"), (ffw, "ff_w"),
                              (rw, "ff_r"), (topw, "top_w")):
                sp.dma_start(dst, d[name]).then_inc(w_late, 16)
            with sp.Fori(1, LAYERS) as i:
                sp.wait_ge(layer_used, 2 * i)
                sp.dma_start(LW[:, :], d["layers"][bass.ds(i, 1)].rearrange("a p n -> (a p) n")).then_inc(w_layer, 16)
            for p in range(PIECES):
                sp.wait_ge(y_psum[p], A_WIN + WIN_PASSES)
            sp.dma_start(t_w1, d["top_w1"]).then_inc(w_late, 16)
            for p in range(PIECES):
                sp.wait_ge(out_ready, p + 1)
                for half in range(HALVES):
                    sp.dma_start(out[HALVES * p + half], QO[0:HQ, p].rearrange("p i h t -> p (i h t)")[:, 0:512]
                                 .rearrange("p (s h f) -> p s h f", s=SETS, h=2)[:, :, half, :]).then_inc(out_sent, 16)
            sp.wait_ge(out_sent, 16 * TILES)

        @block.tensor
        def _(pe):
            def embed_rows(q):
                half = q % 2
                if q >= 4:
                    pe.wait_ge(embedded, 2 * (q - 3))
                lo = 64 if half == 0 else 0
                for c in range(CHUNKS):
                    if c % (CHUNKS // 2) == 0:
                        pe.wait_ge(img_in[q % 2][1 if c else 0], 16 * (q // 2) + 16)
                    last = nc.tensor.matmul(EMBED_BANK[q % 4][:, 0:NP], WA[:, c, lo:lo + 128], img[q % 2][:, c, :],
                                            start=c == 0, stop=c == CHUNKS - 1)
                last.then_inc(embed_psum, 1)

            def embed_squares(q):
                if q >= 2:
                    pe.wait_ge(e_var, q - 1)
                for part_ in range(2):
                    pe.wait_ge(img_sum, 2 * q + part_ + 1)
                    last = nc.tensor.matmul(B[2 + q % 2][:, 0:NP], ones[:, :], SQ[:, 2 * (q % 2) + part_, 0:NP],
                                            start=part_ == 0, stop=part_ == 1)
                last.then_inc(sq_psum, 1)

            pe.wait_ge(raw_kept, 1)
            for c in range(CHUNKS):
                last = nc.tensor.matmul(B[4][:, 0:64], lnp[:, 0, c:c + 1].to_broadcast([128, 128]), raw_w[:, c, :],
                                        start=c == 0, stop=c == CHUNKS - 1)
            last.then_inc(colsum, 1)
            pe.wait_ge(wa_ready, 1)
            for q in range(TILES):
                embed_rows(q)
                if q == 0:
                    for half in range(HALVES):
                        for c in range(CHUNKS):
                            last = nc.tensor.matmul(B[4 + half][rows(half), 0:1], raw_w[:, c, :], lnp[:, 1, c:c + 1],
                                                    start=c == 0, stop=c == CHUNKS - 1)
                    last.then_inc(shift_psum, 1)
                if q >= 1:
                    embed_squares(q - 1)
            embed_squares(TILES - 1)
            pe.wait_ge(w_const, 16)
            pe.wait_ge(shift_ready, 1)
            for p in range(PIECES):
                pe_centre(pe, p, K_EMBED, patches_of(p), NP, (embedded, 2 * TILES))
            for p in range(PIECES):
                pe_variance(pe, p, K_EMBED, NP)

            with pe.Fori(0, LAYERS) as i:
                pe.wait_ge(w_layer, 16 * i + 16)
                pe.wait_ge(rstd_ready[0], 4 * i + 1)
                pe.wait_ge(rstd_ready[1], 4 * i + 1)
                for h in range(HEADS):
                    r = rows(h % 2)
                    hp = h // 2
                    o = B[1 + 2 * (h % 2)]
                    nc.tensor.matmul(o[:, 128 * hp:128 * hp + 64], LW[r, L_Q + 128 * hp:L_Q + 128 * hp + 128],
                                     LW[r, L_K + 64 * hp:L_K + 64 * hp + 64], start=True, stop=True)
                    last = nc.tensor.matmul(o[:, 128 * hp + 64:128 * hp + 128],
                                            LW[r, L_V + 128 * hp:L_V + 128 * hp + 128],
                                            LW[r, L_O + 64 * hp:L_O + 64 * hp + 64], start=True, stop=True)
                last.then_inc(ab_psum, 1)
                for step, p in wave(LAYER_STEPS, LAYER_SKEW):
                    if step == 0:
                        pe_centre(pe, p, 1 + 2 * i, x_of(p), N, (x_ready[p], 2 * i + 1))
                    elif step == 1:
                        if p == 0:
                            pe.wait_ge(ab_ready, 8 * i + 8)
                        pe_variance(pe, p, 1 + 2 * i, N)
                    elif step in (2, 3):
                        if step == 2:
                            pe.wait_ge(h_ready[p], 2 * i + 1)
                        for h in (2 * step - 4, 2 * step - 3):
                            pe_query(pe, p, i, h, AB[:, 0, h, :])
                    elif step == 4:
                        pe.wait_ge(q_ready[p], 4 * i + 4)
                        pe_values(pe, p, None)
                    elif step < 5 + PASS:
                        if step == 5 + S0:
                            pe.wait_ge(keys_ready[p], i + 1)
                        if step == 5 + S1:
                            pe.wait_ge(v_ready[p], i + 1)
                        pe_pass(pe, p, i, step - 5, lambda h: AB[:, 1, h, :])
                    elif step == 5 + PASS:
                        pe_centre(pe, p, 2 + 2 * i, x_of(p), N, (x_ready[p], 2 * i + 2))
                    else:
                        pe_variance(pe, p, 2 + 2 * i, N)
                pe.wait_ge(fvec_ready, i + 1)
                for p in range(PIECES):
                    pe.wait_ge(h_ready[p], 2 * i + 2)
                    for half in range(HALVES):
                        nc.tensor.matmul(bank(p, half)[:, 0:N], lw1[rows(half), :], zv(p)[rows(half)], start=True,
                                         stop=True).then_inc(hid_psum, 1)
                for p in range(PIECES):
                    pe.wait_ge(hid_ready, TILES * i + 2 * p + 2)
                    for half in range(HALVES):
                        last = nc.tensor.matmul(bank(p, 0)[rows(half), 0:N], lw2, PH[:, 2 * p + half, :], start=True,
                                                stop=True)
                    last.then_inc(down_psum, 1)

            def turned(p, r, w, w_swapped):
                if r >= 1:
                    pe.wait_ge(rstd_ready[p], 2 * (K_TILE + r) - 1)
                nc.tensor.matmul(bank(p, 0)[:, 0:N], w, zv(p), start=True, stop=True)
                nc.tensor.matmul(bank(p, 1)[:, 0:N], w_swapped, zv(p), start=True, stop=True).then_inc(centered[p], 1)

            def lengths(p, r):
                pe.wait_ge(squared[p], K_TILE + r + 1)
                pe.wait_ge(r_turned[p], 2 * r + 1)
                nc.tensor.matmul(bank(p, 1)[:, 0:N], avg, SQ[:, p, :], start=True, stop=True).then_inc(var_psum[p], 1)

            pe.wait_ge(w_late, 16 * 7)
            for step, p in wave(len(REST), REST_SKEW):
                kind, n = REST[step]
                g = int(kind[-1]) if kind[-1].isdigit() else 0
                if kind == "final":
                    if n == 0:
                        pe_centre(pe, p, K_FINAL, x_of(p), N, (x_ready[p], X_FINAL))
                    else:
                        pe_variance(pe, p, K_FINAL, N)
                elif kind == "win":
                    if n == 0:
                        pe_centre(pe, p, K_WIN, x_of(p), N, (x_ready[p], X_FINAL + 1))
                    elif n == 1:
                        pe_variance(pe, p, K_WIN, N)
                    elif n == 2:
                        pe.wait_ge(h_ready[p], H_WIN + 1)
                        nc.tensor.matmul(bank(p, 1)[:, 0:N], wk_w, zv(p), start=True, stop=True).then_inc(k_psum, 1)
                        pe_query(pe, p, A_WIN, 0, wq_w(0))
                        pe.wait_ge(k_ready, p + 1)
                        pe_query(pe, p, A_WIN, 1, wq_w(1))
                    elif n == 3:
                        for h in (2, 3):
                            pe_query(pe, p, A_WIN, h, wq_w(h))
                    else:
                        pe.wait_ge(q_ready[p], HEADS * A_WIN + HEADS)
                        pe_values(pe, p, wv_w)
                elif kind == "win queries":
                    if n == 0:
                        pe.wait_ge(x_ready[p], X_WIN + 1)
                    for h in (2 * n, 2 * n + 1):
                        pe_query(pe, p, A_WIN + 1, h, wq_w(HEADS + h))
                elif kind.startswith("win pass"):
                    if n == S1 and g == 0:
                        pe.wait_ge(v_ready[p], LAYERS + 1)
                    if n == S0 and g == 1:
                        pe.wait_ge(q_ready[p], HEADS * (A_WIN + 1) + HEADS)
                    pe_pass(pe, p, A_WIN + g, n, lambda h: wo_w(HEADS * g + h))
                elif kind == "ffn":
                    if n == 0:
                        pe_centre(pe, p, K_FFN, x_of(p), N, (x_ready[p], X_WIN + 2))
                    elif n == 1:
                        pe_variance(pe, p, K_FFN, N)
                    elif n == 2:
                        pe.wait_ge(h_ready[p], H_FFN + 1)
                        for half in range(HALVES):
                            nc.tensor.matmul(bank(p, half)[:, 0:N], f_wi[rows(half), :], zv(p)[rows(half)],
                                             start=True, stop=True).then_inc(hid_psum, 1)
                    elif n in (3, 4):
                        for m in (2 * p, 2 * p + 1):
                            if n == 3:
                                pe.wait_ge(hid_ready, TILES * LAYERS + m + 1)
                                wait_picked(pe, m)
                            else:
                                pe.wait_ge(g_ready, ROUTED.index((m, 0)) + 1)
                            for w in range(PAIRS):
                                last = nc.tensor.matmul(bank(p, m % 2)[:, 2 * T * w:2 * T * w + 2 * T],
                                                        maps(m, n - 3)[:, w, 0:128],
                                                        PH[:, m, 2 * T * w:2 * T * w + 2 * T], start=True, stop=True)
                            last.then_inc(g_psum, 1)
                    else:
                        pe.wait_ge(g_ready, ROUTED.index((2 * p + 1, FFN_LAYERS - 1)) + 1)
                        for half in range(HALVES):
                            last = nc.tensor.matmul(bank(p, 0)[rows(half), 0:N], f_wo, PH[:, 2 * p + half, :],
                                                    start=True, stop=True)
                        last.then_inc(down_psum, 1)
                elif kind == "rot":
                    if n == 0:
                        pe_centre(pe, p, K_ROT, x_of(p), N, (x_ready[p], X_FFN + 1))
                    elif n == 1:
                        pe_variance(pe, p, K_ROT, N)
                    elif n == 2:
                        pe.wait_ge(h_ready[p], H_ROT + 1)
                        turned(p, 0, rotw[:, 3 * ROT_HEADS, :], rotw[:, 3 * ROT_HEADS + 1, :])
                    elif n == 3:
                        lengths(p, 0)
                    else:
                        pe.wait_ge(r_turned[p], 2)
                        pe_values(pe, p, rotw[:, 3 * ROT_HEADS + 2, :])
                elif kind.startswith("heads"):
                    h, r = n // 2, 1 + HEADS * g + n // 2
                    hh = HEADS * g + h
                    if n % 2:
                        lengths(p, r)
                    else:
                        if h:
                            pe.wait_ge(r_turned[p], 2 * r)
                        elif g:
                            pe.wait_ge(x_ready[p], X_ROT + g)
                        else:
                            pe.wait_ge(v_ready[p], LAYERS + 2)
                        turned(p, r, rotw[:, hh, :], rotw[:, ROT_HEADS + hh, :])
                else:
                    if n == S0:
                        pe.wait_ge(r_done[p], 1 + HEADS * g + HEADS)
                        pe.wait_ge(keys_ready[p], LAYERS + 1)
                    pe_pass(pe, p, A_ROT + g, n, lambda h: rotw[:, 2 * ROT_HEADS + HEADS * g + h, :])

            for p in range(PIECES):
                pe_centre(pe, p, K_TOP, x_of(p), N, (x_ready[p], X_TOP))
            for p in range(PIECES):
                pe_variance(pe, p, K_TOP, N)
            for p in range(PIECES):
                pe.wait_ge(h_ready[p], H_TOP + 1)
            for p in range(PIECES):
                for s in range(SETS):
                    n = SETS * p + s
                    last = nc.tensor.matmul(B[6][:, 16 * n:16 * n + 16],
                                            Z[:, p, 4 * s:4 * s + 4, :].rearrange("p i t -> p (i t)"), t_wg,
                                            start=True, stop=True)
            last.then_inc(gate_psum, 1)
            pe.wait_ge(mask_ready, 1)
            for p in range(PIECES):
                for s in range(SETS):
                    n = SETS * p + s
                    last = nc.tensor.transpose(B[4 + p][0:16, 128 * s:128 * s + 128],
                                               gate[:, 2, 2 * n:2 * n + 2, :].rearrange("p a e -> p (a e)"), ident)
                last.then_inc(mt_psum, 1)
            pe.wait_ge(mt_ready, 2 * PIECES)
            pe.wait_ge(w_late, 16 * 8)
            pe.wait_ge(sel_ready, 1)
            pe.wait_ge(w_route, 32)
            for p in range(PIECES):
                nc.tensor.matmul(B[p][:, 0:N], b2d[:, :], mk32[:, p], start=True, stop=False, skip_group_check=True)

            def expert_up(n):
                e, m = n // TILES, n % TILES
                p, half = m // 2, m % 2
                if n >= 2:
                    pe.wait_ge(em_ready, n - 1)
                nc.tensor.matmul(B[4 + n % 2][:, 0:N], t_w1[:, 2 * e + half, :], zv(p), start=True, stop=True)
                nc.tensor.matmul(B[6 + n % 2][:, 0:N], selb[:, 8 * half + e:8 * half + e + 1].to_broadcast([16, 128]),
                                 mkb[:, p, :], start=True, stop=True).then_inc(eh_psum, 1)

            def expert_down(n):
                e, m = n // TILES, n % TILES
                p, half = m // 2, m % 2
                pe.wait_ge(em_ready, n + 1)
                nc.tensor.matmul(B[p][rows(half), 0:N], t_w2[:, e, :], PH[:, m, :], start=False,
                                 stop=e == TOP_EXPERTS - 1, skip_group_check=True).then_inc(top_psum, 1)

            for n in range(TOP_EXPERTS * TILES):
                expert_up(n)
                if n >= 2:
                    expert_down(n - 2)
            expert_down(TOP_EXPERTS * TILES - 2)
            expert_down(TOP_EXPERTS * TILES - 1)

            for p in range(PIECES):
                pe.wait_ge(x_ready[p], X_TOP + 1)
                for s in range(SETS):
                    last = nc.tensor.transpose(B[p][0:HQ, 128 * s:128 * s + 128],
                                               X[:, p, 4 * s:4 * s + 4, :].rearrange("p i t -> p (i t)"), ident)
                last.then_inc(out_psum, 1)

        @block.scalar
        def _(act):
            nc.scalar.preload_act_table_set("natural_log_exp_and_others")
            def embed_rstd(q):
                half = q % 2
                act.wait_ge(embed_psum, q + 1)
                if q >= 1:
                    act.wait_ge(e_var, q)
                nc.scalar.activation(RS[rows(half), 1, 0:NP], EMBED_BANK[q % 4][rows(1 - half), 0:NP], ACT.Square,
                                     scale=1.0 / FEATURES).then_inc(mean_sq, 1)
                act.wait_ge(e_var, q + 1)
                nc.scalar.activation(RS[rows(half), 0, 0:NP], RS[rows(half), 0, 0:NP], ACT.Ln,
                                     bias=eps_t[rows(half), 0:1]).then_inc(e_rstd, 1)
                act.wait_ge(e_rstd, 2 * q + 1)
                nc.scalar.activation(RS[rows(half), 0, 0:NP], RS[rows(half), 0, 0:NP], ACT.Exp,
                                     scale=-0.5).then_inc(e_rstd, 1)

            experts, pairs = {}, pairs_of("act")
            for q in range(TILES):
                for part_ in range(2):
                    act.wait_ge(img_in[q % 2][part_], 16 * (q // 2) + 16)
                    if q >= 1:
                        act.wait_ge(img_sum, 2 * q - 1 + part_)
                    c = slice(12 * part_, 12 * part_ + 12)
                    nc.scalar.activation(sqi[:, c, :], img[q % 2][:, c, :], ACT.Square).then_inc(img_sq, 1)
                if q == 0:
                    act.wait_ge(w_embed, 48)
                    act.wait_ge(shift_psum, 1)
                    for h in range(HALVES):
                        last = nc.scalar.activation(ZN[rows(h), 0, 0:1], B[4 + h][rows(h), 0:1], ACT.Identity,
                                                    bias=epatch_bias[rows(h)])
                    last.then_inc(shift_ready, 1)
                    act.wait_ge(w_route, 32)
                for m, w in pairs[4 * q:4 * q + 4]:
                    load_expert(act, experts, m, w)
                if q >= 1:
                    embed_rstd(q - 1)
            embed_rstd(TILES - 1)
            for p in range(PIECES):
                act_square(act, p, K_EMBED, NP)
            for p in range(PIECES):
                act_rstd(act, p, K_EMBED, NP)

            act.wait_ge(idx_ready, 1)
            with act.Fori(0, LAYERS) as i:
                act.wait_ge(ab_psum, i + 1)
                for kind in range(2):
                    for h in range(HEADS):
                        src = B[1 + 2 * (h % 2)][:, 128 * (h // 2) + 64 * kind:128 * (h // 2) + 64 * kind + 64]
                        nc.scalar.copy(AB[0:64, kind, h, 0:64], src[0:64])
                        nc.scalar.copy(AB[64:128, kind, h, 64:128], src[64:128]).then_inc(ab_ready, 1)
                act.wait_ge(ab_ready, 8 * i + 8)
                act.sem_inc(layer_used, 1)
                for step, p in wave(LAYER_STEPS, LAYER_SKEW):
                    if step == 0:
                        act_square(act, p, 1 + 2 * i, N)
                    elif step == 1:
                        act_rstd(act, p, 1 + 2 * i, N)
                    elif step in (2, 3):
                        for h in (2 * step - 4, 2 * step - 3):
                            act_query(act, p, i, h)
                    elif step == 4:
                        act_values(act, p, i)
                    elif step < 5 + PASS:
                        act_pass(act, p, i, step - 5, DIM ** -0.5)
                    elif step == 5 + PASS:
                        act_square(act, p, 2 + 2 * i, N)
                    else:
                        act_rstd(act, p, 2 + 2 * i, N)
                act.wait_ge(fvec_ready, i + 1)
                for p in range(PIECES):
                    for half in range(HALVES):
                        act.wait_ge(hid_psum, TILES * i + 2 * p + half + 1)
                        nc.scalar.activation(PH[:, 2 * p + half, :], bank(p, half)[:, 0:N], ACT.Gelu,
                                             bias=vec["b1"]).then_inc(hid_ready, 1)
                nc.scalar.preload_act_table_set("natural_log_exp_and_others")

            def rope_inverse(p, r):
                if r >= 1:
                    act.wait_ge(r_done[p], r)
                act_rstd(act, p, K_TILE + r, N, 1)

            act.wait_ge(w_late, 16 * 7)
            early = [mw for mw in pairs if mw[0] < SLOTS]
            norms = {"final": K_FINAL, "win": K_WIN, "ffn": K_FFN, "rot": K_ROT}
            for step, p in wave(len(REST), REST_SKEW):
                kind, n = REST[step]
                g = int(kind[-1]) if kind[-1].isdigit() else 0
                if kind == "win pass 1" and early:
                    act.wait_ge(rw_ready, 4)
                    pick_pair("act", nc.scalar.copy, experts, *early.pop(0))
                if kind in norms and n == 0:
                    act_square(act, p, norms[kind], N)
                elif kind in norms and n == 1:
                    act_rstd(act, p, norms[kind], N)
                elif kind == "win":
                    if n == 2:
                        act.wait_ge(k_psum, p + 1)
                        for half in range(HALVES):
                            last = nc.scalar.activation(KB[rows(half), p, :, half, :],
                                                        tiled(bank(p, 1)[rows(half), 0:N]), ACT.Identity,
                                                        bias=wbk[rows(half)])
                        last.then_inc(k_ready, 1)
                    if n < 4:
                        for h in (2 * n - 4, 2 * n - 3):
                            act_query(act, p, A_WIN, h, wbq(h))
                elif kind == "win queries":
                    for h in (2 * n, 2 * n + 1):
                        act_query(act, p, A_WIN + 1, h, wbq(HEADS + h))
                elif kind.startswith("win pass"):
                    act_pass(act, p, A_WIN + g, n)
                elif kind == "ffn":
                    if n == 2:
                        if PICKER[2 * p + 1] == "act" and 2 * p + 1 >= SLOTS:
                            pick("act", act, nc.scalar.copy, experts, 2 * p + 1)
                        for half in range(HALVES):
                            act.wait_ge(hid_psum, TILES * LAYERS + 2 * p + half + 1)
                            nc.scalar.activation(PH[:, 2 * p + half, :], bank(p, half)[:, 0:N], ACT.Relu,
                                                 bias=f_bi).then_inc(hid_ready, 1)
                    elif n < 5:
                        for m in (2 * p, 2 * p + 1):
                            act.wait_ge(g_biased, ROUTED.index((m, n - 3)) + 1)
                            nc.scalar.activation(PH[:, m, :], PH[:, m, :], ACT.Relu).then_inc(g_ready, 1)
                elif kind == "rot":
                    if n == 2:
                        act_square(act, p, K_TILE, N)
                    elif n == 3:
                        rope_inverse(p, 0)
                    else:
                        act_values(act, p, LAYERS + 1)
                elif kind.startswith("heads"):
                    r = 1 + HEADS * g + n // 2
                    if n % 2:
                        rope_inverse(p, r)
                    else:
                        act_square(act, p, K_TILE + r, N)
                else:
                    act_pass(act, p, A_ROT + g, n)

            for p in range(PIECES):
                act_square(act, p, K_TOP, N)
            for p in range(PIECES):
                act_rstd(act, p, K_TOP, N)
            for p in range(PIECES):
                act.wait_ge(mt_psum, p + 1)
                src = B[4 + p][0:16, :].rearrange("p (i t) -> p i t", t=PAD)[:, :, 0:T]
                nc.scalar.copy(mk32[:, p], src).then_inc(mt_ready, 1)
                nc.scalar.copy(tiled(mkb[:, p, :]), src).then_inc(mt_ready, 1)
            for n in range(TOP_EXPERTS * TILES):
                e, m = n // TILES, n % TILES
                act.wait_ge(eh_psum, n + 1)
                if n >= TILES:
                    act.wait_ge(top_psum, n - TILES + 1)
                nc.scalar.activation(PH[:, m, :], B[4 + n % 2][:, 0:N], ACT.Gelu, bias=t_b1[:, e:e + 1]).then_inc(eh_ready, 1)
            for p in range(PIECES):
                act.wait_ge(out_psum, p + 1)
                nc.scalar.copy(QO[0:HQ, p].rearrange("p i h t -> p (i h t)")[:, 0:512],
                               B[p][0:HQ, :]).then_inc(out_ready, 1)

        @block.vector
        def _(dve):
            nc.vector.memset(ones[:, :], 1.0)
            nc.vector.memset(WA[:, :, 0:64], 1.0).then_inc(scaled, 1)
            nc.vector.memset(WA[:, :, 128:192], 1.0)
            nc.vector.memset(eps_t[:, 0:1], EPS)
            nc.vector.memset(eps_t[:, 1:2], RMS_EPS)
            dve.wait_ge(w_embed, 48)
            nc.vector.tensor_copy(raw_w, WA[:, :, 64:128]).then_inc(raw_kept, 1)
            dve.wait_ge(raw_kept, 1)
            nc.vector.tensor_tensor(WA[:, :, 64:128], WA[:, :, 64:128],
                                    lnp[:, 0, :].unsqueeze(2).to_broadcast([128, CHUNKS, 64]),
                                    ALU.mult).then_inc(scaled, 1)
            dve.wait_ge(colsum, 1)
            nc.vector.tensor_scalar(ZN[:, 1, 0:64], B[4][:, 0:64], 1.0 / FEATURES, None, ALU.mult).then_inc(mean_w, 1)
            dve.wait_ge(mean_w, 1)
            nc.vector.tensor_tensor(WA[:, :, 64:128], WA[:, :, 64:128],
                                    ZN[:, 1, 0:64].unsqueeze(1).to_broadcast([128, CHUNKS, 64]),
                                    ALU.subtract).then_inc(wa_ready, 1)

            def embed_sum(q):
                for part_ in range(2):
                    dve.wait_ge(img_sq, 2 * q + part_ + 1)
                    if q >= 2 and part_ == 0:
                        dve.wait_ge(sq_psum, q - 1)
                    nc.vector.tensor_reduce(SQ[:, 2 * (q % 2) + part_, 0:NP],
                                            sqi[:, 12 * part_:12 * part_ + 12, :].rearrange("p c n -> p n c"), AX.X,
                                            ALU.add).then_inc(img_sum, 1)

            def embed_variance(q):
                half = q % 2
                dve.wait_ge(sq_psum, q + 1)
                dve.wait_ge(mean_sq, q + 1)
                nc.vector.scalar_tensor_tensor(RS[rows(half), 0, 0:NP], B[2 + half][rows(half), 0:NP], 1.0 / FEATURES,
                                               RS[rows(half), 1, 0:NP], ALU.mult, ALU.subtract).then_inc(e_var, 1)

            def embed_scale(q):
                p, half = q // 2, q % 2
                dve.wait_ge(e_rstd, 2 * q + 2)
                y = patches_of(p)[rows(half)]
                nc.vector.tensor_tensor(y, EMBED_BANK[q % 4][rows(half), 0:NP], RS[rows(half), 0, 0:NP], ALU.mult).then_inc(embedded, 1)
                dve.wait_ge(embedded, 2 * q + 1)
                nc.vector.tensor_scalar(y, y, ZN[rows(half), 0, 0:1], None, ALU.add).then_inc(embedded, 1)

            experts, pairs = {}, pairs_of("dve")
            for q in range(TILES):
                embed_sum(q)
                if q == 0:
                    dve.wait_ge(shift_ready, 1)
                    dve.wait_ge(w_route, 32)
                for m, w in pairs[4 * q:4 * q + 4]:
                    load_expert(dve, experts, m, w)
                if q >= 1:
                    embed_variance(q - 1)
                    embed_scale(q - 1)
            embed_variance(TILES - 1)
            embed_scale(TILES - 1)
            for p in range(PIECES):
                dve_norm(dve, p, K_EMBED, NP, zn(p, PATCHES), normed[p])

            with dve.Fori(0, LAYERS) as i:
                rank = {"first": TILES * i, "max": nth(), "sum": nth()}
                for step, p in wave(LAYER_STEPS, LAYER_SKEW):
                    if step == 1:
                        dve_norm(dve, p, 1 + 2 * i, N, zn(p), normed[p])
                    elif step == 2:
                        dve.wait_ge(h_ready[p], 2 * i + 1)
                        for half in range(HALVES):
                            last = nc.vector.tensor_copy(KB[rows(half), p, :, half, :], zv(p)[rows(half)])
                        last.then_inc(keys_ready[p], 1)
                    elif 5 <= step < 5 + PASS:
                        dve_pass(dve, p, i, step - 5, vec["bo"], rank)
                    elif step == 6 + PASS:
                        dve_norm(dve, p, 2 + 2 * i, N, zn(p), normed[p])
                for p in range(PIECES):
                    dve_add(dve, p, down_psum, PIECES * i + p + 1, bank(p, 0), vec["b2"])
            def rope_turn(p, r):
                dve.wait_ge(centered[p], K_TILE + r + 1)
                if r == 1:
                    dve.wait_ge(keys_ready[p], LAYERS + 1)
                if r >= 1:
                    dve.wait_ge(r_done[p], r)
                nc.vector.tensor_tensor(tiled(turned_sin[:, p, :]), tiled(bank(p, 1)[:, 0:N]),
                                        sin_t.unsqueeze(1).to_broadcast([128, IMG, T]), ALU.mult).then_inc(r_turned[p], 1)
                dve.wait_ge(squared[p], K_TILE + r + 1)
                nc.vector.tensor_tensor(zn(p), tiled(bank(p, 0)[:, 0:N]),
                                        cos_t.unsqueeze(1).to_broadcast([128, IMG, T]), ALU.mult).then_inc(r_turned[p], 1)

            dve.wait_ge(w_late, 16 * 7)
            rank = {"first": TILES * A_WIN, "max": nth(), "sum": nth(), "biased": nth()}
            early = [mw for mw in pairs if mw[0] < SLOTS]
            for step, p in wave(len(REST), REST_SKEW):
                kind, n = REST[step]
                g = int(kind[-1]) if kind[-1].isdigit() else 0
                if kind == "win pass 1" and early:
                    dve.wait_ge(rw_ready, 4)
                    pick_pair("dve", nc.vector.tensor_copy, experts, *early.pop(0))
                if kind == "final" and n == 1:
                    dve_norm(dve, p, K_FINAL, N, zn(p), normed[p])
                elif kind == "win" and n == 1:
                    dve_norm(dve, p, K_WIN, N, zv(p), h_ready[p])
                elif kind == "win" and n == 4:
                    dve.wait_ge(v_psum[p], LAYERS + 1)
                    nc.vector.tensor_tensor(VT[:, p, :, :], bank(p, 0)[:, :].rearrange("p (s f) -> p s f", s=SETS),
                                            wbv.unsqueeze(1).to_broadcast([128, SETS, 128]),
                                            ALU.add).then_inc(v_ready[p], 1)
                elif kind.startswith("win pass"):
                    dve_pass(dve, p, A_WIN + g, n, None if g else wbo, rank, table=wtab[g], scale=WIN_DH ** -0.5)
                elif kind == "ffn":
                    if n == 1:
                        dve_norm(dve, p, K_FFN, N, zv(p), h_ready[p])
                    elif n == 2:
                        if PICKER[2 * p] == "dve" and 2 * p >= SLOTS:
                            pick("dve", dve, nc.vector.tensor_copy, experts, 2 * p)
                    elif n in (3, 4):
                        for m in (2 * p, 2 * p + 1):
                            wait_picked(dve, m)
                            dve.wait_ge(g_psum, ROUTED.index((m, n - 3)) + 1)
                            nc.vector.tensor_tensor(PH[:, m, :].rearrange("p (w c) -> p w c", w=PAIRS),
                                                    bank(p, m % 2)[:, 0:N].rearrange("p (w c) -> p w c", w=PAIRS),
                                                    maps(m, n - 3)[:, :, 128:129].to_broadcast([128, PAIRS, 2 * T]),
                                                    ALU.add).then_inc(g_biased, 1)
                    elif n == 5:
                        dve_add(dve, p, down_psum, PIECES * LAYERS + p + 1, bank(p, 0), f_bo)
                elif kind == "rot":
                    if n == 1:
                        dve_norm(dve, p, K_ROT, N, zv(p), h_ready[p])
                    elif n == 2:
                        rope_turn(p, 0)
                    elif n == 4:
                        if p == 0:
                            dve.wait_ge(wqk_ready, 1)
                        dve.wait_ge(r_done[p], 1)
                        for half in range(HALVES):
                            last = nc.vector.tensor_scalar(KB[rows(half), p, :, half, :], zn(p)[rows(half)],
                                                           rotv[rows(half), 0:1], None, ALU.mult)
                        last.then_inc(keys_ready[p], 1)
                elif kind.startswith("heads"):
                    if n % 2 == 0:
                        rope_turn(p, 1 + HEADS * g + n // 2)
                elif kind.startswith("rot pass"):
                    dve_pass(dve, p, A_ROT + g, n, None, rank, table=causal[0:HQ], scale=DIM ** -0.5)

            for p in range(PIECES):
                dve_norm(dve, p, K_TOP, N, zv(p), h_ready[p])
            step = [0]

            def chained(instruction):
                step[0] += 1
                instruction.then_inc(gate_step, 1)
                dve.wait_ge(gate_step, step[0])

            best = gmax[:, :].unsqueeze(2).to_broadcast([128, 32, 8])
            scores, work, mask = gate[:, 0], gate[:, 1], gate[:, 2]
            order = idx[:, :].unsqueeze(1).to_broadcast([128, 32, 8])
            dve.wait_ge(gate_psum, 1)
            dve.wait_ge(idx_ready, 1)
            chained(nc.vector.tensor_tensor(gate[:, 0].rearrange("p (n a) e -> p n (a e)", a=2),
                                            B[6][:, 0:256].rearrange("p (n c) -> p n c", c=16),
                                            t_bg.unsqueeze(1).to_broadcast([128, 16, 16]), ALU.add))
            for rank in range(2):
                chained(nc.vector.tensor_reduce(gmax[:, :], scores, AX.X, ALU.max))
                chained(nc.vector.tensor_tensor(work, scores, best, ALU.is_equal))
                chained(nc.vector.tensor_tensor(work, work, order, ALU.mult))
                chained(nc.vector.tensor_reduce(gmax[:, :], work, AX.X, ALU.max))
                if rank == 0:
                    chained(nc.vector.tensor_tensor(mask, work, best, ALU.is_equal))
                    chained(nc.vector.scalar_tensor_tensor(scores, mask, -3e38, scores, ALU.mult, ALU.add))
                else:
                    chained(nc.vector.tensor_tensor(work, work, best, ALU.is_equal))
                    nc.vector.tensor_tensor(mask, mask, work, ALU.add).then_inc(mask_ready, 1)
            for n in range(TOP_EXPERTS * TILES):
                dve.wait_ge(eh_ready, n + 1)
                nc.vector.tensor_tensor(PH[:, n % TILES, :], B[6 + n % 2][:, 0:N], PH[:, n % TILES, :],
                                        ALU.mult).then_inc(em_ready, 1)
            for p in range(PIECES):
                dve_add(dve, p, top_psum, TOP_EXPERTS * TILES - TILES + 2 * p + 2, B[p], None)

        @block.gpsimd
        def _(pool):
            nc.gpsimd.memset(Z[:, :, :, :], 0.0)
            nc.gpsimd.memset(E[:, :, :, :], 0.0)
            nc.gpsimd.memset(AB[:, :, :, :], 0.0)
            nc.gpsimd.memset(KB[:, :, :, :, :], 0.0)
            for e in range(TOP_EXPERTS):
                nc.gpsimd.memset(idx[:, e:e + 1], float(TOP_EXPERTS - e))
            nc.gpsimd.memset(gmax[:, 0:1], 0.0).then_inc(idx_ready, 1)
            pool.wait_ge(w_embed, 48)
            pool.wait_ge(idx_ready, 1)
            nc.gpsimd.tensor_scalar(evec[:, 7:6 + T], evec[:, 7:6 + T], eshift, None, ALU.add).then_inc(gained, 1)
            nc.gpsimd.tensor_tensor(evec[:, 6:7], evec[:, 6:7], ecls, ALU.add).then_inc(gained, 1)
            pool.wait_ge(gained, 2)
            for p in range(PIECES):
                pool.wait_ge(normed[p], 1)
                nc.gpsimd.tensor_scalar(zn(p, PATCHES), zn(p, PATCHES), egain, None, ALU.mult).then_inc(gained, 1)
                pool.wait_ge(gained, p + 3)
                nc.gpsimd.tensor_tensor(X[:, p, :, 1:T], zn(p, PATCHES),
                                        epos[:, 1:T].unsqueeze(1).to_broadcast([128, IMG, PATCHES]), ALU.add)
                nc.gpsimd.tensor_copy(X[:, p, :, 0:1],
                                      epos[:, 0:1].unsqueeze(1).to_broadcast([128, IMG, 1])).then_inc(x_ready[p], 1)
            with pool.Fori(0, LAYERS) as i:
                pool.wait_ge(w_layer, 16 * i + 16)
                pool.sem_inc(pool_turn, 1)
                nc.gpsimd.tensor_copy(lvec[:, 0:3], LW[:, L_VEC:L_VEC + 3]).then_inc(avec_ready, 1)
                pool.wait_ge(avec_ready, i + 1)
                pool.sem_inc(pool_turn, 1)
                for step, p in wave(LAYER_STEPS, LAYER_SKEW):
                    if step == 1:
                        pool_affine(pool, p, 1 + 2 * i, zv(p), vec["ga"], vec["ba"], h_ready[p])
                        if p == PIECES - 1:
                            nc.gpsimd.tensor_copy(lvec[:, 3:7], LW[:, L_VEC + 3:L_VEC + 7])
                            nc.gpsimd.tensor_copy(lvec[:, 7:199], LW[:, L_W1:L_W1 + 192]).then_inc(fvec_ready, 1)
                            pool.wait_ge(fvec_ready, i + 1)
                            pool.sem_inc(layer_used, 1)
                    elif 5 <= step < 5 + PASS:
                        pool_pass(pool, p, i, step - 5)
                    elif step == 6 + PASS:
                        pool_affine(pool, p, 2 + 2 * i, zv(p), vec["gf"], vec["bf"], h_ready[p])
            def merge(n):
                l, e = divmod(n, EXPERTS)
                if e == 0:
                    nc.gpsimd.tensor_tensor(f_ws[:, l, :], f_ws[:, l, :], ident, ALU.add).then_inc(rw_ready, 1)
                    pool.wait_ge(rw_ready, 2 * l + 1)
                nc.gpsimd.tensor_tensor(rw[:, n, 0:128], rw[:, n, 0:128], f_ws[:, l, :], ALU.add)
                if e == EXPERTS - 1:
                    nc.gpsimd.tensor_scalar(rw[:, EXPERTS * l:EXPERTS * l + EXPERTS, 128:129],
                                            rw[:, EXPERTS * l:EXPERTS * l + EXPERTS, 128:129], f_bs[:, l:l + 1], None,
                                            ALU.add).then_inc(rw_ready, 1)

            rope_rank = nth()

            def rope_finish(p, r, dst):
                pool.wait_ge(r_turned[p], 2 * r + 2)
                nc.gpsimd.tensor_tensor(ZN[:, p, :], ZN[:, p, :], turned_sin[:, p, :], ALU.add).then_inc(r_sum, 1)
                pool.wait_ge(r_sum, rope_rank())
                pool.wait_ge(rstd_ready[p], 2 * (K_TILE + r) + 2)
                nc.gpsimd.tensor_tensor(dst, zn(p), tiled(RS[:, p, :]), ALU.mult).then_inc(r_done[p], 1)

            pool.wait_ge(w_late, 16 * 7)
            pool.wait_ge(w_const, 16)
            nc.gpsimd.tensor_copy(selb[:, :], ident[0:16, 0:16]).then_inc(sel_ready, 1)
            nc.gpsimd.tensor_tensor(rotv[:, 0:1], rotv[:, 0:1], rotv[:, 1:2], ALU.mult).then_inc(wqk_ready, 1)
            merged = 0
            for step, p in wave(len(REST), REST_SKEW):
                kind, n = REST[step]
                g = int(kind[-1]) if kind[-1].isdigit() else 0
                if kind == "final" and n == 1:
                    pool_affine(pool, p, K_FINAL, X[:, p], fgain, fshift, x_ready[p])
                elif "pass" in kind:
                    pool_pass(pool, p, (A_WIN if kind[0] == "w" else A_ROT) + g, n)
                elif kind == "rot" and n == 3:
                    rope_finish(p, 0, zn(p))
                elif kind.startswith("heads") and n % 2:
                    rope_finish(p, 1 + HEADS * g + n // 2, QO[:, p, :, n // 2, :])
                if merged < FFN_LAYERS * EXPERTS:
                    merge(merged)
                    merged += 1


def _blocks(maps):
    n, k, m = maps.shape
    full = np.zeros((2 * k, n, 2 * m), maps.dtype)
    full[:k, :, :m] = full[k:, :, m:] = maps.transpose(1, 0, 2)
    return full


def _twice(a, axis=0):
    return np.concatenate([a, a], axis=axis)


def _rows(*vectors):
    return np.stack([_twice(v) for v in vectors], axis=1)


def _laid_out(v):
    f = {}
    g = lambda name: np.asarray(v[name])
    x = g("x").reshape(IMAGES, CHANNELS, GRID, PATCH, GRID, PATCH).transpose(1, 3, 5, 0, 2, 4)
    f["img"] = x.reshape(CHUNKS, 128, TILES, NP).transpose(2, 1, 0, 3)
    f["w_patch"] = g("L0_tok_W_patch").reshape(CHUNKS, 128, DIM).transpose(1, 0, 2)
    f["ln_p1"] = np.stack([g("L0_tok_ln_p1_g").reshape(CHUNKS, 128).T, g("L0_tok_ln_p1_b").reshape(CHUNKS, 128).T], 1)
    f["evec"] = np.concatenate([_rows(*(g("L0_tok_" + n) for n in ("ln_p2_g", "ln_p2_b", "ln_f_g", "ln_f_b",
                                                                  "b_patch"))),
                                _rows(g("L0_tok_cls").reshape(DIM)), _twice(g("L0_tok_pos").reshape(T, DIM).T)], 1)
    layers = []
    for i in range(LAYERS):
        def heads(m, twice):
            m = m.reshape(2, 128, DIM).transpose(1, 0, 2)
            return (np.concatenate([m, m], 2) if twice else m).reshape(128, -1)
        qkv = g("L0_tok_Wqkv")[i].T.reshape(3, HEADS * DIM, DIM)
        layers.append(np.concatenate(
            [heads(qkv[0], True), heads(qkv[1], False), heads(qkv[2], True), heads(g("L0_tok_Wo")[i], False),
             _twice(g("L0_tok_W1")[i]), g("L0_tok_W2")[i],
             _rows(*(g("L0_tok_" + n)[i] for n in ("attn_ln_g", "attn_ln_b", "bo", "ff_ln_g", "ff_ln_b", "b2"))),
             g("L0_tok_b1")[i][:, None]], 1))
    f["layers"] = np.stack(layers)

    qkv_w, qkv_b, pw = g("L0_attn_qkv_w"), g("L0_attn_qkv_b"), g("L0_attn_proj_w")
    wq, wo, bq = (np.zeros(s, np.float32) for s in ((WIN_HEADS, DIM, DIM), (WIN_HEADS, DIM, DIM), (128, WIN_HEADS)))
    for h in range(WIN_HEADS):
        own = slice(WIN_DH * h, WIN_DH * h + WIN_DH)
        wq[h, :, own] = qkv_w[:, own]
        wo[h, own, :] = pw[own, :]
        bq[own, h] = bq[DIM + WIN_DH * h:DIM + WIN_DH * h + WIN_DH, h] = qkv_b[own]
    f["win_w"] = _blocks(np.concatenate([wq, wo, qkv_w[None, :, DIM:2 * DIM], qkv_w[None, :, 2 * DIM:]]))
    at = np.arange(T)[:, None] - np.arange(T)[None, :] + T - 1
    tab = g("L0_attn_rpb_table")[at].transpose(2, 0, 1).reshape(2, HQ, T)
    tabs = np.zeros((128, 2, T), np.float32)
    tabs[:HQ] = tab.transpose(1, 0, 2)
    f["win_v"] = np.concatenate([bq, _rows(qkv_b[DIM:2 * DIM], g("L0_attn_proj_b")),
                                 np.broadcast_to(_twice(qkv_b[2 * DIM:])[None], (128, 128)),
                                 tabs.reshape(128, -1)], 1)

    wq = g("L1_attn_wq").reshape(ROT_HEADS, DIM, DIM).transpose(0, 2, 1)
    wk, wv = g("L1_attn_wkv").reshape(2, DIM, DIM).transpose(0, 2, 1)
    swap = np.arange(DIM) ^ 1
    wo = g("L1_attn_wo").reshape(DIM, ROT_HEADS, DIM).transpose(1, 2, 0)
    f["rot_w"] = _blocks(np.concatenate([wq, wq[:, :, swap], wo, wk[None], wk[None][:, :, swap], wv[None]]))
    f["rot_v"] = np.concatenate([_rows(g("L1_attn_q_norm_w"), g("L1_attn_k_norm_w")), np.zeros((128, 1), np.float32)], 1)

    f["ff_w"] = np.concatenate([_twice(g("L0_ffn_Wi").T), g("L0_ffn_Wo").T, g("L0_ffn_bi")[:, None],
                                _rows(g("L0_ffn_bo")), g("L0_ffn_bs")[:, 0].T,
                                g("L0_ffn_Ws")[:, 0].transpose(2, 0, 1).reshape(128, 256)], 1)
    wr = g("L0_ffn_Wr").reshape(FFN_LAYERS * EXPERTS, 128, 128).transpose(2, 0, 1)
    br = g("L0_ffn_br").reshape(FFN_LAYERS * EXPERTS, 128).T[:, :, None]
    f["ff_r"] = np.concatenate([wr, br], 2)
    f["route"] = g("L0_ffn_route_id").reshape(1, ROUTES)

    wg = np.zeros((128, 2, 8), np.float32)
    wg[:64, 0] = wg[64:, 1] = g("L1_ffn_Wg")
    w1 = np.zeros((2, DIM, TOP_EXPERTS, 2, 128), np.float32)
    w1[0, :, :, 0] = w1[1, :, :, 1] = g("L1_ffn_W1").transpose(1, 0, 2)
    f["top_w1"] = w1.reshape(128, 2 * TOP_EXPERTS, 128)
    f["top_w"] = np.concatenate([g("L1_ffn_W2").transpose(1, 0, 2).reshape(128, -1), g("L1_ffn_b1").T,
                                 wg.reshape(128, 16), np.broadcast_to(_twice(g("L1_ffn_bg"))[None], (128, 16))], 1)
    b2 = np.zeros((16, 128), np.float32)
    b2[:8, :64] = b2[8:, 64:] = g("L1_ffn_b2")
    f["top_b2"] = b2

    eye = np.eye(128, dtype=np.float32)
    mean = np.zeros((128, 128), np.float32)
    mean[:64, :64] = mean[64:, 64:] = 1.0 / DIM
    freqs = np.float32(10000.0) ** (-2.0 * np.arange(DIM // 2, dtype=np.float32) / DIM).astype(np.float32)
    theta = (np.arange(T, dtype=np.float32)[None] * freqs[:, None]).astype(np.float32)
    cos = _twice(np.repeat(np.cos(theta), 2, axis=0))
    sin = np.repeat(np.sin(theta), 2, axis=0)
    sin[0::2] = -sin[0::2]
    mask = np.zeros((128, T), np.float32)
    mask[:HQ] = np.tile(np.where(np.arange(T)[None] <= np.arange(T)[:, None], 0.0, NEG), (HEADS, 1))
    f["consts"] = np.concatenate([eye, eye - mean, mean, cos, _twice(sin), mask], 1).astype(np.float32)
    return {k: np.ascontiguousarray(a) for k, a in f.items()}


def kernel(**inputs):
    import concourse.bacc as _bacc
    from concourse.bass_utils import run_bass_kernel_spmd as _run

    nc = _bacc.Bacc("TRN2", target_bir_lowering=False, num_devices=1)
    arrays = {f"in_{k}": a for k, a in _laid_out(inputs).items()}
    d = {k[3:]: nc.dram_tensor(k, a.shape, mybir.dt.from_np(a.dtype), kind="ExternalInput").ap()
         for k, a in arrays.items()}
    o = nc.dram_tensor("out_0", (IMAGES, T, DIM), FP32, kind="ExternalOutput").ap()
    o = [o[IMG * m:IMG * m + IMG].rearrange("(s j) t f -> (j t) s f", s=SETS) for m in range(TILES)]
    build(nc, d, o)
    r = _run(nc, [arrays], core_ids=[0])
    return r.results[0]["out_0"]
```

```python
from contextlib import ExitStack

import numpy as np
import concourse.bass as bass
import concourse.mybir as mybir

FP32 = mybir.dt.float32
BF16 = mybir.dt.bfloat16
I32 = mybir.dt.int32
ALU = mybir.AluOpType
ACT = mybir.ActivationFunctionType
AX = mybir.AxisListType

IMAGES, PATCH, GRID, CHANNELS, DIM = 128, 32, 4, 3, 64
PATCHES = GRID * GRID
FEATURES = CHANNELS * PATCH * PATCH
T = PATCHES + 1
LAYERS, HEADS, HIDDEN = 4, 4, 128
PIECES, HALVES = 4, 2
IMG = IMAGES // (PIECES * HALVES)
N = IMG * T
NP = IMG * PATCHES
PAD = 32
SETS = IMG // 4
HQ = HEADS * T
CHUNKS = FEATURES // 128
TILES = PIECES * HALVES
EPS = 1e-5
RMS_EPS = 1.1920929e-07
WIN_HEADS, WIN_DH = 8, 8
ROT_HEADS = 16
ROUTES, FFN_LAYERS, EXPERTS = 64, 2, 16
PAIRS = IMG // 2
SLOTS = 4
PICKER = ["dve", "act"] * (TILES // 2)
ROUTED = [(2 * p + half, l) for p in range(PIECES) for l in range(FFN_LAYERS) for half in range(HALVES)]
TOP_EXPERTS = 8
NEG = -1e30
ARENA = 24600

L_Q, L_K, L_V, L_O, L_W1, L_W2, L_VEC = 0, 256, 384, 640, 768, 896, 960
L_ALL = L_VEC + 7
X_EMBED, X_FINAL, X_WIN, X_FFN, X_ROT, X_TOP = 0, 9, 10, 12, 13, 17
K_EMBED, K_FINAL, K_WIN, K_FFN, K_ROT, K_TILE, K_TOP = 0, 9, 10, 11, 12, 13, 14 + ROT_HEADS
H_WIN, H_FFN, H_ROT, H_TOP = 8, 9, 10, 11
A_WIN, A_ROT = 4, 6
WIN_PASSES, ROT_PASSES = 2, 4


def wave(steps, skew):
    for t in range(steps + skew * (PIECES - 1)):
        for p in range(PIECES):
            if 0 <= t - skew * p < steps:
                yield t - skew * p, p


def build(nc, d, out):
    ctx = ExitStack()
    with ctx:
        def sb(name, shape, dt=FP32):
            return ctx.enter_context(nc.sbuf_tensor(name, shape, dt))

        def sem(name):
            return ctx.enter_context(nc.semaphore(name))

        X = sb("X", [128, PIECES, IMG, T])
        Z = sb("Z", [128, PIECES, IMG, PAD])
        ZN = sb("ZN", [128, PIECES, N])
        SQ = sb("SQ", [128, PIECES, N])
        RS = sb("RS", [128, PIECES, N])
        QO = sb("QO", [128, PIECES, IMG, HEADS, T])
        KB = sb("KB", [128, PIECES, IMG, HALVES, T])
        E = sb("E", [HQ, TILES, IMG, PAD])
        PH = sb("PH", [128, TILES, N])
        VT = sb("VT", [128, PIECES, SETS, 128])
        mx = sb("mx", [HQ, TILES, IMG])
        sm = sb("sm", [HQ, TILES, IMG])
        rc = sb("rc", [HQ, TILES, IMG])
        consts = sb("consts", [128, 3 * 128 + 3 * T])
        ident, cen, avg = (consts[:, 128 * n:128 * n + 128] for n in range(3))
        cos_t, sin_t, causal = (consts[:, 384 + T * n:384 + T * n + T] for n in range(3))
        eps_t = sb("eps_t", [128, 2])
        ones = sb("ones", [128, 128])
        LW = sb("LW", [128, L_ALL])
        lvec = sb("lvec", [128, 7 + 128 + 64])
        AB = sb("AB", [128, 2, HEADS, 128])
        evec = sb("evec", [128, 6 + T])
        arena = sb("arena", [128, ARENA])

        used = [0]

        def part(*shape):
            n = int(np.prod(shape))
            o = used[0]
            used[0] += n
            v = arena[:, o:o + n]
            if len(shape) == 2:
                v = v.rearrange("p (a b) -> p a b", a=shape[0])
            if len(shape) == 3:
                v = v.rearrange("p (a b c) -> p a b c", a=shape[0], b=shape[1])
            return v

        img = [part(CHUNKS, NP) for _ in range(2)]
        sqi = part(CHUNKS, NP)
        WA = part(CHUNKS, 192)
        lnp = part(2, CHUNKS)
        assert used[0] <= ARENA
        used[0] = 0
        winw = part(2 * WIN_HEADS + 2, 128)
        winv = part(WIN_HEADS + 2 + 128 + T * 2 + WIN_HEADS)
        rotw = part(3 * ROT_HEADS + 3, 128)
        rotv = part(3)
        ffw = part(128 + 64 + 2 + 2 + 256)
        rw = part(FFN_LAYERS * EXPERTS, 129)
        picked = part(SLOTS * FFN_LAYERS, PAIRS, 129)
        topw = part(TOP_EXPERTS * (64 + 1) + 16 + 16)
        turned_sin = part(PIECES, N)
        assert used[0] <= ARENA
        gate = picked[:, 0].rearrange("p a b -> p (a b)")[:, 0:768].rearrange("p (a b c) -> p a b c", a=3, b=32)
        mk32 = picked[0:16, 1:3].rearrange("p n a b -> p (n a b)")[:, 0:PIECES * N] \
            .rearrange("p (q i t) -> p q i t", q=PIECES, i=IMG)
        route = sb("route", [1, ROUTES], I32)
        selb = sb("selb", [16, 16], BF16)
        b2d = sb("b2d", [16, 128])
        gmax = sb("gmax", [128, 32])
        idx = sb("idx", [128, 8])
        mkb = sb("mkb", [16, PIECES, N], BF16)
        B = [ctx.enter_context(nc.psum_tensor(f"bank{n}", [128, 512], FP32)) for n in range(8)]

        def each(name):
            return [sem(f"{name}{p}") for p in range(PIECES)]

        w_embed, w_const, w_late, w_route = sem("w_embed"), sem("w_const"), sem("w_late"), sem("w_route")
        w_layer, layer_used = sem("w_layer"), sem("layer_used")
        img_in = [[sem(f"img_in{n}{half}") for half in range(2)] for n in range(2)]
        chunk_sum, scaled, colsum, mean_w, wa_ready = (sem("chunk_sum"), sem("scaled"), sem("colsum"), sem("mean_w"),
                                                      sem("wa_ready"))
        shift_psum, shift_ready = sem("shift_psum"), sem("shift_ready")
        img_sq, img_sum, embed_psum, sq_psum = sem("img_sq"), sem("img_sum"), sem("embed_psum"), sem("sq_psum")
        mean_sq, e_var, e_rstd, embedded = (sem("mean_sq"), sem("e_var"), sem("e_rstd"),
                                                   sem("embedded"))
        x_ready, centered, squared, var_psum = each("x_ready"), each("centered"), each("squared"), each("var_psum")
        rstd_ready, normed, h_ready = each("rstd_ready"), each("normed"), each("h_ready")
        gained = sem("gained")
        ab_psum, ab_ready, fvec_ready, avec_ready = sem("ab_psum"), sem("ab_ready"), sem("fvec_ready"), sem("avec_ready")
        q_psum, q_ready, v_psum, v_ready = each("q_psum"), each("q_ready"), each("v_psum"), each("v_ready")
        k_psum, k_ready, keys_ready = sem("k_psum"), sem("k_ready"), each("keys_ready")
        s_psum, s_biased, maxed, s_ready, expd = (each("s_psum"), sem("s_biased"), sem("maxed"), each("s_ready"),
                                                  each("expd"))
        summed, inv_ready, probs_ready = sem("summed"), each("inv_ready"), each("probs_ready")
        pt_psum, pt_ready, pv_psum, o_ready, y_psum = (each("pt_psum"), each("pt_ready"), each("pv_psum"),
                                                       each("o_ready"), each("y_psum"))
        hid_psum, hid_ready, down_psum = sem("hid_psum"), sem("hid_ready"), sem("down_psum")
        g_psum, g_biased, g_ready = sem("g_psum"), sem("g_biased"), sem("g_ready")
        rw_ready = sem("rw_ready")
        picked_by = {who: sem(f"picked_by_{who}") for who in ("dve", "act")}
        r_turned, r_sum, r_done = each("r_turned"), sem("r_sum"), each("r_done")
        wqk_ready = sem("wqk_ready")
        gate_psum, gate_step, mask_ready, mt_psum, mt_ready = (sem("gate_psum"), sem("gate_step"), sem("mask_ready"),
                                                               sem("mt_psum"), sem("mt_ready"))
        sel_ready, eh_psum, eh_ready, em_ready, top_psum = (sem("sel_ready"), sem("eh_psum"), sem("eh_ready"),
                                                            sem("em_ready"), sem("top_psum"))
        out_psum, out_ready, out_sent = sem("out_psum"), sem("out_ready"), sem("out_sent")
        idx_ready, pool_turn = sem("idx_ready"), sem("pool_turn")

        def rows(half):
            return slice(64 * half, 64 * half + 64)

        def zv(p):
            return Z[:, p, :, 0:T]

        def zn(p, t=T):
            return ZN[:, p, 0:IMG * t].rearrange("p (i t) -> p i t", t=t)

        def tiled(ap):
            return ap.rearrange("p (i t) -> p i t", t=T)

        def bank(p, n):
            return B[2 * p + n]

        def x_of(p):
            return X[:, p, :, :].rearrange("p i t -> p (i t)")

        def patches_of(p):
            return QO[:, p].rearrange("p i h t -> p (i h t)")[:, 0:NP]

        def maps(m, l):
            return picked[:, FFN_LAYERS * (m % SLOTS) + l]

        def pairs_of(who):
            return [(m, w) for m in range(TILES) if PICKER[m] == who for w in range(PAIRS)]

        def load_expert(engine, experts, m, w):
            experts[m, w] = engine.value_load(route[0:1, PAIRS * m + w:PAIRS * m + w + 1], min_val=0,
                                              max_val=EXPERTS - 1)

        def pick_pair(who, copy, experts, m, w):
            for l in range(FFN_LAYERS):
                last = copy(maps(m, l)[:, w, :],
                            rw[:, bass.ds(experts[m, w] + EXPERTS * l, 1), :].rearrange("p a c -> p (a c)"))
            if w == PAIRS - 1:
                last.then_inc(picked_by[who], 1)

        def pick(who, engine, copy, experts, m):
            engine.wait_ge(g_biased, ROUTED.index((m - SLOTS, FFN_LAYERS - 1)) + 1)
            for w in range(PAIRS):
                pick_pair(who, copy, experts, m, w)

        def wait_picked(engine, m):
            engine.wait_ge(picked_by[PICKER[m]], PICKER[:m + 1].count(PICKER[m]))


        def pe_centre(pe, p, k, src, width, ready):
            pe.wait_ge(*ready)
            nc.tensor.matmul(bank(p, 0)[:, 0:width], cen, src, start=True, stop=True).then_inc(centered[p], 1)

        def pe_variance(pe, p, k, width):
            pe.wait_ge(squared[p], k + 1)
            nc.tensor.matmul(bank(p, 1)[:, 0:width], avg, SQ[:, p, 0:width], start=True,
                             stop=True).then_inc(var_psum[p], 1)

        def act_square(act, p, k, width):
            act.wait_ge(centered[p], k + 1)
            nc.scalar.activation(SQ[:, p, 0:width], bank(p, 0)[:, 0:width], ACT.Square).then_inc(squared[p], 1)

        def act_rstd(act, p, k, width, eps=0):
            act.wait_ge(var_psum[p], k + 1)
            nc.scalar.activation(RS[:, p, 0:width], bank(p, 1)[:, 0:width], ACT.Ln,
                                 bias=eps_t[:, eps:eps + 1]).then_inc(rstd_ready[p], 1)
            act.wait_ge(rstd_ready[p], 2 * k + 1)
            nc.scalar.activation(RS[:, p, 0:width], RS[:, p, 0:width], ACT.Exp, scale=-0.5).then_inc(rstd_ready[p], 1)

        def dve_norm(dve, p, k, width, dst, done):
            dve.wait_ge(rstd_ready[p], 2 * k + 2)
            nc.vector.tensor_tensor(dst, bank(p, 0)[:, 0:width].rearrange("p (i t) -> p i t", i=IMG),
                                    RS[:, p, 0:width].rearrange("p (i t) -> p i t", i=IMG), ALU.mult).then_inc(done, 1)

        def pool_affine(pool, p, k, dst, gain, shift, done):
            pool.wait_ge(normed[p], k + 1)
            if not isinstance(k, int):
                pool.sem_inc(pool_turn, 1)
            nc.gpsimd.tensor_scalar(dst, zn(p), gain, shift, ALU.mult, ALU.add).then_inc(done, 1)

        def pe_query(pe, p, a, h, weight):
            if h >= 2:
                pe.wait_ge(q_ready[p], HEADS * a + h - 1)
            nc.tensor.matmul(bank(p, h % 2)[:, 0:N], weight, zv(p), start=True, stop=True).then_inc(q_psum[p], 1)

        def act_query(act, p, a, h):
            act.wait_ge(q_psum[p], HEADS * a + h + 1)
            nc.scalar.copy(QO[:, p, :, h, :], tiled(bank(p, h % 2)[:, 0:N])).then_inc(q_ready[p], 1)

        def act_window_queries(act, p, g):
            act.wait_ge(q_psum[p], HEADS * (A_WIN + g) + HEADS)
            for h in range(HEADS):
                nc.scalar.activation(QO[:, p, :, h, :], tiled(bank(p, 0)[:, 0:N]), ACT.Identity,
                                     scale=own_rows(HEADS * g + h), bias=wbq(HEADS * g + h)).then_inc(q_ready[p], 1)

        def pe_values(pe, p, weight):
            for s in range(SETS):
                src = Z[:, p, 4 * s:4 * s + 4, :].rearrange("p i t -> p (i t)")
                o = bank(p, 0)[:, 128 * s:128 * s + 128]
                if weight is None:
                    last = nc.tensor.transpose(o, src, ident)
                else:
                    last = nc.tensor.matmul(o, src, weight, start=True, stop=True)
            last.then_inc(v_psum[p], 1)

        def act_values(act, p, v):
            act.wait_ge(v_psum[p], v + 1)
            nc.scalar.copy(VT[:, p, :, :], bank(p, 0)[:, :].rearrange("p (s f) -> p s f", s=SETS)).then_inc(v_ready[p], 1)

        def pe_scores(pe, p, u):
            for i in range(IMG // 2):
                o = bank(p, 1 - u)[0:HQ, 0:N].rearrange("p (k i t) -> p k i t", k=HALVES, t=T)[:, :, i, :]
                last = nc.tensor.matmul(o, QO[:, p, IMG // 2 * u + i, :, :].rearrange("p h t -> p (h t)"),
                                        KB[:, p, IMG // 2 * u + i], start=True, stop=True)
            last.then_inc(s_psum[p], 1)

        def probs(p, half):
            return E[:, 2 * p + half, :, 0:T]

        def per_row(stat, p, half):
            return stat[:, 2 * p + half, :].unsqueeze(2).to_broadcast([HQ, IMG, T])

        def nth():
            seen = [0]

            def following():
                seen[0] += 1
                return seen[0]
            return following

        def dve_centre(dve, p, a, half, rank, table=None, scale=1.0):
            dve.wait_ge(s_psum[p], 2 * a + half + 1)
            src = tiled(bank(p, 1 - half)[0:HQ, 0:N])
            if table is not None:
                nc.vector.scalar_tensor_tensor(probs(p, half), src, scale,
                                               table.unsqueeze(1).to_broadcast([HQ, IMG, T]), ALU.mult,
                                               ALU.add).then_inc(s_biased, 1)
                dve.wait_ge(s_biased, rank["biased"]())
                src = probs(p, half)
            nc.vector.tensor_reduce(mx[:, 2 * p + half, :], src, AX.X, ALU.max).then_inc(maxed, 1)
            dve.wait_ge(maxed, rank["first"] + rank["max"]())
            nc.vector.tensor_tensor(probs(p, half), src, per_row(mx, p, half), ALU.subtract).then_inc(s_ready[p], 1)

        def act_exp(act, p, a, half, scale=1.0):
            act.wait_ge(s_ready[p], 2 * a + half + 1)
            nc.scalar.activation(probs(p, half), probs(p, half), ACT.Exp, scale=scale).then_inc(expd[p], 1)

        def dve_total(dve, p, a, half, rank):
            dve.wait_ge(expd[p], 2 * a + half + 1)
            nc.vector.tensor_reduce(sm[:, 2 * p + half, :], probs(p, half), AX.X, ALU.add).then_inc(summed, 1)
            dve.wait_ge(summed, rank["first"] + rank["sum"]())
            nc.vector.reciprocal(rc[:, 2 * p + half, :], sm[:, 2 * p + half, :]).then_inc(inv_ready[p], 1)

        def pool_probs(pool, p, a, half):
            pool.wait_ge(inv_ready[p], 2 * a + half + 1)
            nc.gpsimd.tensor_tensor(probs(p, half), probs(p, half), per_row(rc, p, half),
                                    ALU.mult).then_inc(probs_ready[p], 1)

        def pe_turn_probs(pe, p, a, half):
            pe.wait_ge(probs_ready[p], 2 * a + half + 1)
            for s in range(SETS):
                last = nc.tensor.transpose(bank(p, 1 - half)[:, HQ * s:HQ * s + HQ],
                                           E[:, 2 * p + half, 4 * s:4 * s + 4, :].rearrange("p i t -> p (i t)"),
                                           ident[0:HQ, 0:HQ])
            last.then_inc(pt_psum[p], 1)

        def act_turned(act, p, a, half):
            act.wait_ge(pt_psum[p], 2 * a + half + 1)
            nc.scalar.copy(PH[:, 2 * p + half, :], bank(p, 1 - half)[:, 0:N]).then_inc(pt_ready[p], 1)

        def pe_mix(pe, p, a, j):
            if j == 0:
                pe.wait_ge(pt_ready[p], 2 * a + 2)
            if j >= 2:
                pe.wait_ge(o_ready[p], 4 * a + j - 1)
            for s in range(SETS):
                for half in range(HALVES):
                    at = HQ * (2 * half + s % 2)
                    last = nc.tensor.matmul(bank(p, j % 2)[rows(half), HQ * s:HQ * s + HQ],
                                            VT[PAD * j:PAD * j + PAD, p, s, rows(half)],
                                            PH[PAD * j:PAD * j + PAD, 2 * p + s // 2, at:at + HQ],
                                            start=True, stop=True)
            last.then_inc(pv_psum[p], 1)

        def act_mixed(act, p, a, j):
            act.wait_ge(pv_psum[p], 4 * a + j + 1)
            nc.scalar.copy(QO[:, p, j:IMG:4, :, :].rearrange("p s h t -> p s (h t)"),
                           bank(p, j % 2)[:, 0:N].rearrange("p (s c) -> p s c", s=SETS)).then_inc(o_ready[p], 1)

        def pe_project(pe, p, a, weight):
            pe.wait_ge(o_ready[p], 4 * a + 4)
            for h in range(HEADS):
                last = nc.tensor.matmul(bank(p, 0)[:, 0:N], weight(h), QO[:, p, :, h, :], start=h == 0,
                                        stop=h == HEADS - 1)
            last.then_inc(y_psum[p], 1)

        def dve_add(dve, p, produced, count, src, bias):
            dve.wait_ge(produced, count)
            if bias is None:
                nc.vector.tensor_tensor(X[:, p], tiled(src[:, 0:N]), X[:, p], ALU.add).then_inc(x_ready[p], 1)
            else:
                nc.vector.scalar_tensor_tensor(X[:, p], tiled(src[:, 0:N]), bias, X[:, p], ALU.add,
                                               ALU.add).then_inc(x_ready[p], 1)

        S0, S1, SM, PT, M0, M1, PR = range(7)
        PASS = 7

        def pe_pass(pe, p, a, step, weight):
            if step in (S0, S1):
                pe_scores(pe, p, step - S0)
            elif step == PT:
                for half in range(HALVES):
                    pe_turn_probs(pe, p, a, half)
            elif step in (M0, M1):
                for j in (2 * (step - M0), 2 * (step - M0) + 1):
                    pe_mix(pe, p, a, j)
            elif step == PR:
                pe_project(pe, p, a, weight)

        def act_pass(act, p, a, step, scale=1.0):
            if step in (S1, SM):
                act_exp(act, p, a, step - S1, scale)
            elif step == PT:
                for half in range(HALVES):
                    act_turned(act, p, a, half)
            elif step in (M0, M1):
                for j in (2 * (step - M0), 2 * (step - M0) + 1):
                    act_mixed(act, p, a, j)

        def dve_pass(dve, p, a, step, bias, rank, **table):
            if step in (S0, S1):
                dve_centre(dve, p, a, step - S0, rank, **table)
            if step in (S1, SM):
                dve_total(dve, p, a, step - S1, rank)
            elif step == PR:
                dve_add(dve, p, y_psum[p], a + 1, bank(p, 0), bias)

        def pool_pass(pool, p, a, step):
            if step in (S1, SM):
                pool_probs(pool, p, a, step - S1)

        vec = {name: lvec[:, n:n + 1] for n, name in enumerate(["ga", "ba", "bo", "gf", "bf", "b2", "b1"])}
        lw1, lw2 = lvec[:, 7:135], lvec[:, 135:199]
        egain, eshift, fgain, fshift = (evec[:, n:n + 1] for n in range(4))
        epatch_bias, ecls = evec[:, 4:5], evec[:, 5:6]
        epos = evec[:, 6:6 + T]
        wo_w = lambda h: winw[:, h, :]
        wq_w, wk_w, wv_w = (winw[:, WIN_HEADS + n, :] for n in range(3))
        wbq, wbk, wbo = (lambda h: winv[:, h:h + 1]), winv[:, WIN_HEADS:WIN_HEADS + 1], \
            winv[:, WIN_HEADS + 1:WIN_HEADS + 2]
        wbv = winv[:, WIN_HEADS + 2:WIN_HEADS + 130]
        wtab = [winv[0:HQ, WIN_HEADS + 130 + T * g:WIN_HEADS + 130 + T * g + T] for g in range(2)]
        own_rows = lambda h: winv[:, 2 * T + WIN_HEADS + 130 + h:2 * T + WIN_HEADS + 131 + h]
        f_wi, f_wo = ffw[:, 0:128], ffw[:, 128:192]
        f_bi, f_bo, f_bs = ffw[:, 192:193], ffw[:, 193:194], ffw[:, 194:196]
        f_ws = ffw[:, 196:452].rearrange("p (l f) -> p l f", l=2)
        t_w1 = winw[:, 0:16, :]
        t_w2 = topw[:, 0:512].rearrange("p (e f) -> p e f", e=8)
        t_b1, t_wg, t_bg = topw[:, 512:520], topw[:, 520:536], topw[:, 536:552]
        EMBED_BANK = [B[0], B[1], B[6], B[7]]
        raw_w = PH[:, :, :].rearrange("p m n -> p (m n)")[:, 0:CHUNKS * DIM].rearrange("p (c f) -> p c f", c=CHUNKS)

        LAYER_STEPS = 3 + PASS + 2
        LAYER_SKEW = 2
        REST = [(kind, n) for kind, steps in (("win", 4), ("win pass 0", PASS), ("win queries", 1),
                                              ("win pass 1", PASS), ("ffn", 6), ("rot", 5)) for n in range(steps)]
        REST += [step for g in range(ROT_PASSES) for step in [(f"heads {g}", n) for n in range(2 * HEADS)]
                 + [(f"rot pass {g}", n) for n in range(PASS)]]
        REST += [("top", n) for n in range(4)]
        REST_SKEW = 3

        block = ctx.enter_context(nc.Block())

        @block.sync
        def _(sp):
            def load_image(q):
                if q >= 2:
                    sp.wait_ge(embed_psum, q - 1)
                    sp.wait_ge(img_sq, 2 * (q - 1))
                for n in range(2):
                    c = slice(n * CHUNKS // 2, (n + 1) * CHUNKS // 2)
                    sp.dma_start(img[q % 2][:, c, :], d["img"][q][:, c, :]).then_inc(img_in[q % 2][n], 16)

            sp.dma_start(raw_w, d["w_patch"]).then_inc(w_embed, 16)
            sp.dma_start(lnp, d["ln_p1"]).then_inc(w_embed, 16)
            sp.dma_start(evec[:, :], d["evec"]).then_inc(w_embed, 16)
            sp.dma_start(route[:, :], d["route"]).then_inc(w_route, 16)
            sp.dma_start(b2d[:, :], d["top_b2"]).then_inc(w_route, 16)
            load_image(0)
            sp.dma_start(consts[:, :], d["consts"]).then_inc(w_const, 16)
            load_image(1)
            sp.dma_start(LW[:, :], d["layers"][0]).then_inc(w_layer, 16)
            for q in range(2, TILES):
                load_image(q)
            sp.wait_ge(embedded, 2 * TILES)
            sp.wait_ge(shift_psum, HALVES * CHUNKS)
            for dst, name in ((winw[:, 0:WIN_HEADS + 3, :], "win_w"), (winv, "win_v"), (rotw, "rot_w"), (rotv, "rot_v"), (ffw, "ff_w"),
                              (rw, "ff_r"), (topw, "top_w")):
                sp.dma_start(dst, d[name]).then_inc(w_late, 16)
            with sp.Fori(1, LAYERS) as i:
                sp.wait_ge(layer_used, 2 * i)
                sp.dma_start(LW[:, :], d["layers"][bass.ds(i, 1)].rearrange("a p n -> (a p) n")).then_inc(w_layer, 16)
            for p in range(PIECES):
                sp.wait_ge(y_psum[p], A_WIN + WIN_PASSES)
            sp.dma_start(t_w1, d["top_w1"]).then_inc(w_late, 16)
            for p in range(PIECES):
                sp.wait_ge(out_ready, p + 1)
                for half in range(HALVES):
                    sp.dma_start(out[HALVES * p + half], QO[0:HQ, p].rearrange("p i h t -> p (i h t)")[:, 0:512]
                                 .rearrange("p (s h f) -> p s h f", s=SETS, h=2)[:, :, half, :]).then_inc(out_sent, 16)
            sp.wait_ge(out_sent, 16 * TILES)

        @block.tensor
        def _(pe):
            def embed_rows(q):
                half = q % 2
                if q == 2:
                    pe.wait_ge(shift_ready, 1)
                if q >= 4:
                    pe.wait_ge(embedded, 2 * (q - 3))
                lo = 64 if half == 0 else 0
                for c in range(CHUNKS):
                    if c % (CHUNKS // 2) == 0:
                        pe.wait_ge(img_in[q % 2][1 if c else 0], 16 * (q // 2) + 16)
                    last = nc.tensor.matmul(EMBED_BANK[q % 4][:, 0:NP], WA[:, c, lo:lo + 128], img[q % 2][:, c, :],
                                            start=c == 0, stop=c == CHUNKS - 1)
                last.then_inc(embed_psum, 1)

            def embed_squares(q):
                if q >= 2:
                    pe.wait_ge(e_var, q - 1)
                pe.wait_ge(img_sum, 3 * q + 3)
                nc.tensor.matmul(B[2 + q % 2][:, 0:NP], ones[:, :], SQ[:, 2 * (q % 2), 0:NP], start=True,
                                 stop=True).then_inc(sq_psum, 1)

            def shift(half):
                for c in range(CHUNKS):
                    nc.tensor.matmul(B[5 + half][rows(half), 0:1], raw_w[:, c, :], lnp[:, 1, c:c + 1], start=c == 0,
                                     stop=c == CHUNKS - 1).then_inc(shift_psum, 1)

            pe.wait_ge(w_embed, 48)
            shift(0)
            pe.wait_ge(chunk_sum, 1)
            nc.tensor.matmul(B[4][:, 0:64], ones[:, :], SQ[:, 0, 0:64], start=True, stop=True).then_inc(colsum, 1)
            shift(1)
            pe.wait_ge(wa_ready, 1)
            for q in range(TILES):
                embed_rows(q)
                if q >= 1:
                    embed_squares(q - 1)
            embed_squares(TILES - 1)
            pe.wait_ge(w_const, 16)
            pe.wait_ge(shift_ready, 1)
            for p in range(PIECES):
                pe_centre(pe, p, K_EMBED, patches_of(p), NP, (embedded, 2 * TILES))
            for p in range(PIECES):
                pe_variance(pe, p, K_EMBED, NP)

            def layer_maps(i, logs):
                pe.wait_ge(w_layer, 16 * i + 16)
                pe.wait_ge(rstd_ready[0], logs)
                pe.wait_ge(rstd_ready[1], logs)
                for h in range(HEADS):
                    r = rows(h % 2)
                    hp = h // 2
                    o = B[1 + 2 * (h % 2)]
                    nc.tensor.matmul(o[:, 64 * hp:64 * hp + 64], LW[r, L_Q + 128 * hp:L_Q + 128 * hp + 128],
                                     LW[r, L_K + 64 * hp:L_K + 64 * hp + 64], start=True, stop=True)
                    last = nc.tensor.matmul(o[:, 128 + 64 * hp:192 + 64 * hp],
                                            LW[r, L_V + 128 * hp:L_V + 128 * hp + 128],
                                            LW[r, L_O + 64 * hp:L_O + 64 * hp + 64], start=True, stop=True)
                last.then_inc(ab_psum, 1)

            def norm_all(k, u):
                for p in range(PIECES):
                    pe_centre(pe, p, k, x_of(p), N, (x_ready[p], u))
                for p in range(PIECES):
                    pe_variance(pe, p, k, N)

            def layer(i, last_layer):
                pe.wait_ge(ab_ready, 8 * i + 8)
                for step, p in wave(LAYER_STEPS, LAYER_SKEW):
                    if step in (0, 1):
                        if step == 0:
                            pe.wait_ge(h_ready[p], 2 * i + 1)
                        for h in (2 * step, 2 * step + 1):
                            pe_query(pe, p, i, h, AB[:, 0, h, :])
                    elif step == 2:
                        pe.wait_ge(q_ready[p], 4 * i + 4)
                        pe_values(pe, p, None)
                    elif step < 3 + PASS:
                        if step == 3 + S0:
                            pe.wait_ge(keys_ready[p], i + 1)
                        if step == 3 + S1:
                            pe.wait_ge(v_ready[p], i + 1)
                        pe_pass(pe, p, i, step - 3, lambda h: AB[:, 1, h, :])
                    elif step == 3 + PASS:
                        pe_centre(pe, p, 2 + 2 * i, x_of(p), N, (x_ready[p], 2 * i + 2))
                        if p == 2 and not last_layer:
                            layer_maps(i + 1, 4 * i + 5)
                    else:
                        pe_variance(pe, p, 2 + 2 * i, N)
                pe.wait_ge(fvec_ready, i + 1)
                for p in range(PIECES):
                    pe.wait_ge(h_ready[p], 2 * i + 2)
                    if p == 0 and not last_layer:
                        pe.wait_ge(ab_ready, 8 * i + 16)
                    for half in range(HALVES):
                        nc.tensor.matmul(bank(p, half)[:, 0:N], lw1[rows(half), :], zv(p)[rows(half)], start=True,
                                         stop=True).then_inc(hid_psum, 1)
                for p in range(PIECES):
                    pe.wait_ge(hid_ready, TILES * i + 2 * p + 2)
                    for half in range(HALVES):
                        last = nc.tensor.matmul(bank(p, 0)[rows(half), 0:N], lw2, PH[:, 2 * p + half, :], start=True,
                                                stop=True)
                    last.then_inc(down_psum, 1)
                norm_all(3 + 2 * i, 2 * i + 3)

            layer_maps(0, 1)
            for p in range(PIECES):
                pe_centre(pe, p, 1, x_of(p), N, (x_ready[p], 1))
            pe.wait_ge(ab_ready, 8)
            for p in range(PIECES):
                pe_variance(pe, p, 1, N)
            with pe.Fori(0, LAYERS - 1) as i:
                layer(i, False)
            layer(LAYERS - 1, True)

            def turned(p, r, w, w_swapped):
                if r >= 1:
                    pe.wait_ge(rstd_ready[p], 2 * (K_TILE + r) - 1)
                nc.tensor.matmul(bank(p, 0)[:, 0:N], w, zv(p), start=True, stop=True)
                nc.tensor.matmul(bank(p, 1)[:, 0:N], w_swapped, zv(p), start=True, stop=True).then_inc(centered[p], 1)

            def lengths(p, r):
                pe.wait_ge(squared[p], K_TILE + r + 1)
                pe.wait_ge(r_turned[p], 2 * r + 1)
                nc.tensor.matmul(bank(p, 1)[:, 0:N], avg, SQ[:, p, :], start=True, stop=True).then_inc(var_psum[p], 1)

            pe.wait_ge(w_late, 16 * 7)
            for step, p in wave(len(REST), REST_SKEW):
                kind, n = REST[step]
                g = int(kind[-1]) if kind[-1].isdigit() else 0
                if kind == "win":
                    if n == 0:
                        pe_centre(pe, p, K_WIN, x_of(p), N, (x_ready[p], X_FINAL + 1))
                    elif n == 1:
                        pe_variance(pe, p, K_WIN, N)
                    elif n == 2:
                        pe.wait_ge(h_ready[p], H_WIN + 1)
                        nc.tensor.matmul(bank(p, 1)[:, 0:N], wk_w, zv(p), start=True, stop=True).then_inc(k_psum, 1)
                        nc.tensor.matmul(bank(p, 0)[:, 0:N], wq_w, zv(p), start=True,
                                         stop=True).then_inc(q_psum[p], HEADS)
                    else:
                        pe.wait_ge(q_ready[p], HEADS * A_WIN + HEADS)
                        pe_values(pe, p, wv_w)
                elif kind == "win queries":
                    pe.wait_ge(x_ready[p], X_WIN + 1)
                    nc.tensor.matmul(bank(p, 0)[:, 0:N], wq_w, zv(p), start=True, stop=True).then_inc(q_psum[p], HEADS)
                elif kind.startswith("win pass"):
                    if n == S1 and g == 0:
                        pe.wait_ge(v_ready[p], LAYERS + 1)
                    if n == S0 and g == 1:
                        pe.wait_ge(q_ready[p], HEADS * (A_WIN + 1) + HEADS)
                    pe_pass(pe, p, A_WIN + g, n, lambda h: wo_w(HEADS * g + h))
                elif kind == "ffn":
                    if n == 0:
                        pe_centre(pe, p, K_FFN, x_of(p), N, (x_ready[p], X_WIN + 2))
                    elif n == 1:
                        pe_variance(pe, p, K_FFN, N)
                    elif n == 2:
                        pe.wait_ge(h_ready[p], H_FFN + 1)
                        for half in range(HALVES):
                            nc.tensor.matmul(bank(p, half)[:, 0:N], f_wi[rows(half), :], zv(p)[rows(half)],
                                             start=True, stop=True).then_inc(hid_psum, 1)
                    elif n in (3, 4):
                        for m in (2 * p, 2 * p + 1):
                            if n == 3:
                                pe.wait_ge(hid_ready, TILES * LAYERS + m + 1)
                                wait_picked(pe, m)
                            else:
                                pe.wait_ge(g_ready, ROUTED.index((m, 0)) + 1)
                            for w in range(PAIRS):
                                last = nc.tensor.matmul(bank(p, m % 2)[:, 2 * T * w:2 * T * w + 2 * T],
                                                        maps(m, n - 3)[:, w, 0:128],
                                                        PH[:, m, 2 * T * w:2 * T * w + 2 * T], start=True, stop=True)
                            last.then_inc(g_psum, 1)
                    else:
                        pe.wait_ge(g_ready, ROUTED.index((2 * p + 1, FFN_LAYERS - 1)) + 1)
                        for half in range(HALVES):
                            last = nc.tensor.matmul(bank(p, 0)[rows(half), 0:N], f_wo, PH[:, 2 * p + half, :],
                                                    start=True, stop=True)
                        last.then_inc(down_psum, 1)
                elif kind == "rot":
                    if n == 0:
                        pe_centre(pe, p, K_ROT, x_of(p), N, (x_ready[p], X_FFN + 1))
                    elif n == 1:
                        pe_variance(pe, p, K_ROT, N)
                    elif n == 2:
                        pe.wait_ge(h_ready[p], H_ROT + 1)
                        turned(p, 0, rotw[:, 3 * ROT_HEADS, :], rotw[:, 3 * ROT_HEADS + 1, :])
                    elif n == 3:
                        lengths(p, 0)
                    else:
                        pe.wait_ge(r_turned[p], 2)
                        pe_values(pe, p, rotw[:, 3 * ROT_HEADS + 2, :])
                elif kind.startswith("heads"):
                    h, r = n // 2, 1 + HEADS * g + n // 2
                    hh = HEADS * g + h
                    if n % 2:
                        lengths(p, r)
                    else:
                        if h:
                            pe.wait_ge(r_turned[p], 2 * r)
                        elif g:
                            pe.wait_ge(x_ready[p], X_ROT + g)
                        else:
                            pe.wait_ge(v_ready[p], LAYERS + 2)
                        turned(p, r, rotw[:, hh, :], rotw[:, ROT_HEADS + hh, :])
                elif kind == "top":
                    if n == 0:
                        pe_centre(pe, p, K_TOP, x_of(p), N, (x_ready[p], X_TOP))
                    elif n == 1:
                        pe_variance(pe, p, K_TOP, N)
                    elif n == 2:
                        pe.wait_ge(h_ready[p], H_TOP + 1)
                        for s in range(SETS):
                            last = nc.tensor.matmul(bank(p, 0)[:, 16 * s:16 * s + 16],
                                                    Z[:, p, 4 * s:4 * s + 4, :].rearrange("p i t -> p (i t)"), t_wg,
                                                    start=True, stop=True)
                        last.then_inc(gate_psum, 1)
                    else:
                        pe.wait_ge(mask_ready, p + 1)
                        for s in range(SETS):
                            c = SETS * p + s
                            last = nc.tensor.transpose(bank(p, 1)[0:16, 128 * s:128 * s + 128],
                                                       gate[:, 2, 2 * c:2 * c + 2, :].rearrange("p a e -> p (a e)"),
                                                       ident)
                        last.then_inc(mt_psum, 1)
                else:
                    if n == S0:
                        pe.wait_ge(r_done[p], 1 + HEADS * g + HEADS)
                        pe.wait_ge(keys_ready[p], LAYERS + 1)
                    pe_pass(pe, p, A_ROT + g, n, lambda h: rotw[:, 2 * ROT_HEADS + HEADS * g + h, :])

            pe.wait_ge(mt_ready, 2 * PIECES)
            pe.wait_ge(w_late, 16 * 8)
            pe.wait_ge(sel_ready, 1)
            pe.wait_ge(w_route, 32)
            for p in range(PIECES):
                nc.tensor.matmul(B[p][:, 0:N], b2d[:, :], mk32[:, p], start=True, stop=False, skip_group_check=True)

            def expert_up(n):
                e, m = n // TILES, n % TILES
                p, half = m // 2, m % 2
                if n >= 2:
                    pe.wait_ge(em_ready, n - 1)
                nc.tensor.matmul(B[4 + n % 2][:, 0:N], t_w1[:, 2 * e + half, :], zv(p), start=True, stop=True)
                nc.tensor.matmul(B[6 + n % 2][:, 0:N], selb[:, 8 * half + e:8 * half + e + 1].to_broadcast([16, 128]),
                                 mkb[:, p, :], start=True, stop=True).then_inc(eh_psum, 1)

            def expert_down(n):
                e, m = n // TILES, n % TILES
                p, half = m // 2, m % 2
                pe.wait_ge(em_ready, n + 1)
                nc.tensor.matmul(B[p][rows(half), 0:N], t_w2[:, e, :], PH[:, m, :], start=False,
                                 stop=e == TOP_EXPERTS - 1, skip_group_check=True).then_inc(top_psum, 1)

            for n in range(TOP_EXPERTS * TILES):
                expert_up(n)
                if n >= 2:
                    expert_down(n - 2)
            expert_down(TOP_EXPERTS * TILES - 2)
            expert_down(TOP_EXPERTS * TILES - 1)

            for p in range(PIECES):
                pe.wait_ge(x_ready[p], X_TOP + 1)
                for s in range(SETS):
                    last = nc.tensor.transpose(B[p][0:HQ, 128 * s:128 * s + 128],
                                               X[:, p, 4 * s:4 * s + 4, :].rearrange("p i t -> p (i t)"), ident)
                last.then_inc(out_psum, 1)

        @block.scalar
        def _(act):
            nc.scalar.preload_act_table_set("natural_log_exp_and_others")
            def embed_rstd(q):
                half = q % 2
                act.wait_ge(embed_psum, q + 1)
                if q >= 1:
                    act.wait_ge(e_var, q)
                nc.scalar.activation(RS[rows(half), 1, 0:NP], EMBED_BANK[q % 4][rows(1 - half), 0:NP], ACT.Square,
                                     scale=1.0 / FEATURES).then_inc(mean_sq, 1)
                act.wait_ge(e_var, q + 1)
                nc.scalar.activation(RS[rows(half), 0, 0:NP], RS[rows(half), 0, 0:NP], ACT.Ln,
                                     bias=eps_t[rows(half), 0:1]).then_inc(e_rstd, 1)
                act.wait_ge(e_rstd, 2 * q + 1)
                nc.scalar.activation(RS[rows(half), 0, 0:NP], RS[rows(half), 0, 0:NP], ACT.Exp,
                                     scale=-0.5).then_inc(e_rstd, 1)

            experts, pairs = {}, pairs_of("act")
            for q in range(TILES):
                for part_ in range(2):
                    act.wait_ge(img_in[q % 2][part_], 16 * (q // 2) + 16)
                    if q >= 1:
                        act.wait_ge(img_sum, 3 * q - 2 + part_)
                    c = slice(12 * part_, 12 * part_ + 12)
                    nc.scalar.activation(sqi[:, c, :], img[q % 2][:, c, :], ACT.Square).then_inc(img_sq, 1)
                if q == 0:
                    act.wait_ge(w_embed, 48)
                    act.wait_ge(shift_psum, HALVES * CHUNKS)
                    for h in range(HALVES):
                        last = nc.scalar.activation(ZN[rows(h), 0, 0:1], B[5 + h][rows(h), 0:1], ACT.Identity,
                                                    bias=epatch_bias[rows(h)])
                    last.then_inc(shift_ready, 1)
                    act.wait_ge(w_route, 32)
                for m, w in pairs[4 * q:4 * q + 4]:
                    load_expert(act, experts, m, w)
                if q >= 1:
                    embed_rstd(q - 1)
            embed_rstd(TILES - 1)
            for p in range(PIECES):
                act_square(act, p, K_EMBED, NP)
            for p in range(PIECES):
                act_rstd(act, p, K_EMBED, NP)

            act.wait_ge(idx_ready, 1)
            def place_maps(kind):
                for odd in range(2):
                    src = B[1 + 2 * odd][:, 128 * kind:128 * kind + 128].rearrange("p (h f) -> p h f", h=2)
                    for half in range(HALVES):
                        nc.scalar.copy(AB[rows(half), kind, odd:HEADS:2, 64 * half:64 * half + 64],
                                       src[rows(half)]).then_inc(ab_ready, 1)

            def norm_all(k):
                for p in range(PIECES):
                    act_square(act, p, k, N)
                for p in range(PIECES):
                    act_rstd(act, p, k, N)

            def layer(i, last_layer):
                for step, p in wave(LAYER_STEPS, LAYER_SKEW):
                    if step in (0, 1):
                        for h in (2 * step, 2 * step + 1):
                            act_query(act, p, i, h)
                    elif step == 2:
                        act_values(act, p, i)
                    elif step < 3 + PASS:
                        act_pass(act, p, i, step - 3, DIM ** -0.5)
                    elif step == 3 + PASS:
                        act_square(act, p, 2 + 2 * i, N)
                        if not last_layer and p == 2:
                            act.wait_ge(ab_psum, i + 2)
                            place_maps(0)
                        if not last_layer and p == 3:
                            place_maps(1)
                            act.wait_ge(ab_ready, 8 * i + 16)
                            act.sem_inc(layer_used, 1)
                    else:
                        act_rstd(act, p, 2 + 2 * i, N)
                act.wait_ge(fvec_ready, i + 1)
                for p in range(PIECES):
                    for half in range(HALVES):
                        act.wait_ge(hid_psum, TILES * i + 2 * p + half + 1)
                        nc.scalar.activation(PH[:, 2 * p + half, :], bank(p, half)[:, 0:N], ACT.Gelu,
                                             bias=vec["b1"]).then_inc(hid_ready, 1)
                nc.scalar.preload_act_table_set("natural_log_exp_and_others")
                norm_all(3 + 2 * i)

            act.wait_ge(ab_psum, 1)
            for kind in range(2):
                place_maps(kind)
            act.wait_ge(ab_ready, 8)
            act.sem_inc(layer_used, 1)
            norm_all(1)
            with act.Fori(0, LAYERS - 1) as i:
                layer(i, False)
            layer(LAYERS - 1, True)

            def rope_inverse(p, r):
                if r >= 1:
                    act.wait_ge(r_done[p], r)
                act_rstd(act, p, K_TILE + r, N, 1)

            act.wait_ge(w_late, 16 * 7)
            early = [mw for mw in pairs if mw[0] < SLOTS]
            norms = {"win": K_WIN, "ffn": K_FFN, "rot": K_ROT, "top": K_TOP}
            for step, p in wave(len(REST), REST_SKEW):
                kind, n = REST[step]
                g = int(kind[-1]) if kind[-1].isdigit() else 0
                if kind == "win pass 1" and early:
                    act.wait_ge(rw_ready, 4)
                    pick_pair("act", nc.scalar.copy, experts, *early.pop(0))
                if kind in norms and n == 0:
                    act_square(act, p, norms[kind], N)
                elif kind in norms and n == 1:
                    act_rstd(act, p, norms[kind], N)
                elif kind == "win":
                    if n == 2:
                        act.wait_ge(k_psum, p + 1)
                        for half in range(HALVES):
                            last = nc.scalar.activation(KB[rows(half), p, :, half, :],
                                                        tiled(bank(p, 1)[rows(half), 0:N]), ACT.Identity,
                                                        bias=wbk[rows(half)])
                        last.then_inc(k_ready, 1)
                        act_window_queries(act, p, 0)
                elif kind == "win queries":
                    act_window_queries(act, p, 1)
                elif kind.startswith("win pass"):
                    act_pass(act, p, A_WIN + g, n)
                elif kind == "ffn":
                    if n == 2:
                        if PICKER[2 * p + 1] == "act" and 2 * p + 1 >= SLOTS:
                            pick("act", act, nc.scalar.copy, experts, 2 * p + 1)
                        for half in range(HALVES):
                            act.wait_ge(hid_psum, TILES * LAYERS + 2 * p + half + 1)
                            nc.scalar.activation(PH[:, 2 * p + half, :], bank(p, half)[:, 0:N], ACT.Relu,
                                                 bias=f_bi).then_inc(hid_ready, 1)
                    elif n < 5:
                        for m in (2 * p, 2 * p + 1):
                            act.wait_ge(g_biased, ROUTED.index((m, n - 3)) + 1)
                            nc.scalar.activation(PH[:, m, :], PH[:, m, :], ACT.Relu).then_inc(g_ready, 1)
                elif kind == "rot":
                    if n == 2:
                        act_square(act, p, K_TILE, N)
                    elif n == 3:
                        rope_inverse(p, 0)
                    else:
                        act_values(act, p, LAYERS + 1)
                elif kind.startswith("heads"):
                    r = 1 + HEADS * g + n // 2
                    if n % 2:
                        rope_inverse(p, r)
                    else:
                        act_square(act, p, K_TILE + r, N)
                elif kind == "top":
                    if n == 3:
                        act.wait_ge(mt_psum, p + 1)
                        src = bank(p, 1)[0:16, :].rearrange("p (i t) -> p i t", t=PAD)[:, :, 0:T]
                        nc.scalar.copy(mk32[:, p], src).then_inc(mt_ready, 1)
                        nc.scalar.copy(tiled(mkb[:, p, :]), src).then_inc(mt_ready, 1)
                else:
                    act_pass(act, p, A_ROT + g, n)

            for n in range(TOP_EXPERTS * TILES):
                e, m = n // TILES, n % TILES
                act.wait_ge(eh_psum, n + 1)
                if n >= TILES:
                    act.wait_ge(top_psum, n - TILES + 1)
                nc.scalar.activation(PH[:, m, :], B[4 + n % 2][:, 0:N], ACT.Gelu, bias=t_b1[:, e:e + 1]).then_inc(eh_ready, 1)
            for p in range(PIECES):
                act.wait_ge(out_psum, p + 1)
                nc.scalar.copy(QO[0:HQ, p].rearrange("p i h t -> p (i h t)")[:, 0:512],
                               B[p][0:HQ, :]).then_inc(out_ready, 1)

        @block.vector
        def _(dve):
            nc.vector.memset(ones[:, :], 1.0)
            nc.vector.memset(WA[:, :, 0:64], 1.0).then_inc(scaled, 1)
            nc.vector.memset(WA[:, :, 128:192], 1.0)
            nc.vector.memset(eps_t[:, 0:1], EPS)
            nc.vector.memset(eps_t[:, 1:2], RMS_EPS)
            dve.wait_ge(w_embed, 48)
            nc.vector.tensor_tensor(WA[:, :, 64:128], raw_w, lnp[:, 0, :].unsqueeze(2).to_broadcast([128, CHUNKS, 64]),
                                    ALU.mult).then_inc(scaled, 1)
            dve.wait_ge(scaled, 2)
            nc.vector.tensor_reduce(SQ[:, 0, 0:64], WA[:, :, 64:128].rearrange("p c f -> p f c"), AX.X,
                                    ALU.add).then_inc(chunk_sum, 1)
            dve.wait_ge(colsum, 1)
            nc.vector.tensor_scalar(ZN[:, 1, 0:64], B[4][:, 0:64], 1.0 / FEATURES, None, ALU.mult).then_inc(mean_w, 1)
            dve.wait_ge(mean_w, 1)
            nc.vector.tensor_tensor(WA[:, :, 64:128], WA[:, :, 64:128],
                                    ZN[:, 1, 0:64].unsqueeze(1).to_broadcast([128, CHUNKS, 64]),
                                    ALU.subtract).then_inc(wa_ready, 1)

            def embed_sum(q):
                for part_ in range(2):
                    if part_ == 1 and q >= 1:
                        embed_variance(q - 1)
                    dve.wait_ge(img_sq, 2 * q + part_ + 1)
                    if q >= 2 and part_ == 0:
                        dve.wait_ge(sq_psum, q - 1)
                    nc.vector.tensor_reduce(SQ[:, 2 * (q % 2) + part_, 0:NP],
                                            sqi[:, 12 * part_:12 * part_ + 12, :].rearrange("p c n -> p n c"), AX.X,
                                            ALU.add).then_inc(img_sum, 1)
                dve.wait_ge(img_sum, 3 * q + 2)
                nc.vector.tensor_tensor(SQ[:, 2 * (q % 2), 0:NP], SQ[:, 2 * (q % 2), 0:NP],
                                        SQ[:, 2 * (q % 2) + 1, 0:NP], ALU.add).then_inc(img_sum, 1)

            def embed_variance(q):
                half = q % 2
                dve.wait_ge(sq_psum, q + 1)
                dve.wait_ge(mean_sq, q + 1)
                nc.vector.scalar_tensor_tensor(RS[rows(half), 0, 0:NP], B[2 + half][rows(half), 0:NP], 1.0 / FEATURES,
                                               RS[rows(half), 1, 0:NP], ALU.mult, ALU.subtract).then_inc(e_var, 1)

            def embed_scale(q):
                p, half = q // 2, q % 2
                dve.wait_ge(e_rstd, 2 * q + 2)
                y = patches_of(p)[rows(half)]
                nc.vector.tensor_tensor(y, EMBED_BANK[q % 4][rows(half), 0:NP], RS[rows(half), 0, 0:NP], ALU.mult).then_inc(embedded, 1)
                dve.wait_ge(embedded, 2 * q + 1)
                nc.vector.tensor_scalar(y, y, ZN[rows(half), 0, 0:1], None, ALU.add).then_inc(embedded, 1)

            for q in range(TILES):
                embed_sum(q)
                if q == 0:
                    dve.wait_ge(shift_ready, 1)
                else:
                    embed_scale(q - 1)
            embed_variance(TILES - 1)
            embed_scale(TILES - 1)
            for p in range(PIECES):
                dve_norm(dve, p, K_EMBED, NP, zn(p, PATCHES), normed[p])

            def norm_all(k):
                for p in range(PIECES):
                    dve_norm(dve, p, k, N, zn(p), normed[p])

            def layer(i):
                rank = {"first": TILES * i, "max": nth(), "sum": nth()}
                for step, p in wave(LAYER_STEPS, LAYER_SKEW):
                    if step == 0:
                        dve.wait_ge(h_ready[p], 2 * i + 1)
                        for half in range(HALVES):
                            last = nc.vector.tensor_copy(KB[rows(half), p, :, half, :], zv(p)[rows(half)])
                        last.then_inc(keys_ready[p], 1)
                    elif 3 <= step < 3 + PASS:
                        dve_pass(dve, p, i, step - 3, vec["bo"], rank)
                    elif step == 4 + PASS:
                        dve_norm(dve, p, 2 + 2 * i, N, zn(p), normed[p])
                for p in range(PIECES):
                    dve_add(dve, p, down_psum, PIECES * i + p + 1, bank(p, 0), vec["b2"])
                norm_all(3 + 2 * i)

            norm_all(1)
            with dve.Fori(0, LAYERS - 1) as i:
                layer(i)
            layer(LAYERS - 1)

            def rope_turn(p, r):
                dve.wait_ge(centered[p], K_TILE + r + 1)
                if r == 1:
                    dve.wait_ge(keys_ready[p], LAYERS + 1)
                if r >= 1:
                    dve.wait_ge(r_done[p], r)
                nc.vector.tensor_tensor(tiled(turned_sin[:, p, :]), tiled(bank(p, 1)[:, 0:N]),
                                        sin_t.unsqueeze(1).to_broadcast([128, IMG, T]), ALU.mult).then_inc(r_turned[p], 1)
                dve.wait_ge(squared[p], K_TILE + r + 1)
                nc.vector.tensor_tensor(zn(p), tiled(bank(p, 0)[:, 0:N]),
                                        cos_t.unsqueeze(1).to_broadcast([128, IMG, T]), ALU.mult).then_inc(r_turned[p], 1)

            step_of = nth()

            def chained(instruction):
                instruction.then_inc(gate_step, 1)
                dve.wait_ge(gate_step, step_of())

            def choose(p):
                at = slice(2 * SETS * p, 2 * SETS * p + 2 * SETS)
                scores, work, mask = (gate[:, n, at, :] for n in range(3))
                best = gmax[:, at].unsqueeze(2).to_broadcast([128, 2 * SETS, 8])
                order = idx[:, :].unsqueeze(1).to_broadcast([128, 2 * SETS, 8])
                dve.wait_ge(gate_psum, p + 1)
                chained(nc.vector.tensor_tensor(scores.rearrange("p (n a) e -> p n (a e)", a=2),
                                                bank(p, 0)[:, 0:64].rearrange("p (n c) -> p n c", c=16),
                                                t_bg.unsqueeze(1).to_broadcast([128, SETS, 16]), ALU.add))
                for rank in range(2):
                    chained(nc.vector.tensor_reduce(gmax[:, at], scores, AX.X, ALU.max))
                    chained(nc.vector.tensor_tensor(work, scores, best, ALU.is_equal))
                    chained(nc.vector.tensor_tensor(work, work, order, ALU.mult))
                    chained(nc.vector.tensor_reduce(gmax[:, at], work, AX.X, ALU.max))
                    if rank == 0:
                        chained(nc.vector.tensor_tensor(mask, work, best, ALU.is_equal))
                        chained(nc.vector.scalar_tensor_tensor(scores, mask, -3e38, scores, ALU.mult, ALU.add))
                    else:
                        chained(nc.vector.tensor_tensor(work, work, best, ALU.is_equal))
                        nc.vector.tensor_tensor(mask, mask, work, ALU.add).then_inc(mask_ready, 1)

            dve.wait_ge(w_late, 16 * 7)
            dve.wait_ge(idx_ready, 1)
            rank = {"first": TILES * A_WIN, "max": nth(), "sum": nth(), "biased": nth()}
            dve.wait_ge(w_route, 32)
            experts, pairs = {}, pairs_of("dve")
            early = [mw for mw in pairs if mw[0] < SLOTS]
            for step, p in wave(len(REST), REST_SKEW):
                kind, n = REST[step]
                g = int(kind[-1]) if kind[-1].isdigit() else 0
                if kind in ("win", "win pass 0"):
                    for m, w in pairs[:1]:
                        load_expert(dve, experts, m, w)
                    del pairs[:1]
                if kind == "win pass 1" and early:
                    dve.wait_ge(rw_ready, 4)
                    pick_pair("dve", nc.vector.tensor_copy, experts, *early.pop(0))
                if kind == "win" and n == 1:
                    dve_norm(dve, p, K_WIN, N, zv(p), h_ready[p])
                elif kind == "win" and n == 3:
                    dve.wait_ge(v_psum[p], LAYERS + 1)
                    nc.vector.tensor_tensor(VT[:, p, :, :], bank(p, 0)[:, :].rearrange("p (s f) -> p s f", s=SETS),
                                            wbv.unsqueeze(1).to_broadcast([128, SETS, 128]),
                                            ALU.add).then_inc(v_ready[p], 1)
                elif kind.startswith("win pass"):
                    dve_pass(dve, p, A_WIN + g, n, None if g else wbo, rank, table=wtab[g], scale=WIN_DH ** -0.5)
                elif kind == "ffn":
                    if n == 1:
                        dve_norm(dve, p, K_FFN, N, zv(p), h_ready[p])
                    elif n == 2:
                        if PICKER[2 * p] == "dve" and 2 * p >= SLOTS:
                            pick("dve", dve, nc.vector.tensor_copy, experts, 2 * p)
                    elif n in (3, 4):
                        for m in (2 * p, 2 * p + 1):
                            wait_picked(dve, m)
                            dve.wait_ge(g_psum, ROUTED.index((m, n - 3)) + 1)
                            nc.vector.tensor_tensor(PH[:, m, :].rearrange("p (w c) -> p w c", w=PAIRS),
                                                    bank(p, m % 2)[:, 0:N].rearrange("p (w c) -> p w c", w=PAIRS),
                                                    maps(m, n - 3)[:, :, 128:129].to_broadcast([128, PAIRS, 2 * T]),
                                                    ALU.add).then_inc(g_biased, 1)
                    elif n == 5:
                        dve_add(dve, p, down_psum, PIECES * LAYERS + p + 1, bank(p, 0), f_bo)
                elif kind == "rot":
                    if n == 1:
                        dve_norm(dve, p, K_ROT, N, zv(p), h_ready[p])
                    elif n == 2:
                        rope_turn(p, 0)
                    elif n == 4:
                        if p == 0:
                            dve.wait_ge(wqk_ready, 1)
                        dve.wait_ge(r_done[p], 1)
                        for half in range(HALVES):
                            last = nc.vector.tensor_scalar(KB[rows(half), p, :, half, :], zn(p)[rows(half)],
                                                           rotv[rows(half), 0:1], None, ALU.mult)
                        last.then_inc(keys_ready[p], 1)
                elif kind.startswith("heads"):
                    if n % 2 == 0:
                        rope_turn(p, 1 + HEADS * g + n // 2)
                elif kind == "top":
                    if n == 1:
                        dve_norm(dve, p, K_TOP, N, zv(p), h_ready[p])
                    elif n == 2:
                        choose(p)
                elif kind.startswith("rot pass"):
                    dve_pass(dve, p, A_ROT + g, n, None, rank, table=causal[0:HQ], scale=DIM ** -0.5)

            for n in range(TOP_EXPERTS * TILES):
                dve.wait_ge(eh_ready, n + 1)
                nc.vector.tensor_tensor(PH[:, n % TILES, :], B[6 + n % 2][:, 0:N], PH[:, n % TILES, :],
                                        ALU.mult).then_inc(em_ready, 1)
            for p in range(PIECES):
                dve_add(dve, p, top_psum, TOP_EXPERTS * TILES - TILES + 2 * p + 2, B[p], None)

        @block.gpsimd
        def _(pool):
            nc.gpsimd.memset(Z[:, :, :, :], 0.0)
            nc.gpsimd.memset(E[:, :, :, :], 0.0)
            nc.gpsimd.memset(AB[:, :, :, :], 0.0)
            nc.gpsimd.memset(KB[:, :, :, :, :], 0.0)
            for e in range(TOP_EXPERTS):
                nc.gpsimd.memset(idx[:, e:e + 1], float(TOP_EXPERTS - e))
            nc.gpsimd.memset(gmax[:, 0:1], 0.0).then_inc(idx_ready, 1)
            pool.wait_ge(w_embed, 48)
            pool.wait_ge(idx_ready, 1)
            nc.gpsimd.tensor_scalar(evec[:, 7:6 + T], evec[:, 7:6 + T], eshift, None, ALU.add).then_inc(gained, 1)
            nc.gpsimd.tensor_tensor(evec[:, 6:7], evec[:, 6:7], ecls, ALU.add).then_inc(gained, 1)
            pool.wait_ge(gained, 2)
            for p in range(PIECES):
                pool.wait_ge(normed[p], 1)
                nc.gpsimd.tensor_scalar(zn(p, PATCHES), zn(p, PATCHES), egain, None, ALU.mult).then_inc(gained, 1)
                pool.wait_ge(gained, p + 3)
                nc.gpsimd.tensor_tensor(X[:, p, :, 1:T], zn(p, PATCHES),
                                        epos[:, 1:T].unsqueeze(1).to_broadcast([128, IMG, PATCHES]), ALU.add)
                nc.gpsimd.tensor_copy(X[:, p, :, 0:1],
                                      epos[:, 0:1].unsqueeze(1).to_broadcast([128, IMG, 1])).then_inc(x_ready[p], 1)
            with pool.Fori(0, LAYERS) as i:
                pool.wait_ge(w_layer, 16 * i + 16)
                pool.sem_inc(pool_turn, 1)
                nc.gpsimd.tensor_copy(lvec[:, 0:3], LW[:, L_VEC:L_VEC + 3]).then_inc(avec_ready, 1)
                pool.wait_ge(avec_ready, i + 1)
                pool.sem_inc(pool_turn, 1)
                for p in range(PIECES):
                    pool_affine(pool, p, 1 + 2 * i, zv(p), vec["ga"], vec["ba"], h_ready[p])
                nc.gpsimd.tensor_copy(lvec[:, 3:7], LW[:, L_VEC + 3:L_VEC + 7])
                nc.gpsimd.tensor_copy(lvec[:, 7:199], LW[:, L_W1:L_W1 + 192]).then_inc(fvec_ready, 1)
                pool.wait_ge(fvec_ready, i + 1)
                pool.sem_inc(layer_used, 1)
                for step, p in wave(LAYER_STEPS, LAYER_SKEW):
                    if 3 <= step < 3 + PASS:
                        pool_pass(pool, p, i, step - 3)
                    elif step == 4 + PASS:
                        pool_affine(pool, p, 2 + 2 * i, zv(p), vec["gf"], vec["bf"], h_ready[p])
            for p in range(PIECES):
                pool_affine(pool, p, K_FINAL, X[:, p], fgain, fshift, x_ready[p])

            def merge(n):
                l, e = divmod(n, EXPERTS)
                if e == 0:
                    nc.gpsimd.tensor_tensor(f_ws[:, l, :], f_ws[:, l, :], ident, ALU.add).then_inc(rw_ready, 1)
                    pool.wait_ge(rw_ready, 2 * l + 1)
                nc.gpsimd.tensor_tensor(rw[:, n, 0:128], rw[:, n, 0:128], f_ws[:, l, :], ALU.add)
                if e == EXPERTS - 1:
                    nc.gpsimd.tensor_scalar(rw[:, EXPERTS * l:EXPERTS * l + EXPERTS, 128:129],
                                            rw[:, EXPERTS * l:EXPERTS * l + EXPERTS, 128:129], f_bs[:, l:l + 1], None,
                                            ALU.add).then_inc(rw_ready, 1)

            rope_rank = nth()

            def rope_finish(p, r, dst):
                pool.wait_ge(r_turned[p], 2 * r + 2)
                nc.gpsimd.tensor_tensor(ZN[:, p, :], ZN[:, p, :], turned_sin[:, p, :], ALU.add).then_inc(r_sum, 1)
                pool.wait_ge(r_sum, rope_rank())
                pool.wait_ge(rstd_ready[p], 2 * (K_TILE + r) + 2)
                nc.gpsimd.tensor_tensor(dst, zn(p), tiled(RS[:, p, :]), ALU.mult).then_inc(r_done[p], 1)

            pool.wait_ge(w_late, 16 * 7)
            pool.wait_ge(w_const, 16)
            nc.gpsimd.tensor_copy(selb[:, :], ident[0:16, 0:16]).then_inc(sel_ready, 1)
            nc.gpsimd.tensor_tensor(rotv[:, 0:1], rotv[:, 0:1], rotv[:, 1:2], ALU.mult).then_inc(wqk_ready, 1)
            merged = 0
            for step, p in wave(len(REST), REST_SKEW):
                kind, n = REST[step]
                g = int(kind[-1]) if kind[-1].isdigit() else 0
                if "pass" in kind:
                    pool_pass(pool, p, (A_WIN if kind[0] == "w" else A_ROT) + g, n)
                elif kind == "rot" and n == 3:
                    rope_finish(p, 0, zn(p))
                elif kind.startswith("heads") and n % 2:
                    rope_finish(p, 1 + HEADS * g + n // 2, QO[:, p, :, n // 2, :])
                for _ in range(2):
                    if merged < FFN_LAYERS * EXPERTS:
                        merge(merged)
                        merged += 1


def _blocks(maps):
    n, k, m = maps.shape
    full = np.zeros((2 * k, n, 2 * m), maps.dtype)
    full[:k, :, :m] = full[k:, :, m:] = maps.transpose(1, 0, 2)
    return full


def _twice(a, axis=0):
    return np.concatenate([a, a], axis=axis)


def _rows(*vectors):
    return np.stack([_twice(v) for v in vectors], axis=1)


def _laid_out(v):
    f = {}
    g = lambda name: np.asarray(v[name])
    x = g("x").reshape(IMAGES, CHANNELS, GRID, PATCH, GRID, PATCH).transpose(1, 3, 5, 0, 2, 4)
    f["img"] = x.reshape(CHUNKS, 128, TILES, NP).transpose(2, 1, 0, 3)
    f["w_patch"] = g("L0_tok_W_patch").reshape(CHUNKS, 128, DIM).transpose(1, 0, 2)
    f["ln_p1"] = np.stack([g("L0_tok_ln_p1_g").reshape(CHUNKS, 128).T, g("L0_tok_ln_p1_b").reshape(CHUNKS, 128).T], 1)
    f["evec"] = np.concatenate([_rows(*(g("L0_tok_" + n) for n in ("ln_p2_g", "ln_p2_b", "ln_f_g", "ln_f_b",
                                                                  "b_patch"))),
                                _rows(g("L0_tok_cls").reshape(DIM)), _twice(g("L0_tok_pos").reshape(T, DIM).T)], 1)
    layers = []
    for i in range(LAYERS):
        def heads(m, twice):
            m = m.reshape(2, 128, DIM).transpose(1, 0, 2)
            return (np.concatenate([m, m], 2) if twice else m).reshape(128, -1)
        qkv = g("L0_tok_Wqkv")[i].T.reshape(3, HEADS * DIM, DIM)
        layers.append(np.concatenate(
            [heads(qkv[0], True), heads(qkv[1], False), heads(qkv[2], True), heads(g("L0_tok_Wo")[i], False),
             _twice(g("L0_tok_W1")[i]), g("L0_tok_W2")[i],
             _rows(*(g("L0_tok_" + n)[i] for n in ("attn_ln_g", "attn_ln_b", "bo", "ff_ln_g", "ff_ln_b", "b2"))),
             g("L0_tok_b1")[i][:, None]], 1))
    f["layers"] = np.stack(layers)

    qkv_w, qkv_b, pw = g("L0_attn_qkv_w"), g("L0_attn_qkv_b"), g("L0_attn_proj_w")
    wo, bq, own_rows = (np.zeros(s, np.float32) for s in ((WIN_HEADS, DIM, DIM), (128, WIN_HEADS), (128, WIN_HEADS)))
    for h in range(WIN_HEADS):
        own = slice(WIN_DH * h, WIN_DH * h + WIN_DH)
        wo[h, own, :] = pw[own, :]
        bq[own, h] = bq[DIM + WIN_DH * h:DIM + WIN_DH * h + WIN_DH, h] = qkv_b[own]
        own_rows[own, h] = own_rows[DIM + WIN_DH * h:DIM + WIN_DH * h + WIN_DH, h] = 1.0
    f["win_w"] = _blocks(np.concatenate([wo] + [qkv_w[None, :, DIM * n:DIM * n + DIM] for n in range(3)]))
    at = np.arange(T)[:, None] - np.arange(T)[None, :] + T - 1
    tab = g("L0_attn_rpb_table")[at].transpose(2, 0, 1).reshape(2, HQ, T)
    tabs = np.zeros((128, 2, T), np.float32)
    tabs[:HQ] = tab.transpose(1, 0, 2)
    f["win_v"] = np.concatenate([bq, _rows(qkv_b[DIM:2 * DIM], g("L0_attn_proj_b")),
                                 np.broadcast_to(_twice(qkv_b[2 * DIM:])[None], (128, 128)),
                                 tabs.reshape(128, -1), own_rows], 1)

    wq = g("L1_attn_wq").reshape(ROT_HEADS, DIM, DIM).transpose(0, 2, 1)
    wk, wv = g("L1_attn_wkv").reshape(2, DIM, DIM).transpose(0, 2, 1)
    swap = np.arange(DIM) ^ 1
    wo = g("L1_attn_wo").reshape(DIM, ROT_HEADS, DIM).transpose(1, 2, 0)
    f["rot_w"] = _blocks(np.concatenate([wq, wq[:, :, swap], wo, wk[None], wk[None][:, :, swap], wv[None]]))
    f["rot_v"] = np.concatenate([_rows(g("L1_attn_q_norm_w"), g("L1_attn_k_norm_w")), np.zeros((128, 1), np.float32)], 1)

    f["ff_w"] = np.concatenate([_twice(g("L0_ffn_Wi").T), g("L0_ffn_Wo").T, g("L0_ffn_bi")[:, None],
                                _rows(g("L0_ffn_bo")), g("L0_ffn_bs")[:, 0].T,
                                g("L0_ffn_Ws")[:, 0].transpose(2, 0, 1).reshape(128, 256)], 1)
    wr = g("L0_ffn_Wr").reshape(FFN_LAYERS * EXPERTS, 128, 128).transpose(2, 0, 1)
    br = g("L0_ffn_br").reshape(FFN_LAYERS * EXPERTS, 128).T[:, :, None]
    f["ff_r"] = np.concatenate([wr, br], 2)
    f["route"] = g("L0_ffn_route_id").reshape(1, ROUTES)

    wg = np.zeros((128, 2, 8), np.float32)
    wg[:64, 0] = wg[64:, 1] = g("L1_ffn_Wg")
    w1 = np.zeros((2, DIM, TOP_EXPERTS, 2, 128), np.float32)
    w1[0, :, :, 0] = w1[1, :, :, 1] = g("L1_ffn_W1").transpose(1, 0, 2)
    f["top_w1"] = w1.reshape(128, 2 * TOP_EXPERTS, 128)
    f["top_w"] = np.concatenate([g("L1_ffn_W2").transpose(1, 0, 2).reshape(128, -1), g("L1_ffn_b1").T,
                                 wg.reshape(128, 16), np.broadcast_to(_twice(g("L1_ffn_bg"))[None], (128, 16))], 1)
    b2 = np.zeros((16, 128), np.float32)
    b2[:8, :64] = b2[8:, 64:] = g("L1_ffn_b2")
    f["top_b2"] = b2

    eye = np.eye(128, dtype=np.float32)
    mean = np.zeros((128, 128), np.float32)
    mean[:64, :64] = mean[64:, 64:] = 1.0 / DIM
    freqs = np.float32(10000.0) ** (-2.0 * np.arange(DIM // 2, dtype=np.float32) / DIM).astype(np.float32)
    theta = (np.arange(T, dtype=np.float32)[None] * freqs[:, None]).astype(np.float32)
    cos = _twice(np.repeat(np.cos(theta), 2, axis=0))
    sin = np.repeat(np.sin(theta), 2, axis=0)
    sin[0::2] = -sin[0::2]
    mask = np.zeros((128, T), np.float32)
    mask[:HQ] = np.tile(np.where(np.arange(T)[None] <= np.arange(T)[:, None], 0.0, NEG), (HEADS, 1))
    f["consts"] = np.concatenate([eye, eye - mean, mean, cos, _twice(sin), mask], 1).astype(np.float32)
    return {k: np.ascontiguousarray(a) for k, a in f.items()}


def kernel(**inputs):
    import concourse.bacc as _bacc
    from concourse.bass_utils import run_bass_kernel_spmd as _run

    nc = _bacc.Bacc("TRN2", target_bir_lowering=False, num_devices=1)
    arrays = {f"in_{k}": a for k, a in _laid_out(inputs).items()}
    d = {k[3:]: nc.dram_tensor(k, a.shape, mybir.dt.from_np(a.dtype), kind="ExternalInput").ap()
         for k, a in arrays.items()}
    o = nc.dram_tensor("out_0", (IMAGES, T, DIM), FP32, kind="ExternalOutput").ap()
    o = [o[IMG * m:IMG * m + IMG].rearrange("(s j) t f -> (j t) s f", s=SETS) for m in range(TILES)]
    build(nc, d, o)
    r = _run(nc, [arrays], core_ids=[0])
    return r.results[0]["out_0"]
```
